# Optimizing a Trainium2 kernel written in Bass

```python
import numpy as np
import jax
import jax.numpy as jnp

def _softmax(x, axis=-1):
    return jax.nn.softmax(x, axis=axis)

def _gelu(x):
    return jax.nn.gelu(x, approximate=True)

def _silu(x):
    return jax.nn.silu(x)

def _sigmoid(x):
    return jax.nn.sigmoid(x)

def _layernorm(x, axis=-1, eps=1e-05):
    m = jnp.mean(x, axis=axis, keepdims=True)
    v = jnp.var(x, axis=axis, keepdims=True)
    return (x - m) / jnp.sqrt(v + eps)

def _scatter_add(tgt, idx, src, axis=0):
    return tgt.at[idx].add(src)

def _segment_sum(src, seg, n):
    return jax.ops.segment_sum(src, seg, n)
kernel_name = 'mk_audio_tower_d1_tok_audfeat512_r4_7a1646'

def setup_inputs(seed: int=0):
    np.random.seed(seed)
    _w = jnp.asarray

    def _rec_inputs():
        import jax
        import jax.numpy as jnp
        _rk = jax.random.key(seed)
        x = 7.22013e-05 + 1.00017 * jax.random.normal(jax.random.fold_in(_rk, 1), (16, 750, 64), jnp.float32)
        return x
    x = _rec_inputs()

    def _L0_tok_setup():
        import jax, jax.numpy as jnp
        import numpy as np
        EPS = 1e-07
        C_CURV = 1.0
        LAM_HALF = 1.0 / (1.0 + EPS)
        key = jax.random.key(seed)
        k1, k2 = jax.random.split(key)
        B, L, Cin, K, F = (32, 256, 64, 9, 128)
        x = jax.random.normal(k1, (B, L, Cin), dtype=jnp.float32)
        lim = float(np.sqrt(6.0 / (K * Cin + F)))
        kernel = jax.random.uniform(k2, (K, Cin, F), dtype=jnp.float32, minval=-lim, maxval=lim)
        bias = jnp.zeros((F,), dtype=jnp.float32)
        return {'x': x, 'kernel': kernel, 'bias': bias}
    _L0_tok_all = _L0_tok_setup()
    _L0_tok_in = {k: v for k, v in _L0_tok_all.items() if k in ('kernel', 'bias')}
    del _L0_tok_all

    def _L0_attn_setup():
        import jax, jax.numpy as jnp
        import numpy as np
        import math
        D_MODEL = 128
        NUM_HEADS = 8
        HEAD_DIM = D_MODEL // NUM_HEADS
        B, L = (2, 512)
        LN_EPS = 1e-05
        DEN_EPS = 1e-05
        key = jax.random.key(seed)
        ks = jax.random.split(key, 6)
        s = 1.0 / math.sqrt(D_MODEL)
        return {'x': jax.random.normal(ks[0], (B, L, D_MODEL), dtype=jnp.float32), 'Wqkv': jax.random.normal(ks[1], (D_MODEL, 3 * D_MODEL), dtype=jnp.float32) * s, 'bqkv': jnp.zeros((3 * D_MODEL,), dtype=jnp.float32), 'Wout': jax.random.normal(ks[2], (D_MODEL, D_MODEL), dtype=jnp.float32) * s, 'bout': jnp.zeros((D_MODEL,), dtype=jnp.float32), 'ln_gamma': jnp.ones((D_MODEL,), dtype=jnp.float32), 'ln_beta': jnp.zeros((D_MODEL,), dtype=jnp.float32), 'decay_logits': jnp.full((NUM_HEADS,), 5.0, dtype=jnp.float32)}
    _L0_attn_all = _L0_attn_setup()
    _L0_attn_in = {k: v for k, v in _L0_attn_all.items() if k in ('Wqkv', 'bqkv', 'Wout', 'bout', 'ln_gamma', 'ln_beta', 'decay_logits')}
    del _L0_attn_all

    def _L0_ffn_setup():
        import jax, jax.numpy as jnp
        import numpy as np
        NUM_EXPERTS = 32
        GROUP_SIZE = 4
        NUM_GROUPS = NUM_EXPERTS // GROUP_SIZE
        C_CAP = 1.0
        key = jax.random.key(seed)
        ks = jax.random.split(key, 5)
        B, S, H = (16, 512, 128)
        D_FF = int(H * 4 * (2.0 / 3.0))
        x = jax.random.normal(ks[0], (B, S, H), dtype=jnp.float32)
        W_router = jax.random.normal(ks[1], (H, NUM_EXPERTS), dtype=jnp.float32) * (1.0 / np.sqrt(H))
        b_router = jnp.zeros((NUM_EXPERTS,), dtype=jnp.float32)
        W_up = jax.random.normal(ks[2], (NUM_GROUPS, H, D_FF), dtype=jnp.float32) * (1.0 / np.sqrt(H))
        b_up = jnp.zeros((NUM_GROUPS, D_FF), dtype=jnp.float32)
        W_down = jax.random.normal(ks[3], (NUM_EXPERTS, D_FF, H), dtype=jnp.float32) * (1.0 / np.sqrt(D_FF))
        b_down = jnp.zeros((NUM_EXPERTS, H), dtype=jnp.float32)
        return {'x': x, 'W_router': W_router, 'b_router': b_router, 'W_up': W_up, 'b_up': b_up, 'W_down': W_down, 'b_down': b_down}
    _L0_ffn_all = _L0_ffn_setup()
    _L0_ffn_in = {k: v for k, v in _L0_ffn_all.items() if k in ('W_router', 'b_router', 'W_up', 'b_up', 'W_down', 'b_down')}
    del _L0_ffn_all
    return {'x': x, 'L0_tok_kernel': _L0_tok_in['kernel'], 'L0_tok_bias': _L0_tok_in['bias'], 'L0_attn_Wqkv': _L0_attn_in['Wqkv'], 'L0_attn_bqkv': _L0_attn_in['bqkv'], 'L0_attn_Wout': _L0_attn_in['Wout'], 'L0_attn_bout': _L0_attn_in['bout'], 'L0_attn_ln_gamma': _L0_attn_in['ln_gamma'], 'L0_attn_ln_beta': _L0_attn_in['ln_beta'], 'L0_attn_decay_logits': _L0_attn_in['decay_logits'], 'L0_ffn_W_router': _L0_ffn_in['W_router'], 'L0_ffn_b_router': _L0_ffn_in['b_router'], 'L0_ffn_W_up': _L0_ffn_in['W_up'], 'L0_ffn_b_up': _L0_ffn_in['b_up'], 'L0_ffn_W_down': _L0_ffn_in['W_down'], 'L0_ffn_b_down': _L0_ffn_in['b_down']}

def reference(x, L0_tok_kernel, L0_tok_bias, L0_attn_Wqkv, L0_attn_bqkv, L0_attn_Wout, L0_attn_bout, L0_attn_ln_gamma, L0_attn_ln_beta, L0_attn_decay_logits, L0_ffn_W_router, L0_ffn_b_router, L0_ffn_W_up, L0_ffn_b_up, L0_ffn_W_down, L0_ffn_b_down):
    import jax
    import jax.numpy as jnp

    def _L0_tok_ref(x, kernel, bias):
        import jax, jax.numpy as jnp
        import numpy as np
        EPS = 1e-07
        C_CURV = 1.0
        LAM_HALF = 1.0 / (1.0 + EPS)
        B, L, Cin = x.shape
        K, _, F = kernel.shape
        Lout = L - K + 1
        sq = jnp.sum(x * x, axis=-1)
        cs = jnp.concatenate([jnp.zeros((B, 1), x.dtype), jnp.cumsum(sq, axis=1)], axis=1)
        wsq = cs[:, K:] - cs[:, :Lout]
        wnorm = jnp.sqrt(jnp.maximum(wsq, 0.0))
        scale = jnp.where(wnorm < 1.0, 1.0, 1.0 / (wnorm + EPS))[..., None]
        conv = jax.lax.conv_general_dilated(x, kernel, window_strides=(1,), padding='VALID', dimension_numbers=('NWC', 'WIO', 'NWC'))
        v = conv * scale
        v_norm = jnp.maximum(jnp.abs(v), EPS)
        y = jnp.tanh(v_norm * LAM_HALF) * (v / v_norm)
        return jax.nn.relu(y + bias)

    def _L0_attn_ref(x, Wqkv, bqkv, Wout, bout, ln_gamma, ln_beta, decay_logits):
        import jax, jax.numpy as jnp
        import numpy as np
        import math
        D_MODEL = 128
        NUM_HEADS = 8
        HEAD_DIM = D_MODEL // NUM_HEADS
        B, L = (2, 512)
        LN_EPS = 1e-05
        DEN_EPS = 1e-05
        Bv, Lv, D = x.shape
        H = decay_logits.shape[0]
        E = D // H
        qkv = x @ Wqkv + bqkv
        q, k, v = jnp.split(qkv, 3, axis=-1)
        q = q.reshape(Bv, Lv, H, E)
        k = k.reshape(Bv, Lv, H, E)
        v = v.reshape(Bv, Lv, H, E)
        q = (jax.nn.elu(q) + 1.0) / jnp.sqrt(jnp.asarray(E, x.dtype))
        k = jax.nn.elu(k) + 1.0
        lambdas = jax.nn.sigmoid(decay_logits).reshape(1, 1, H, 1)
        t = jnp.arange(Lv, dtype=x.dtype).reshape(1, Lv, 1, 1)
        decay_k = jnp.power(lambdas, -t)
        decay_q = jnp.power(lambdas, t)
        k_dec = k * decay_k
        kv = jnp.einsum('blhe,blhf->blhef', k_dec, v)
        memory = jnp.cumsum(kv, axis=1)
        k_sum = jnp.cumsum(k_dec, axis=1)
        q_dec = q * decay_q
        num = jnp.einsum('blhe,blhef->blhf', q_dec, memory)
        den = jnp.einsum('blhe,blhe->blh', q_dec, k_sum)[..., None] + DEN_EPS
        out = (num / den).reshape(Bv, Lv, D)
        out = out @ Wout + bout
        mu = jnp.mean(out, axis=-1, keepdims=True)
        var = jnp.var(out, axis=-1, keepdims=True)
        out = (out - mu) / jnp.sqrt(var + LN_EPS) * ln_gamma + ln_beta
        return out

    def _L0_ffn_ref(x, W_router, b_router, W_up, b_up, W_down, b_down):
        import jax, jax.numpy as jnp
        import numpy as np
        NUM_EXPERTS = 32
        GROUP_SIZE = 4
        NUM_GROUPS = NUM_EXPERTS // GROUP_SIZE
        C_CAP = 1.0
        B, S, H = x.shape
        bs = B * S
        E = NUM_EXPERTS
        k = min(int(bs * C_CAP) // E, bs)
        xf = x.reshape(bs, H)
        h = xf @ W_router + b_router
        Sm = jax.nn.softmax(h, axis=-1)
        G_ek, idx_ek = jax.lax.top_k(Sm.T, k)
        tokens = xf[idx_ek]
        D_FF = W_up.shape[-1]
        tok_g = tokens.reshape(NUM_GROUPS, GROUP_SIZE, k, H)
        up = jnp.einsum('gjkh,ghf->gjkf', tok_g, W_up) + b_up[:, None, None, :]
        act = jax.nn.silu(up).reshape(E, k, D_FF)
        Eout = jnp.einsum('ekf,efh->ekh', act, W_down) + b_down[:, None, :]
        weighted = G_ek[..., None] * Eout
        y = jnp.zeros((bs, H), dtype=x.dtype).at[idx_ek.reshape(-1)].add(weighted.reshape(-1, H))
        return y.reshape(B, S, H)
    h = _L0_tok_ref(x, L0_tok_kernel, L0_tok_bias)
    h = h + _L0_attn_ref(_layernorm(h, axis=-1), L0_attn_Wqkv, L0_attn_bqkv, L0_attn_Wout, L0_attn_bout, L0_attn_ln_gamma, L0_attn_ln_beta, L0_attn_decay_logits)
    h = h + _L0_ffn_ref(_layernorm(h, axis=-1), L0_ffn_W_router, L0_ffn_b_router, L0_ffn_W_up, L0_ffn_b_up, L0_ffn_W_down, L0_ffn_b_down)
    return h

_drawn_inputs = setup_inputs


def setup_inputs(seed=0):
    import zlib

    import numpy as np

    out = dict(_drawn_inputs(seed))
    spreads = {'L0_tok_bias': (0.0, 0.1),
     'L0_attn_bqkv': (0.0, 0.1),
     'L0_attn_bout': (0.0, 0.1),
     'L0_attn_ln_gamma': (1.0, 0.2),
     'L0_attn_ln_beta': (0.0, 0.1),
     'L0_attn_decay_logits': (5.0, 0.6),
     'L0_ffn_b_router': (0.0, 0.8),
     'L0_ffn_b_up': (0.0, 2.0),
     'L0_ffn_b_down': (0.0, 0.8)}
    factors = {}
    for name, (base, spread) in spreads.items():
        noise = np.random.default_rng([zlib.crc32(name.encode()), seed]).standard_normal(out[name].shape)
        drawn = base * np.exp(spread * noise) if base else spread * noise
        out[name] = jnp.asarray(drawn.astype(out[name].dtype))
    for name, factor in factors.items():
        out[name] = (out[name] * factor).astype(out[name].dtype)
    return out
```

```python
import concourse.bass as bass
from concourse import mybir
from contextlib import ExitStack


def audio_tower_kernel(nc, x, tok_w, tok_b, w_qkv, b_qkv, w_out, b_out, ln_g, ln_b, decay,
                       w_router, b_router, w_up, b_up, w_down, b_down, out):
    f32, bf16, f16 = mybir.dt.float32, mybir.dt.bfloat16, mybir.dt.float16
    i32, u32 = mybir.dt.int32, mybir.dt.uint32
    ALU, ACT, AX = mybir.AluOpType, mybir.ActivationFunctionType, mybir.AxisListType

    NB, L, CIN = x.shape
    TAPS, _, D = tok_w.shape
    LO = L - TAPS + 1
    C = 106
    NC = LO // C
    XC = (L - 1) // NC
    H = decay.shape[0]
    E = D // H
    E1 = E + 1
    N = NB * LO
    NJ = NB * NC
    NE = w_router.shape[1]
    NG = w_up.shape[0]
    GS = NE // NG
    F = w_up.shape[2]
    CAP = N // NE
    FC = 114
    SL = 124
    ROW = D + NE
    SEG = 128 // NE
    JS = NJ // SEG
    HALF = [(0, 4), (4, NC)]
    QH = LO // 2
    LAM = 1.0 / (1.0 + 1e-07)
    EPS_W, EPS_LN, EPS_DEN = 1e-07, 1e-05, 1e-05
    assert NC * C == LO and XC * NC == L - 1 and CAP * NE == N and 3 * FC == F + 1

    ctx = ExitStack()
    with ctx:
        def sb(name, shape, dt=f32):
            return ctx.enter_context(nc.sbuf_tensor(name, shape, dt))

        def pb(name):
            return ctx.enter_context(nc.psum_tensor(name, [128, 512], f32))

        def sem(name):
            return ctx.enter_context(nc.semaphore(name))

        rows = nc.dram_tensor("token_rows", (N, ROW), f32, kind="Internal").ap()

        ident = sb("ident", [128, 128])
        ones = sb("ones", [128, 1])
        zero_w = sb("zero_w", [128, 128])
        wc = sb("wc", [128, (TAPS + 1) // 2, D])
        wqkv = sb("wqkv", [128, 3 * D])
        wo = sb("wo", [128, D])
        wr = sb("wr", [128, NE])
        bqk = sb("bqk", [128, 2])
        rowb = sb("rowb", [128, 5, D])
        brow = sb("brow", [128, NE])
        lam_in = sb("lam_in", [128, 1])
        lam_row_in = sb("lam_row_in", [128, H])
        lam = sb("lam", [128, 1])
        lam_row = sb("lam_row", [128, H])
        lamc = sb("lamc", [128, 1])
        steps = sb("steps", [128, C])
        steps_neg = sb("steps_neg", [128, C])
        step_cols = sb("step_cols", [128, H])
        cexp = sb("cexp", [128, 1])
        dq = sb("dq", [128, C])
        dk = sb("dk", [128, C])
        dks8 = sb("dks8", [128, H])
        head4 = sb("head4", [128, 4])
        blk = sb("blk", [128, H * E1])
        causal = sb("causal", [128, C])
        expo = sb("expo", [128, 3, NC])

        xw = sb("xw", [XC, 2, NC, 2 * CIN])
        xT = sb("xT", [128, L - 1])
        sq = sb("sq", [128, L - 1])
        sq2 = sb("sq2", [128, L - 1])
        sq4 = sb("sq4", [128, LO])
        wnorm = sb("wnorm", [C, 4, NC])
        y = sb("y", [C, NC, D])
        hres = sb("hres", [C, 2, NC, D])
        st1 = sb("st1", [C, NC, 6])
        mv1 = sb("mv1", [C, NC])
        tmp1 = sb("tmp1", [C, 3, NC])
        ve1 = sb("ve1", [C, NC])
        rs1 = sb("rs1", [C, NC])
        hn = sb("hn", [C, NC, D])
        hnT = sb("hnT", [128, LO])
        tqk = sb("tqk", [128, 2, LO])
        eqk = sb("eqk", [128, 2, LO])
        fqk = sb("fqk", [128, 2, LO])
        qd = sb("qd", [128, 2, LO])
        qb = sb("qb", [128, 2, 4, LO])
        kd = sb("kd", [128, 2, LO])
        kt = sb("kt", [C, 2, NC, D])
        v1 = sb("v1", [C, 2, NC, H, E1])
        P = sb("P", [C, 2, H, C])
        state = sb("state", [128, 3, H * E1])
        state_in = sb("state_in", [128, H * E1])
        den = sb("den", [C, 2, H])
        o = sb("o", [C, 2, NC, D])
        oT = sb("oT", [128, LO])
        z = sb("z", [C, NC, D])
        st2 = sb("st2", [C, NC, 6])
        mv2 = sb("mv2", [C, NC])
        tmp2 = sb("tmp2", [C, 3, NC])
        ve2 = sb("ve2", [C, NC])
        rs2 = sb("rs2", [C, NC])
        hb = sb("hb", [C, NC, D])
        h2 = sb("h2", [C, 2, NC, D])
        st3 = sb("st3", [C, NC, 6])
        mv3 = sb("mv3", [C, NC])
        tmp3 = sb("tmp3", [C, 3, NC])
        ve3 = sb("ve3", [C, NC])
        rs3 = sb("rs3", [C, NC])
        row = sb("row", [C, 2, NC, ROW])
        h2T = sb("h2T", [128, LO])
        lg = sb("lg", [C, NC, NE])
        lmax = sb("lmax", [C, NC])
        lsum = sb("lsum", [C, 2, NC])
        probs = sb("probs", [C, NJ, NE])

        seg_probs = qb[:, 0, :, :].rearrange("p a b -> p (a b)")
        seg_hits = qb[:, 1, 0:2, :].rearrange("p a b -> p (a b)").bitcast(bf16)
        same_expert = sb("same_expert", [128, 128])
        thr_bits = sb("thr_bits", [128, 1], i32)
        bit = sb("bit", [128, 2], i32)
        cand = sb("cand", [128, 1], i32)
        hits = sb("hits", [128, 1])
        keep = sb("keep", [128, 1], i32)
        thr_wide = sb("thr_wide", [NE, C])
        thr = sb("thr", [C, NE])
        onesb = sb("onesb", [128, 128], bf16)
        chunkb = sb("chunkb", [128, 1], bf16)
        above = sb("above", [C, C], bf16)
        upto = sb("upto", [C, C], bf16)
        before = sb("before", [NJ, NJ], bf16)
        slots_h = sb("slots_h", [NJ, CAP + 1], f16)
        slots_f = sb("slots_f", [C, CAP + 1])
        mask = sb("mask", [C, 1 + 2 * NJ], bf16)
        cnt = sb("cnt", [NJ, 2], bf16)
        cex = sb("cex", [NJ, 2])
        reach = sb("reach", [NJ, 2, CAP + 1], bf16)
        dcum = sb("dcum", [NJ, 2, C], bf16)
        inside = sb("inside", [C, CAP + 1], bf16)
        wrap = sb("wrap", [SL, 3])
        idx = sb("idx", [SL, 4, 3], i32)
        xg = sb("xg", [SL, 2, 3, ROW])
        gcol = sb("gcol", [SL, 2, 3])
        xgT = sb("xgT", [128, CAP])
        wup = sb("wup", [128, 2, F])
        wdn = sb("wdn", [FC, 2, 3, D])
        bup = sb("bup", [FC, NG, 3])
        act = sb("act", [FC, 2, 3, CAP])
        yw = sb("yw", [SL, 2, 3, D])

        pa = [pb("pa0"), pb("pa1")]
        ps = [pb("ps0"), pb("ps1")]
        po = pb("po")
        pst = pb("pst")
        pc = [pb("pc0"), pb("pc1")]

        p_xg, p_up, p_dn, p_small, p_dcum, p_cum = pa[0], [pa[1], ps[0], ps[1]], po, pst, pc[0], pc[1]

        names = """weights_in consts_pool consts_dve lam_exp lam_done decays_done
            xt_ps xt_sb sq_done win_done wsum_ps wsum_sb wnorm_done scale_step conv_ps tanh_done ybias_done h_done
            stats1  ve1_done rs1_done hn_done hnt_ps hnt_sb qk_ps t_sb e_sb emin_done f_done qd_done qb_done
            kd_done v_ps v_sb kt_ps kt_sb s_ps p0_done p1_raw p1_done o_ps st_ps stm_done state_done den_step o_done
            ot_ps ot_sb wo_ps z_done stats2  ve2_done rs2_done zn_done zg_done hb_done h2_done
            stats3  ve3_done rs3_done hn2_done h2t_ps h2t_sb r_ps lg_done lmax_done lsub_done lexp_done
            lsum_done lrec_done probs_done probs_row
            held_sync held_pool held_act bup_in
            seg_ps seg_act seg_dve bit_step hits_done hits_ps thr_step thr_ps thr_done
            mask_done cnt_ps cnt_sb cex_ps cex_sb dcum_ps dcum_sb reach_done cum_ps inside_done idx_ps wrap_done idx_done
            xgt_ps gcol_done xgt_sb up_ps act_done dn_ps yw_done eps1_done eps2_done eps3_done""".split()
        S = {n: sem(n) for n in names}
        x_in = [sem("x_in0"), sem("x_in1")]
        w_in = [sem("w_in0"), sem("w_in1")]
        x_got = [sem("x_got0"), sem("x_got1")]
        y_out = sem("y_out")
        h2_out = [sem("h2_out0"), sem("h2_out1")]
        row_out = [sem("row_out0"), sem("row_out1")]

        class Batch:
            def __init__(self, m, par):
                self.m, self.par = m, par

            def count(self, per, k, back=0):
                return self.m * (2 * per) + (per * (self.par - back) + k)

            def index(self):
                return self.m * 2 + self.par

        def BEFORE(b):
            return Batch(b.m, 0) if b.par else Batch(b.m - 1, 1)

        def AFTER(b):
            return Batch(b.m + 1, 0) if b.par else Batch(b.m, 1)

        WSUM_AT = 2

        def need(eng, s, value):
            if isinstance(value, int) and value <= 0:
                return
            eng.wait_ge(S[s] if isinstance(s, str) else s, value)

        def chunks(half):
            return range(*HALF[half])

        def hold(eng, s, value):
            if isinstance(value, int) and value <= 0:
                return
            eng.wait_ge(S[s] if isinstance(s, str) else s, value)
            eng.sem_inc(S["held_sync" if eng is nc.sync else "held_pool" if eng is nc.gpsimd else "held_act"])

        ORDER = [("C", "o"), ("A", "x"), ("C", "w"), ("S", 0), ("A", "win"), ("S", 1), ("V", 0), ("C", "z"),
                 ("A", "conv0"), ("A", "w"), ("S", 2), ("V", 1), ("A", "scale"), ("A", "conv1"), ("S", 3),
                 ("V", 2), ("A", "h0"), ("A", "h1"), ("S", 4), ("V", 3), ("C", "norm"), ("A", "hn"), ("S", 5),
                 ("V", 4), ("A", "hnT"), ("C", "hn"), ("S", 6), ("V", 5), ("A", "qk"), ("C", "t"), ("V", 6),
                 ("A", "v"), ("C", "r"), ("A", "kt"), ("C", "max"), ("C", "soft")]
        PEEL_IN, TAIL = 4, 2

        def run(eng, part):
            def iteration(M, p, a, b, c):
                before = Batch(M, 0) if p else Batch(M - 1, 1)
                batch = {"A": Batch(M, p), "S": before, "V": before, "C": Batch(M - 1, p)}
                for stage, what in ORDER:
                    if {"A": a, "S": b, "V": b, "C": c}[stage]:
                        part(stage, what, batch[stage])
            for i in range(PEEL_IN):
                iteration(i // 2, i % 2, True, i >= 1, i >= 2)
            with eng.Fori(PEEL_IN // 2, NB // 2) as M:
                for p in range(2):
                    iteration(M, p, True, True, True)
            for i in range(NB, NB + TAIL):
                iteration(i // 2, i % 2, False, i < NB + 1, True)

        SEG_BANKS = [pa[0], pa[1], ps[0], ps[1], pc[0], pc[1], po]

        class Expert:
            def __init__(self, m, k):
                self.m, self.k = m + k // 4, k % 4
                self.par = k % 2

            def count(self, per, k, back=0):
                return self.m * (4 * per) + (per * (self.k - back) + k)

            def half(self, back=0):
                return self.m * 2 + (self.k // 2 + 1 - back)

            def index(self):
                return self.m * 4 + self.k

        ORDER2 = [("I", "mask"), ("F", "x"), ("I", "cnt"), ("F", "up"), ("I", "reach"), ("I", "cum"),
                  ("F", "down"), ("I", "idx"), ("F", "out")]

        def run2(eng, part):
            def iteration(M, p, i_on, f_on):
                expert = {"I": Expert(M, p), "F": Expert(M, p - 2) if p >= 2 else Expert(M - 1, p + 2)}
                for stage, what in ORDER2:
                    if {"I": i_on, "F": f_on}[stage]:
                        part(stage, what, expert[stage])
            for i in range(4):
                iteration(0, i, True, i >= 2)
            with eng.Fori(1, NE // 4) as M:
                for p in range(4):
                    iteration(M, p, True, True)
            for i in range(2):
                iteration(NE // 4, i, False, True)

        block = ctx.enter_context(nc.Block())

        @block.sync
        def _(eng):
            w2 = tok_w[0:TAPS - 1, :, :].rearrange("(k t) c f -> t c k f", t=2)
            n = 0
            for dst, src in [
                (wc[0:CIN, 0:4, :], w2[0]), (wc[CIN:128, 0:4, :], w2[1]), (wc[CIN:128, 4, :], tok_w[TAPS - 1]),
                (wqkv[:, :], w_qkv), (wo[:, :], w_out), (wr[:, :], w_router),
                (bqk[:, 0:1], b_qkv[0:D].unsqueeze(1)), (bqk[:, 1:2], b_qkv[D:2 * D].unsqueeze(1)),
                (rowb[:, 0, :], tok_b.partition_broadcast(128)), (rowb[:, 1, :], b_qkv[2 * D:].partition_broadcast(128)),
                (rowb[:, 2, :], b_out.partition_broadcast(128)), (rowb[:, 3, :], ln_g.partition_broadcast(128)),
                (rowb[:, 4, :], ln_b.partition_broadcast(128)), (brow[:, :], b_router.partition_broadcast(128)),
                (lam_row_in[:, :], decay.partition_broadcast(128)),
            ] + [(lam_in[E * h:E * h + E, :], decay[h:h + 1].partition_broadcast(E)) for h in range(H)]:
                eng.dma_start(dst, src).then_inc(S["weights_in"], 16)
                n += 1
            assert n == N_WEIGHTS

            def store_rows(b):
                hold(eng, "hn2_done", b.count(2, 2))
                hold(eng, "probs_row", b.count(1, 1))
                eng.dma_start(rows[bass.ds(b.index() * LO, LO), :].rearrange("(c p) d -> p c d", p=C),
                              row[:, b.par, :, :]).then_inc(row_out[b.par], 16)

            def part(stage, what, b):
                if (stage, what) == ("A", "x"):
                    hold(eng, "xt_ps", b.count(2, 2, back=2))
                    for t in range(2):
                        eng.dma_start(xw[:, b.par, :, t * CIN:(t + 1) * CIN],
                                      x[b.index(), t:t + L - 1, :].rearrange("(c p) d -> p c d", p=XC)
                                      ).then_inc(x_in[b.par], 16)
                if (stage, what) == ("C", "hn"):
                    hold(eng, "h2_done", b.count(2, 2))
                    eng.dma_start(out[b.index(), :, :].rearrange("(c p) d -> p c d", p=C),
                                  h2[:, b.par, :, :]).then_inc(h2_out[b.par], 16)
                if (stage, what) == ("C", "w") and not (isinstance(b.m, int) and b.index() == 0):
                    store_rows(BEFORE(b))
            run(eng, part)
            store_rows(Batch(NB // 2 - 1, 1))
            for g in range(NG):
                for k in range(3):
                    n = FC if k < 2 else FC - 1
                    eng.dma_start(bup[0:n, g, k:k + 1], b_up[g, k * FC:k * FC + n].unsqueeze(1)).then_inc(S["bup_in"], 16)

            def part2(stage, what, e):
                if (stage, what) == ("I", "mask"):
                    hold(eng, "up_ps", e.count(3, 3, back=2))
                    hold(eng, "dn_ps", e.count(1, 1, back=2))
                    w = wdn[:, e.par, :, :]
                    n = e.index()
                    eng.dma_start(wup[:, e.par, :], w_up[e.m, :, :]).then_inc(w_in[e.par], 16)
                    eng.dma_start(w[:, 0:2, :], w_down[n, 0:2 * FC, :].rearrange("(k p) d -> p k d", p=FC)
                                  ).then_inc(w_in[e.par], 16)
                    eng.dma_start(w[0:FC - 1, 2, :], w_down[n, 2 * FC:F, :]).then_inc(w_in[e.par], 16)
                    eng.dma_start(w[FC - 1:FC, 2, :], b_down[bass.ds(n, 1), :]).then_inc(w_in[e.par], 16)
            run2(eng, part2)
            eng.wait_ge(y_out, 16 * 3 * NE)

        @block.gpsimd
        def _(eng):
            made = [0]

            def step(ins):
                made[0] += 1
                ins.then_inc(S["consts_pool"], 1)
                eng.wait_ge(S["consts_pool"], made[0])

            eng.memset(ones[:, :], 1.0).then_inc(S["consts_pool"], 1)
            eng.memset(v1[:, :, :, :, :], 1.0).then_inc(S["consts_pool"], 1)
            eng.memset(expo[:, 0, :], -0.5).then_inc(S["consts_pool"], 1)
            eng.memset(expo[:, 1, :], 0.5).then_inc(S["consts_pool"], 1)
            eng.memset(cexp[:, :], float(C)).then_inc(S["consts_pool"], 1)
            eng.memset(expo[:, 2, :], EPS_LN).then_inc(S["consts_pool"], 1)
            made[0] = 6
            eng.memset(ident[:, :], 0.0).then_inc(S["consts_pool"], 1)
            eng.memset(causal[:, :], 1.0).then_inc(S["consts_pool"], 1)
            eng.memset(head4[:, :], 1.0).then_inc(S["consts_pool"], 1)
            made[0] = 9
            step(eng.memset(blk[:, :], 1.0))
            step(eng.affine_select(out=ident[:, :], in_=ident[:, :], compare_op=ALU.not_equal, fill=1.0, base=0,
                                   pattern=[[-1, 128]], channel_multiplier=1))
            step(eng.affine_select(out=causal[:, :], in_=causal[:, :], compare_op=ALU.is_ge, fill=0.0, base=0,
                                   pattern=[[1, C]], channel_multiplier=-1))
            for g in range(2):
                w = head4[64 * g:64 * g + 64, :]
                step(eng.affine_select(out=w, in_=w, compare_op=ALU.is_ge, fill=0.0, base=0,
                                       pattern=[[-E, 4]], channel_multiplier=1))
                step(eng.affine_select(out=w, in_=w, compare_op=ALU.is_ge, fill=0.0, base=E - 1,
                                       pattern=[[E, 4]], channel_multiplier=-1))
            b3 = blk[:, :].rearrange("p (h e) -> p h e", h=H)
            step(eng.affine_select(out=b3, in_=b3, compare_op=ALU.is_ge, fill=0.0, base=0,
                                   pattern=[[-E, H], [0, E1]], channel_multiplier=1))
            step(eng.affine_select(out=b3, in_=b3, compare_op=ALU.is_ge, fill=0.0, base=E - 1,
                                   pattern=[[E, H], [0, E1]], channel_multiplier=-1))
            eng.iota(steps[:, :], pattern=[[1, C]], base=0, channel_multiplier=0,
                     allow_small_or_imprecise_dtypes=True).then_inc(S["consts_pool"], 1)
            eng.iota(steps_neg[:, :], pattern=[[-1, C]], base=0, channel_multiplier=0,
                     allow_small_or_imprecise_dtypes=True).then_inc(S["consts_pool"], 1)
            made[0] += 2
            step(eng.iota(step_cols[:, :], pattern=[[0, H]], base=C, channel_multiplier=-1,
                          allow_small_or_imprecise_dtypes=True))
            step(eng.memset(same_expert[:, :], 0.0))
            for k in range(-3, 4):
                step(eng.affine_select(out=same_expert[:, :], in_=same_expert[:, :], compare_op=ALU.not_equal, fill=1.0,
                                       base=NE * k, pattern=[[-1, 128]], channel_multiplier=1))
            eng.memset(onesb[:, :], 1.0).then_inc(S["consts_pool"], 1)
            eng.memset(chunkb[:, :], float(C)).then_inc(S["consts_pool"], 1)
            eng.memset(mask[:, :], 0.0).then_inc(S["consts_pool"], 1)
            eng.memset(act[:, :, :, :], 1.0).then_inc(S["consts_pool"], 1)
            eng.memset(bit[:, :], 1 << 29).then_inc(S["consts_pool"], 1)
            made[0] += 5
            for m in (above, upto, before):
                step(eng.memset(m[:, :], 1.0))
            step(eng.affine_select(out=above[:, :], in_=above[:, :], compare_op=ALU.is_gt, fill=0.0, base=0,
                                   pattern=[[-1, C]], channel_multiplier=1))
            step(eng.affine_select(out=upto[:, :], in_=upto[:, :], compare_op=ALU.is_ge, fill=0.0, base=0,
                                   pattern=[[1, C]], channel_multiplier=-1))
            step(eng.affine_select(out=before[:, :], in_=before[:, :], compare_op=ALU.is_gt, fill=0.0, base=0,
                                   pattern=[[1, NJ]], channel_multiplier=-1))
            step(eng.iota(slots_h[:, :], pattern=[[1, CAP + 1]], base=0, channel_multiplier=0,
                          allow_small_or_imprecise_dtypes=True))
            step(eng.iota(slots_f[:, :], pattern=[[1, CAP + 1]], base=0, channel_multiplier=0,
                          allow_small_or_imprecise_dtypes=True))
            assert made[0] == N_CONSTS
            eng.wait_ge(S["lam_done"], 4)
            lb = lam[:, :].to_broadcast([128, C])
            eng.tensor_tensor(dq[:, :], lb, steps[:, :], ALU.pow).then_inc(S["decays_done"], 1)
            eng.tensor_tensor(dk[:, :], lb, steps_neg[:, :], ALU.pow).then_inc(S["decays_done"], 1)
            eng.tensor_tensor(dks8[:, :], lam_row[:, :], step_cols[:, :], ALU.pow).then_inc(S["decays_done"], 1)
            eng.tensor_tensor(lamc[:, :], lam[:, :], cexp[:, :], ALU.pow).then_inc(S["decays_done"], 1)
            eng.wait_ge(S["decays_done"], 4)
            eng.tensor_scalar(dq[:, :], dq[:, :], float(E) ** -0.5, None, ALU.mult).then_inc(S["decays_done"], 1)
            eng.wait_ge(S["decays_done"], 5)

            def part(stage, what, b):
                if (stage, what) == ("A", "w"):
                    need(eng, "wsum_sb", b.count(1, 1))
                    eng.tensor_tensor(wnorm[:, 1, :], wnorm[:, 0, :], expo[0:C, 1, :], ALU.pow).then_inc(S["wnorm_done"], 1)
                if (stage, what) == ("A", "h1"):
                    need(eng, "ve1_done", b.count(1, 1))
                    need(eng, "hn_done", b.count(2, 2, back=1))
                    eng.tensor_tensor(ve1[:, :], ve1[:, :], expo[0:C, 2, :], ALU.add).then_inc(S["eps1_done"], 1)
                    need(eng, "eps1_done", b.count(1, 1))
                    eng.tensor_tensor(rs1[:, :], ve1[:, :], expo[0:C, 0, :], ALU.pow).then_inc(S["rs1_done"], 1)
                if stage == "S":
                    c = what
                    hold(eng, "p1_raw", b.count(7, c + 1))
                    w = P[:, c % 2, 4:8, :]
                    eng.affine_select(out=w, in_=w, compare_op=ALU.is_ge, fill=0.0, base=0,
                                      pattern=[[0, 4], [1, C]], channel_multiplier=-1).then_inc(S["p1_done"], 1)
                if (stage, what) == ("C", "o"):
                    need(eng, "h2_done", b.count(2, 2, back=1))
                    eng.tensor_tensor(hb[:, :, :], hres[:, b.par, :, :],
                                      rowb[0:C, 4:5, :].to_broadcast([C, NC, D]), ALU.add).then_inc(S["hb_done"], 1)
                if (stage, what) == ("C", "z"):
                    need(eng, "ve2_done", b.count(1, 1))
                    need(eng, "zn_done", b.count(2, 2, back=1))
                    eng.tensor_tensor(ve2[:, :], ve2[:, :], expo[0:C, 2, :], ALU.add).then_inc(S["eps2_done"], 1)
                    need(eng, "eps2_done", b.count(1, 1))
                    eng.tensor_tensor(rs2[:, :], ve2[:, :], expo[0:C, 0, :], ALU.pow).then_inc(S["rs2_done"], 1)
                if (stage, what) == ("C", "norm"):
                    need(eng, "ve3_done", b.count(1, 1))
                    need(eng, "hn2_done", b.count(2, 2, back=1))
                    eng.tensor_tensor(ve3[:, :], ve3[:, :], expo[0:C, 2, :], ALU.add).then_inc(S["eps3_done"], 1)
                    need(eng, "eps3_done", b.count(1, 1))
                    eng.tensor_tensor(rs3[:, :], ve3[:, :], expo[0:C, 0, :], ALU.pow).then_inc(S["rs3_done"], 1)
            eng.wait_ge(S["weights_in"], 16 * N_WEIGHTS)
            run(eng, part)
            for p in range(2):
                eng.wait_ge(h2_out[p], 16 * NB // 2)
                eng.wait_ge(row_out[p], 16 * NB // 2)
            out_rows = out.rearrange("b t d -> (b t) d")

            def rows_of(t):
                return SL if t < 2 else CAP - 2 * SL

            def part2(stage, what, e):
                if (stage, what) == ("I", "idx"):
                    hold(eng, "idx_done", e.count(1, 1))
                    hold(eng, "xgt_ps", e.count(1, 1, back=2))
                    hold(eng, "gcol_done", e.count(2, 2, back=2))
                    for t in range(3):
                        n = rows_of(t)
                        eng.indirect_dma_start(
                            out=xg[0:n, e.par, t, :], out_offset=None, in_=rows[:, :],
                            in_offset=bass.IndirectOffsetOnAxis(ap=idx[0:n, e.k, t:t + 1], axis=0)
                        ).then_inc(x_got[e.par], 16)
                if (stage, what) == ("F", "out"):
                    hold(eng, "yw_done", e.count(2, 2))
                    hold(eng, y_out, e.count(48, 0))
                    for t in range(3):
                        n = rows_of(t)
                        eng.indirect_dma_start(
                            out=out_rows, out_offset=bass.IndirectOffsetOnAxis(ap=idx[0:n, e.k, t:t + 1], axis=0),
                            in_=yw[0:n, e.par, t, :], in_offset=None, compute_op=ALU.add).then_inc(y_out, 16)
            run2(eng, part2)

        @block.scalar
        def _(eng):
            eng.wait_ge(S["weights_in"], 16 * N_WEIGHTS)
            eng.wait_ge(S["consts_pool"], N_CONSTS)
            eng.activation(lam[:, :], lam_in[:, :], ACT.Exp, scale=-1.0).then_inc(S["lam_exp"], 1)
            eng.activation(lam_row[:, :], lam_row_in[:, :], ACT.Exp, scale=-1.0).then_inc(S["lam_exp"], 1)

            def part(stage, what, b):
                if (stage, what) == ("A", "x"):
                    for half in range(2):
                        lo, hi = HALF[half]
                        need(eng, "xt_ps", b.count(2, half + 1))
                        need(eng, "sq_done", b.count(1, 1, back=1))
                        need(eng, "conv_ps", b.count(2, 2, back=1))
                        eng.activation(xT[:, lo * XC:hi * XC], pa[half][:, 0:(hi - lo) * XC],
                                       ACT.Copy).then_inc(S["xt_sb"], 1)
                    need(eng, "xt_sb", b.count(2, 2))
                    need(eng, "win_done", b.count(3, 3, back=1))
                    eng.activation(sq[:, :], xT[:, :], ACT.Square).then_inc(S["sq_done"], 1)
                if (stage, what) in (("A", "h0"), ("A", "h1")):
                    need(eng, "scale_step", b.count(3, 3))
                    for half in [int(what[1])]:
                        need(eng, "conv_ps", b.count(2, half + 1))
                        need(eng, "h_done", b.count(2, half + 1, back=1))
                        for c in chunks(half):
                            k = c - HALF[half][0]
                            eng.activation(y[:, c, :], pa[half][0:C, k * D:(k + 1) * D], ACT.Tanh,
                                           scale=wnorm[:, 3, c:c + 1]).then_inc(S["tanh_done"], 1)
                if (stage, what) == ("A", "hnT"):
                    for half in range(2):
                        lo, hi = HALF[half]
                        need(eng, "hnt_ps", b.count(2, half + 1))
                        need(eng, "v_ps", b.count(2, 2, back=1))
                        eng.activation(hnT[:, lo * C:hi * C], pa[half][:, 0:(hi - lo) * C],
                                       ACT.Copy).then_inc(S["hnt_sb"], 1)
                if (stage, what) == ("A", "qk"):
                    for n in range(4):
                        w, half = n // 2, n % 2
                        need(eng, "qk_ps", b.count(4, n + 1))
                        need(eng, "f_done", b.count(4, n + 1, back=1))
                        cols = slice(half * QH, half * QH + QH)
                        eng.activation(tqk[:, w, cols], pa[half][:, 0:QH], ACT.Identity,
                                       bias=bqk[:, w:w + 1]).then_inc(S["t_sb"], 1)
                        need(eng, "t_sb", b.count(4, n + 1))
                        eng.activation(eqk[:, w, cols], tqk[:, w, cols], ACT.Exp).then_inc(S["e_sb"], 1)
                if (stage, what) == ("A", "kt"):
                    need(eng, "qd_done", b.count(1, 1))
                    need(eng, "s_ps", b.count(14, 14, back=2))
                    for j in range(4):
                        eng.activation(qb[:, b.par, j, :], qd[:, b.par, :], ACT.Copy, scale=head4[:, j:j + 1]
                                       ).then_inc(S["qb_done"], 1)
                if stage == "S":
                    c = what
                    need(eng, "s_ps", b.count(14, 2 * c + 2))
                    need(eng, "o_ps", b.count(7, c - 1))
                    eng.activation(P[:, c % 2, 4:8, :], ps[1][0:C, 0:4 * C].rearrange("p (h t) -> p h t", h=4),
                                   ACT.Copy).then_inc(S["p1_raw"], 1)
                if (stage, what) == ("C", "o"):
                    for half in range(2):
                        lo, hi = HALF[half]
                        need(eng, "ot_ps", b.count(2, half + 1))
                        need(eng, "wo_ps", b.count(2, 2, back=1))
                        eng.activation(oT[:, lo * C:hi * C], pc[half][:, 0:(hi - lo) * C],
                                       ACT.Copy).then_inc(S["ot_sb"], 1)
                if (stage, what) == ("C", "t"):
                    for half in range(2):
                        lo, hi = HALF[half]
                        need(eng, "h2t_ps", b.count(2, half + 1))
                        need(eng, "r_ps", b.count(2, 2, back=1))
                        eng.activation(h2T[:, lo * C:hi * C], pc[half][:, 0:(hi - lo) * C],
                                       ACT.Copy).then_inc(S["h2t_sb"], 1)
                if (stage, what) == ("C", "soft"):
                    need(eng, "lsub_done", b.count(1, 1))
                    eng.activation(lg[:, :, :], lg[:, :, :], ACT.Exp).then_inc(S["lexp_done"], 1)
            run(eng, part)
            for n in range(1, JS // 4, 2):
                eng.wait_ge(S["seg_ps"], n + 1)
                eng.activation(seg_probs[:, n * 4 * C:(n + 1) * 4 * C], SEG_BANKS[n][:, 0:4 * C],
                               ACT.Copy).then_inc(S["seg_act"], 1)
            eng.wait_ge(S["bup_in"], 16 * 3 * NG)

            def part2(stage, what, e):
                if (stage, what) == ("F", "x"):
                    need(eng, "xgt_ps", e.count(1, 1))
                    need(eng, "up_ps", e.count(3, 3, back=1))
                    eng.activation(xgT[:, :], p_xg[:, 0:CAP], ACT.Copy).then_inc(S["xgt_sb"], 1)
                if (stage, what) == ("F", "up"):
                    need(eng, "dn_ps", e.count(1, 1, back=2))
                    for k in range(3):
                        n = FC if k < 2 else FC - 1
                        hold(eng, "up_ps", e.count(3, k + 1))
                        eng.activation(act[0:n, e.par, k, :], p_up[k][0:n, 0:CAP], ACT.Silu,
                                       bias=bup[0:n, e.m, k:k + 1]).then_inc(S["act_done"], 1)
                if (stage, what) == ("I", "reach"):
                    need(eng, "dcum_ps", e.count(1, 1))
                    need(eng, "cum_ps", e.count(1, 1, back=1))
                    eng.activation(dcum[:, :, :], p_dcum[0:NJ, 0:2 * C].rearrange("p (h t) -> p h t", h=2),
                                   ACT.Copy).then_inc(S["dcum_sb"], 1)
            run2(eng, part2)

        @block.tensor
        def _(eng):
            eng.wait_ge(S["weights_in"], 16 * N_WEIGHTS)
            eng.wait_ge(S["consts_pool"], N_CONSTS)

            def part(stage, what, b):
                if (stage, what) == ("A", "x"):
                    need(eng, x_in[b.par], b.m * 32 + 32)
                    for half in range(2):
                        need(eng, "kt_sb", b.count(2, half + 1, back=1))
                        for c in chunks(half):
                            k = c - HALF[half][0]
                            mm = eng.transpose(pa[half][:, k * XC:(k + 1) * XC], xw[:, b.par, c, :], ident[0:XC, 0:XC])
                        mm.then_inc(S["xt_ps"], 1)
                if (stage, what) == ("A", "w"):
                    need(eng, "win_done", b.count(3, 3))
                    need(eng, "stm_done", Batch.count(BEFORE(b), 5, WSUM_AT - 1))
                    for c in range(NC):
                        mm = eng.matmul(pst[0:C, c:c + 1], sq4[:, c * C:(c + 1) * C], ones[:, :], start=True, stop=True)
                    mm.then_inc(S["wsum_ps"], 1)
                if (stage, what) in (("A", "conv0"), ("A", "conv1")):
                    need(eng, "xt_sb", b.count(2, 2))
                    for half in [int(what[4])]:
                        for c in chunks(half):
                            k = c - HALF[half][0]
                            dst = pa[half][0:C, k * D:(k + 1) * D]
                            for t in range(4):
                                a = c * C + 2 * t
                                eng.matmul(dst, xT[:, a:a + C], wc[:, t, :], start=(t == 0), stop=False)
                            a = c * C + TAPS - 2
                            mm = eng.matmul(dst, xT[CIN:128, a:a + C], wc[CIN:128, 4, :], start=False, stop=True)
                        mm.then_inc(S["conv_ps"], 1)
                if (stage, what) == ("A", "hnT"):
                    for half in range(2):
                        need(eng, "hn_done", b.count(2, half + 1))
                        need(eng, "tanh_done", b.count(NC, HALF[half][1]))
                        for c in chunks(half):
                            k = c - HALF[half][0]
                            mm = eng.transpose(pa[half][:, k * C:(k + 1) * C], hn[:, c, :], ident[0:C, 0:C])
                        mm.then_inc(S["hnt_ps"], 1)
                if (stage, what) == ("A", "qk"):
                    for n in range(4):
                        w, half = n // 2, n % 2
                        need(eng, "hnt_sb", b.count(2, 2 if half or w else 1))
                        if w:
                            need(eng, "t_sb", b.count(4, half + 1))
                        eng.matmul(pa[half][:, 0:QH], wqkv[:, w * D:(w + 1) * D], hnT[:, half * QH:half * QH + QH],
                                   start=True, stop=True).then_inc(S["qk_ps"], 1)
                if (stage, what) == ("A", "v"):
                    for half in range(2):
                        need(eng, "t_sb", b.count(4, half + 3))
                        for c in chunks(half):
                            k = c - HALF[half][0]
                            mm = eng.matmul(pa[half][0:C, k * D:(k + 1) * D], hnT[:, c * C:(c + 1) * C],
                                            wqkv[:, 2 * D:3 * D], start=True, stop=True)
                        mm.then_inc(S["v_ps"], 1)
                if (stage, what) == ("A", "kt"):
                    need(eng, "f_done", b.count(4, 4))
                    for half in range(2):
                        need(eng, "v_sb", b.count(2, half + 1))
                        for c in chunks(half):
                            k = c - HALF[half][0]
                            mm = eng.transpose(pa[half][0:C, k * D:(k + 1) * D], fqk[:, 1, c * C:(c + 1) * C], ident[:, :])
                        mm.then_inc(S["kt_ps"], 1)
                if stage == "S":
                    c = what
                    tok = slice(c * C, (c + 1) * C)
                    if c == 0:
                        need(eng, "qb_done", b.count(4, 4))
                        need(eng, "kd_done", b.count(1, 1))
                        need(eng, "kt_sb", b.count(2, 2))
                        need(eng, "v_sb", b.count(2, 2))
                    for g in range(2):
                        need(eng, ["p0_done", "p1_raw"][g], b.count(7, c))
                        eng.matmul(ps[g][0:C, 0:4 * C], kd[64 * g:64 * g + 64, b.par, tok],
                                   qb[64 * g:64 * g + 64, b.par, :, tok], start=True, stop=True).then_inc(S["s_ps"], 1)
                    if c < NC - 1:
                        if c == 1:
                            need(eng, "state_done", b.count(6, 1))
                        else:
                            need(eng, "stm_done", b.count(5, c - 1) if c else b.count(5, 5, back=1))
                        if c == WSUM_AT and not (isinstance(b.m, int) and b.index() == NB - 1):
                            need(eng, "wsum_sb", AFTER(b).count(1, 1))
                        eng.matmul(pst[:, 0:H * E1], kt[:, b.par, c, :],
                                   v1[:, b.par, c, :, :].rearrange("p h e -> p (h e)"),
                                   start=True, stop=True).then_inc(S["st_ps"], 1)
                if stage == "V":
                    c = what
                    tok = slice(c * C, (c + 1) * C)
                    need(eng, "o_done", b.count(7, c))
                    if c > 0:
                        need(eng, "state_done", b.count(6, c))
                        eng.matmul(po[0:C, 0:H * E1], qd[:, b.par, tok], state[:, c % 3, :], start=True, stop=False,
                                   skip_group_check=True)
                    for h in range(H):
                        if h % 4 == 0:
                            need(eng, ["p0_done", "p1_done"][h // 4], b.count(7, c + 1))
                        mm = eng.matmul(po[0:C, h * E1:(h + 1) * E1], P[:, c % 2, h, :], v1[:, b.par, c, h, :],
                                        start=(c == 0 and h == 0), stop=(h == H - 1), skip_group_check=True)
                    mm.then_inc(S["o_ps"], 1)
                if (stage, what) == ("C", "o"):
                    for half in range(2):
                        need(eng, "o_done", b.count(7, HALF[half][1]))
                        need(eng, "lg_done", b.count(2, half + 1, back=1))
                        for c in chunks(half):
                            k = c - HALF[half][0]
                            mm = eng.transpose(pc[half][:, k * C:(k + 1) * C], o[:, b.par, c, :], ident[0:C, 0:C])
                        mm.then_inc(S["ot_ps"], 1)
                if (stage, what) == ("C", "w"):
                    for half in range(2):
                        need(eng, "ot_sb", b.count(2, half + 1))
                        for c in chunks(half):
                            k = c - HALF[half][0]
                            mm = eng.matmul(pc[half][0:C, k * D:(k + 1) * D], oT[:, c * C:(c + 1) * C], wo[:, :],
                                            start=True, stop=True)
                        mm.then_inc(S["wo_ps"], 1)
                if (stage, what) == ("C", "t"):
                    for half in range(2):
                        need(eng, "hn2_done", b.count(2, half + 1))
                        need(eng, "z_done", b.count(2, half + 1))
                        for c in chunks(half):
                            k = c - HALF[half][0]
                            mm = eng.transpose(pc[half][:, k * C:(k + 1) * C], row[:, b.par, c, 0:D], ident[0:C, 0:C])
                        mm.then_inc(S["h2t_ps"], 1)
                if (stage, what) == ("C", "r"):
                    for half in range(2):
                        need(eng, "h2t_sb", b.count(2, half + 1))
                        for c in chunks(half):
                            k = c - HALF[half][0]
                            mm = eng.matmul(pc[half][0:C, k * NE:(k + 1) * NE], h2T[:, c * C:(c + 1) * C], wr[:, :],
                                            start=True, stop=True)
                        mm.then_inc(S["r_ps"], 1)
            run(eng, part)
            eng.wait_ge(S["probs_done"], NB)
            for n in range(JS // 4):
                for k in range(4):
                    j = 4 * (4 * n + k)
                    mm = eng.transpose(SEG_BANKS[n][:, k * C:(k + 1) * C],
                                       probs[:, j:j + 4, :].rearrange("p j e -> p (j e)"), ident[0:C, 0:C])
                mm.then_inc(S["seg_ps"], 1)
            with eng.Fori(0, BITS // 2) as r:
                for k in range(2):
                    need(eng, "hits_done", r * 2 + (k + 1))
                    eng.matmul(pst[:, 0:1], same_expert[:, :], hits[:, :], start=True, stop=True).then_inc(S["hits_ps"], 1)
            eng.wait_ge(S["thr_step"], 1)
            eng.transpose(pst[0:C, 0:NE], thr_wide[:, :], ident[0:NE, 0:NE]).then_inc(S["thr_ps"], 1)

            def part2(stage, what, e):
                if (stage, what) == ("F", "x"):
                    need(eng, x_got[e.par], e.half() * 48)
                    need(eng, "xgt_sb", e.count(1, 1, back=1))
                    for t in range(3):
                        n = SL if t < 2 else CAP - 2 * SL
                        mm = eng.transpose(p_xg[:, t * SL:t * SL + n], xg[0:n, e.par, t, 0:D], ident[0:n, 0:n])
                    mm.then_inc(S["xgt_ps"], 1)
                if (stage, what) == ("F", "up"):
                    need(eng, w_in[e.par], e.half() * 64)
                    need(eng, "xgt_sb", e.count(1, 1))
                    for k in range(3):
                        n = FC if k < 2 else FC - 1
                        need(eng, "act_done", e.count(3, k + 1, back=1))
                        eng.matmul(p_up[k][0:n, 0:CAP], wup[:, e.par, k * FC:k * FC + n], xgT[:, :],
                                   start=True, stop=True).then_inc(S["up_ps"], 1)
                if (stage, what) == ("F", "down"):
                    need(eng, "yw_done", e.count(2, 2, back=1))
                    need(eng, "act_done", e.count(3, 3))
                    for t in range(3):
                        n = SL if t < 2 else CAP - 2 * SL
                        for k in range(3):
                            mm = eng.matmul(p_dn[0:n, t * D:(t + 1) * D], act[:, e.par, k, t * SL:t * SL + n],
                                            wdn[:, e.par, k, :], start=(k == 0), stop=(k == 2))
                    mm.then_inc(S["dn_ps"], 1)
                if (stage, what) == ("I", "cnt"):
                    need(eng, "mask_done", e.count(2, 2))
                    need(eng, "idx_done", e.count(1, 1, back=1))
                    for h in range(2):
                        mm = eng.matmul(p_small[0:NJ, h:h + 1], mask[:, 1 + h * NJ:1 + (h + 1) * NJ], onesb[0:C, 0:1],
                                        start=True, stop=True)
                    mm.then_inc(S["cnt_ps"], 1)
                    need(eng, "dcum_sb", e.count(1, 1, back=1))
                    for h in range(2):
                        eng.matmul(p_dcum[0:NJ, h * C:(h + 1) * C], mask[:, h * NJ:(h + 1) * NJ], above[:, :],
                                   start=True, stop=False)
                        mm = eng.matmul(p_dcum[0:NJ, h * C:(h + 1) * C], mask[:, 1 + h * NJ:1 + (h + 1) * NJ], upto[:, :],
                                        start=False, stop=True)
                    mm.then_inc(S["dcum_ps"], 1)
                if (stage, what) == ("I", "reach"):
                    need(eng, "cnt_sb", e.count(1, 1))
                    eng.matmul(p_small[0:NJ, 2:3], before[:, :], cnt[:, 0:1], start=True, stop=True)
                    eng.matmul(p_small[0:NJ, 3:4], before[:, :], cnt[:, 1:2], start=True, stop=False)
                    eng.matmul(p_small[0:NJ, 3:4], onesb[0:NJ, 0:NJ], cnt[:, 0:1], start=False, stop=True
                               ).then_inc(S["cex_ps"], 1)
                if (stage, what) == ("I", "cum"):
                    need(eng, "reach_done", e.count(2, 2))
                    need(eng, "dcum_sb", e.count(1, 1))
                    need(eng, "inside_done", e.count(1, 1, back=1))
                    for h in range(2):
                        mm = eng.matmul(p_cum[0:C, 0:CAP + 1], dcum[:, h, :], reach[:, h, :], start=(h == 0), stop=(h == 1))
                    mm.then_inc(S["cum_ps"], 1)
                if (stage, what) == ("I", "idx"):
                    need(eng, "inside_done", e.count(1, 1))
                    for t in range(3):
                        sl = slice(t * SL, (t + 1) * SL)
                        dst = p_small[0:SL, 4 + t:5 + t]
                        eng.matmul(dst, inside[:, sl], onesb[0:C, 0:1], start=True, stop=False)
                        eng.matmul(dst, reach[:, 0, sl], chunkb[0:NJ, :], start=False, stop=False)
                        mm = eng.matmul(dst, reach[:, 1, sl], chunkb[0:NJ, :], start=False, stop=True)
                    mm.then_inc(S["idx_ps"], 1)
            run2(eng, part2)

        @block.vector
        def _(eng):
            eng.wait_ge(S["lam_exp"], 2)
            eng.tensor_scalar(lam[:, :], lam[:, :], 1.0, None, ALU.add).then_inc(S["lam_done"], 1)
            eng.tensor_scalar(lam_row[:, :], lam_row[:, :], 1.0, None, ALU.add).then_inc(S["lam_done"], 1)
            eng.wait_ge(S["lam_done"], 2)
            eng.reciprocal(lam[:, :], lam[:, :]).then_inc(S["lam_done"], 1)
            eng.reciprocal(lam_row[:, :], lam_row[:, :]).then_inc(S["lam_done"], 1)
            eng.wait_ge(S["decays_done"], 5)
            eng.wait_ge(S["weights_in"], 16 * N_WEIGHTS)
            eng.wait_ge(S["consts_pool"], N_CONSTS)

            def norm(b, src, st, mv, ve, tmp, steps_done, ve_done, root_done, last_read):
                need(eng, last_read, b.count(2, 2, back=1))
                need(eng, root_done, b.count(1, 1, back=1))
                base = NC + 5
                for c in range(NC):
                    eng.bn_stats(st[:, c, :], src(c)).then_inc(S[steps_done], 1)
                need(eng, steps_done, b.count(base, NC))
                eng.tensor_tensor(tmp[:, 0, :], st[:, :, 1], st[:, :, 4], ALU.add).then_inc(S[steps_done], 1)
                eng.tensor_tensor(tmp[:, 1, :], st[:, :, 1], st[:, :, 4], ALU.subtract).then_inc(S[steps_done], 1)
                eng.tensor_tensor(tmp[:, 2, :], st[:, :, 2], st[:, :, 5], ALU.add).then_inc(S[steps_done], 1)
                need(eng, steps_done, b.count(base, NC + 3))
                eng.tensor_scalar(mv[:, :], tmp[:, 0, :], 0.5, None, ALU.mult).then_inc(S[steps_done], 1)
                eng.scalar_tensor_tensor(out=tmp[:, 1, :], in0=tmp[:, 1, :], scalar=0.25, in1=tmp[:, 1, :],
                                         op0=ALU.mult, op1=ALU.mult).then_inc(S[steps_done], 1)
                need(eng, steps_done, b.count(base, NC + 5))
                eng.scalar_tensor_tensor(out=ve[:, :], in0=tmp[:, 2, :], scalar=1.0 / D, in1=tmp[:, 1, :],
                                         op0=ALU.mult, op1=ALU.add).then_inc(S[ve_done], 1)

            def part(stage, what, b):
                if (stage, what) == ("A", "win"):
                    need(eng, "sq_done", b.count(1, 1))
                    need(eng, "wsum_ps", b.count(1, 1, back=1))
                    eng.tensor_tensor(sq2[:, 0:L - 3], sq[:, 0:L - 3], sq[:, 2:L - 1], ALU.add).then_inc(S["win_done"], 1)
                    need(eng, "win_done", b.count(3, 1))
                    eng.tensor_tensor(sq4[:, :], sq2[:, 0:LO], sq2[:, 4:LO + 4], ALU.add).then_inc(S["win_done"], 1)
                    need(eng, "win_done", b.count(3, 2))
                    eng.tensor_tensor(sq4[CIN:128, :], sq4[CIN:128, :], sq[CIN:128, TAPS - 2:TAPS - 2 + LO],
                                      ALU.add).then_inc(S["win_done"], 1)
                if (stage, what) == ("A", "w"):
                    need(eng, "wsum_ps", b.count(1, 1))
                    need(eng, "wnorm_done", b.count(1, 1, back=1))
                    eng.tensor_scalar(wnorm[:, 0, :], pst[0:C, 0:NC], 0.0, None, ALU.max).then_inc(S["wsum_sb"], 1)
                if (stage, what) == ("A", "scale"):
                    need(eng, "wnorm_done", b.count(1, 1))
                    eng.tensor_scalar(wnorm[:, 2, :], wnorm[:, 1, :], EPS_W, None, ALU.add).then_inc(S["scale_step"], 1)
                    need(eng, "scale_step", b.count(3, 1))
                    eng.reciprocal(wnorm[:, 2, :], wnorm[:, 2, :]).then_inc(S["scale_step"], 1)
                    need(eng, "scale_step", b.count(3, 2))
                    need(eng, "tanh_done", b.count(NC, NC, back=1))
                    eng.tensor_scalar(wnorm[:, 3, :], wnorm[:, 2, :], 1.0, LAM, ALU.min, ALU.mult).then_inc(S["scale_step"], 1)
                if (stage, what) in (("A", "h0"), ("A", "h1")):
                    for half in [int(what[1])]:
                        lo, hi = HALF[half]
                        need(eng, "tanh_done", b.count(NC, hi))
                        eng.tensor_tensor(y[:, lo:hi, :], y[:, lo:hi, :], rowb[0:C, 0:1, :].to_broadcast([C, hi - lo, D]),
                                          ALU.add).then_inc(S["ybias_done"], 1)
                        need(eng, "ybias_done", b.count(2, half + 1))
                        need(eng, "hb_done", b.count(1, 1, back=2))
                        eng.tensor_scalar(hres[:, b.par, lo:hi, :], y[:, lo:hi, :], 0.0, None,
                                          ALU.max).then_inc(S["h_done"], 1)
                if (stage, what) == ("A", "h1"):
                    need(eng, "h_done", b.count(2, 2))
                    norm(b, lambda c: hres[:, b.par, c, :], st1, mv1, ve1, tmp1, "stats1", "ve1_done", "rs1_done", "hn_done")
                if (stage, what) == ("A", "hn"):
                    need(eng, "rs1_done", b.count(1, 1))
                    need(eng, "hnt_ps", b.count(2, 2, back=1))
                    for half in range(2):
                        for c in chunks(half):
                            ins = eng.tensor_scalar(hn[:, c, :], hres[:, b.par, c, :], mv1[:, c:c + 1], rs1[:, c:c + 1],
                                                    ALU.subtract, ALU.mult)
                        ins.then_inc(S["hn_done"], 1)
                if (stage, what) == ("A", "qk"):
                    need(eng, "kt_ps", b.count(2, 2, back=1))
                    need(eng, "kd_done", b.count(1, 1, back=1))
                    for n in range(4):
                        w, half = n // 2, n % 2
                        cols = slice(half * QH, half * QH + QH)
                        need(eng, "e_sb", b.count(4, n + 1))
                        eng.tensor_scalar(eqk[:, w, cols], eqk[:, w, cols], 1.0, None, ALU.min).then_inc(S["emin_done"], 1)
                        need(eng, "emin_done", b.count(4, n + 1))
                        eng.scalar_tensor_tensor(out=fqk[:, w, cols], in0=tqk[:, w, cols], scalar=0.0, in1=eqk[:, w, cols],
                                                 op0=ALU.max, op1=ALU.add).then_inc(S["f_done"], 1)
                        if n == 1:
                            need(eng, "f_done", b.count(4, 2))
                            need(eng, "o_ps", b.count(7, 7, back=2))
                            need(eng, "qb_done", b.count(4, 4, back=2))
                            eng.tensor_tensor(qd[:, b.par, :].rearrange("p (c t) -> p c t", c=NC),
                                              fqk[:, 0, :].rearrange("p (c t) -> p c t", c=NC),
                                              dq[:, :].unsqueeze(1).to_broadcast([128, NC, C]),
                                              ALU.mult).then_inc(S["qd_done"], 1)
                    need(eng, "f_done", b.count(4, 4))
                    need(eng, "s_ps", b.count(14, 14, back=2))
                    eng.tensor_tensor(kd[:, b.par, :].rearrange("p (c t) -> p c t", c=NC),
                                      fqk[:, 1, :].rearrange("p (c t) -> p c t", c=NC),
                                      dk[:, :].unsqueeze(1).to_broadcast([128, NC, C]),
                                      ALU.mult).then_inc(S["kd_done"], 1)
                if (stage, what) == ("A", "v"):
                    need(eng, "o_ps", b.count(7, 7, back=2))
                    for half in range(2):
                        lo, hi = HALF[half]
                        need(eng, "v_ps", b.count(2, half + 1))
                        eng.tensor_tensor(v1[:, b.par, lo:hi, :, 0:E],
                                          pa[half][0:C, 0:(hi - lo) * D].rearrange("p (c h e) -> p c h e", h=H, e=E),
                                          rowb[0:C, 1:2, :].to_broadcast([C, hi - lo, D]).rearrange("p c (h e) -> p c h e", h=H),
                                          ALU.add).then_inc(S["v_sb"], 1)
                if (stage, what) == ("A", "kt"):
                    need(eng, "st_ps", b.count(6, 6, back=2))
                    for half in range(2):
                        lo, hi = HALF[half]
                        need(eng, "kt_ps", b.count(2, half + 1))
                        eng.tensor_tensor(kt[:, b.par, lo:hi, :].rearrange("p c (h e) -> p c h e", h=H),
                                          pa[half][0:C, 0:(hi - lo) * D].rearrange("p (c h e) -> p c h e", h=H, e=E),
                                          dks8[0:C, :].unsqueeze(1).unsqueeze(3).to_broadcast([C, hi - lo, H, E]),
                                          ALU.mult).then_inc(S["kt_sb"], 1)
                if stage == "S":
                    c = what
                    need(eng, "s_ps", b.count(14, 2 * c + 1))
                    need(eng, "o_ps", b.count(7, c - 1))
                    eng.tensor_tensor(P[:, c % 2, 0:4, :], ps[0][0:C, 0:4 * C].rearrange("p (h t) -> p h t", h=4),
                                      causal[0:C, :].unsqueeze(1).to_broadcast([C, 4, C]),
                                      ALU.mult).then_inc(S["p0_done"], 1)
                    if c < NC - 1:
                        need(eng, "st_ps", b.count(6, c + 1))
                        if c == 0:
                            need(eng, "o_ps", b.count(7, 7, back=1))
                            need(eng, "state_done", b.count(6, 6, back=1))
                            eng.tensor_tensor(state[:, 1, :], pst[:, 0:H * E1], blk[:, :], ALU.mult).then_inc(S["state_done"], 1)
                        else:
                            need(eng, "state_done", b.count(6, c))
                            eng.tensor_tensor(state_in[:, :], pst[:, 0:H * E1], blk[:, :], ALU.mult).then_inc(S["stm_done"], 1)
                            need(eng, "stm_done", b.count(5, c))
                            need(eng, "o_ps", b.count(7, c - 1))
                            eng.scalar_tensor_tensor(out=state[:, (c + 1) % 3, :], in0=state[:, c % 3, :], scalar=lamc[:, 0:1],
                                                     in1=state_in[:, :], op0=ALU.mult, op1=ALU.add).then_inc(S["state_done"], 1)
                if stage == "V":
                    c = what
                    need(eng, "o_ps", b.count(7, c + 1))
                    if c == 0:
                        need(eng, "ot_ps", b.count(2, 2, back=2))
                    ov = po[0:C, 0:H * E1].rearrange("p (h e) -> p h e", h=H)
                    need(eng, "o_done", b.count(7, c))
                    eng.tensor_scalar(den[:, 0, :], ov[:, :, E], EPS_DEN, None, ALU.add).then_inc(S["den_step"], 1)
                    need(eng, "den_step", b.count(14, 2 * c + 1))
                    eng.reciprocal(den[:, 1, :], den[:, 0, :]).then_inc(S["den_step"], 1)
                    need(eng, "den_step", b.count(14, 2 * c + 2))
                    eng.tensor_tensor(o[:, b.par, c, :].rearrange("p (h e) -> p h e", h=H), ov[:, :, 0:E],
                                      den[:, 1, :].unsqueeze(2).to_broadcast([C, H, E]), ALU.mult).then_inc(S["o_done"], 1)
                if (stage, what) == ("C", "z"):
                    for half in range(2):
                        lo, hi = HALF[half]
                        need(eng, "wo_ps", b.count(2, half + 1))
                        need(eng, "h2_done", b.count(2, 2, back=1))
                        eng.tensor_tensor(z[:, lo:hi, :], pc[half][0:C, 0:(hi - lo) * D].rearrange("p (c d) -> p c d", d=D),
                                          rowb[0:C, 2:3, :].to_broadcast([C, hi - lo, D]), ALU.add).then_inc(S["z_done"], 1)
                    need(eng, "z_done", b.count(2, 2))
                    norm(b, lambda c: z[:, c, :], st2, mv2, ve2, tmp2, "stats2", "ve2_done", "rs2_done", "zn_done")
                if (stage, what) == ("C", "norm"):
                    need(eng, "rs2_done", b.count(1, 1))
                    for half in range(2):
                        lo, hi = HALF[half]
                        for c in chunks(half):
                            ins = eng.tensor_scalar(z[:, c, :], z[:, c, :], mv2[:, c:c + 1], rs2[:, c:c + 1],
                                                    ALU.subtract, ALU.mult)
                        ins.then_inc(S["zn_done"], 1)
                    for half in range(2):
                        lo, hi = HALF[half]
                        need(eng, "zn_done", b.count(2, half + 1))
                        eng.tensor_tensor(z[:, lo:hi, :], z[:, lo:hi, :], rowb[0:C, 3:4, :].to_broadcast([C, hi - lo, D]),
                                          ALU.mult).then_inc(S["zg_done"], 1)
                    need(eng, "hb_done", b.count(1, 1))
                    need(eng, h2_out[b.par], b.m * 16)
                    for half in range(2):
                        lo, hi = HALF[half]
                        need(eng, "zg_done", b.count(2, half + 1))
                        eng.tensor_tensor(h2[:, b.par, lo:hi, :], z[:, lo:hi, :], hb[:, lo:hi, :],
                                          ALU.add).then_inc(S["h2_done"], 1)
                    need(eng, "h2_done", b.count(2, 2))
                    norm(b, lambda c: h2[:, b.par, c, :], st3, mv3, ve3, tmp3, "stats3", "ve3_done", "rs3_done", "hn2_done")
                if (stage, what) == ("C", "hn"):
                    need(eng, "rs3_done", b.count(1, 1))
                    need(eng, row_out[b.par], b.m * 16)
                    need(eng, "h2t_ps", b.count(2, 2, back=2))
                    for half in range(2):
                        for c in chunks(half):
                            ins = eng.tensor_scalar(row[:, b.par, c, 0:D], h2[:, b.par, c, :], mv3[:, c:c + 1], rs3[:, c:c + 1],
                                                    ALU.subtract, ALU.mult)
                        ins.then_inc(S["hn2_done"], 1)
                if (stage, what) == ("C", "max"):
                    need(eng, "probs_done", b.count(1, 1, back=1))
                    need(eng, "probs_row", b.count(1, 1, back=1))
                    for half in range(2):
                        lo, hi = HALF[half]
                        need(eng, "r_ps", b.count(2, half + 1))
                        eng.tensor_tensor(lg[:, lo:hi, :], pc[half][0:C, 0:(hi - lo) * NE].rearrange("p (c e) -> p c e", e=NE),
                                          brow[0:C, :].unsqueeze(1).to_broadcast([C, hi - lo, NE]), ALU.add).then_inc(S["lg_done"], 1)
                    need(eng, "lg_done", b.count(2, 2))
                    eng.tensor_reduce(lmax[:, :], lg[:, :, :], AX.X, ALU.max).then_inc(S["lmax_done"], 1)
                    need(eng, "lmax_done", b.count(1, 1))
                    eng.tensor_tensor(lg[:, :, :], lg[:, :, :], lmax[:, :].unsqueeze(2).to_broadcast([C, NC, NE]),
                                      ALU.subtract).then_inc(S["lsub_done"], 1)
                if (stage, what) == ("C", "soft"):
                    need(eng, "lexp_done", b.count(1, 1))
                    eng.tensor_reduce(lsum[:, 0, :], lg[:, :, :], AX.X, ALU.add).then_inc(S["lsum_done"], 1)
                    need(eng, "lsum_done", b.count(1, 1))
                    eng.reciprocal(lsum[:, 1, :], lsum[:, 0, :]).then_inc(S["lrec_done"], 1)
                    need(eng, "lrec_done", b.count(1, 1))
                    rb = lsum[:, 1, :].unsqueeze(2).to_broadcast([C, NC, NE])
                    eng.tensor_tensor(row[:, b.par, :, D:ROW], lg[:, :, :], rb, ALU.mult).then_inc(S["probs_row"], 1)
                    eng.tensor_tensor(probs[:, bass.ds(b.index() * NC, NC), :], lg[:, :, :], rb,
                                      ALU.mult).then_inc(S["probs_done"], 1)
            run(eng, part)
            for n in range(0, JS // 4, 2):
                eng.wait_ge(S["seg_ps"], n + 1)
                eng.tensor_copy(seg_probs[:, n * 4 * C:(n + 1) * 4 * C], SEG_BANKS[n][:, 0:4 * C]).then_inc(S["seg_dve"], 1)
            eng.wait_ge(S["seg_dve"], (JS // 4 + 1) // 2)
            eng.wait_ge(S["seg_act"], JS // 8)
            steps_per = 4
            eng.memset(thr_bits[:, :], 0).then_inc(S["bit_step"], 1)
            with eng.Fori(0, BITS // 2) as r:
                for k in range(2):
                    def after(n):
                        return r * (2 * steps_per) + (1 + steps_per * k + n)
                    eng.wait_ge(S["bit_step"], after(0))
                    eng.tensor_tensor(cand[:, :], thr_bits[:, :], bit[:, k:k + 1], ALU.bitwise_or).then_inc(S["bit_step"], 1)
                    eng.wait_ge(S["bit_step"], after(1))
                    eng.tensor_scalar(seg_hits[:, :], seg_probs[:, :], cand[:, :].bitcast(f32), None, ALU.is_ge, ALU.add,
                                      accum_out=hits[:, :]).then_inc(S["hits_done"], 1)
                    eng.tensor_scalar(bit[:, 1 - k:2 - k], bit[:, k:k + 1], 1, None,
                                      ALU.logical_shift_right).then_inc(S["bit_step"], 1)
                    eng.wait_ge(S["hits_ps"], r * 2 + (k + 1))
                    eng.tensor_scalar(keep[:, :], pst[:, 0:1], float(CAP), -1.0, ALU.is_ge, ALU.mult).then_inc(S["bit_step"], 1)
                    eng.wait_ge(S["bit_step"], after(3))
                    eng.scalar_tensor_tensor(out=thr_bits[:, :], in0=keep[:, :], scalar=bit[:, k:k + 1], in1=thr_bits[:, :],
                                             op0=ALU.bitwise_and, op1=ALU.bitwise_or).then_inc(S["bit_step"], 1)
            eng.wait_ge(S["bit_step"], 1 + steps_per * BITS)
            eng.tensor_copy(thr_wide[:, :], thr_bits[0:NE, :].bitcast(f32).to_broadcast([NE, C])).then_inc(S["thr_step"], 1)
            eng.wait_ge(S["thr_ps"], 1)
            eng.tensor_copy(thr[:, :], pst[0:C, 0:NE]).then_inc(S["thr_done"], 1)
            eng.wait_ge(S["thr_done"], 1)

            def part2(stage, what, e):
                if (stage, what) == ("I", "mask"):
                    need(eng, "dcum_ps", e.count(1, 1, back=1))
                    own, at = probs[:, :, bass.ds(e.index(), 1)], thr[:, bass.ds(e.index(), 1)]
                    for h, op in enumerate((ALU.is_gt, ALU.is_equal)):
                        eng.tensor_scalar(mask[:, 1 + h * NJ:1 + (h + 1) * NJ].unsqueeze(2), own, at, None, op
                                          ).then_inc(S["mask_done"], 1)
                if (stage, what) == ("F", "x"):
                    need(eng, x_got[e.par], e.half() * 48)
                    need(eng, "yw_done", e.count(2, 2, back=2))
                    own = bass.ds(e.index() + D, 1)
                    eng.tensor_copy(gcol[:, e.par, 0:2].unsqueeze(2), xg[:, e.par, 0:2, own]).then_inc(S["gcol_done"], 1)
                    n = CAP - 2 * SL
                    eng.tensor_copy(gcol[0:n, e.par, 2:3], xg[0:n, e.par, 2, own]).then_inc(S["gcol_done"], 1)
                if (stage, what) == ("I", "cnt"):
                    need(eng, "cnt_ps", e.count(1, 1))
                    need(eng, "cex_ps", e.count(1, 1, back=1))
                    eng.tensor_copy(cnt[:, :], p_small[0:NJ, 0:2]).then_inc(S["cnt_sb"], 1)
                if (stage, what) == ("I", "reach"):
                    need(eng, "cex_ps", e.count(1, 1))
                    need(eng, "reach_done", e.count(2, 2, back=1))
                    eng.tensor_copy(cex[:, :], p_small[0:NJ, 2:4]).then_inc(S["cex_sb"], 1)
                    need(eng, "cex_sb", e.count(1, 1))
                    need(eng, "idx_ps", e.count(1, 1, back=1))
                    for h in range(2):
                        eng.tensor_scalar(reach[:, h, :], slots_h[:, :], cex[:, h:h + 1], None, ALU.is_ge
                                          ).then_inc(S["reach_done"], 1)
                if (stage, what) == ("I", "cum"):
                    need(eng, "cum_ps", e.count(1, 1))
                    eng.tensor_tensor(inside[:, :], p_cum[0:C, 0:CAP + 1], slots_f[:, :], ALU.is_le
                                      ).then_inc(S["inside_done"], 1)
                if (stage, what) == ("I", "idx"):
                    need(eng, "idx_ps", e.count(1, 1))
                    need(eng, "idx_done", e.count(1, 1, back=1))
                    need(eng, y_out, e.count(48, 0, back=3))
                    eng.tensor_scalar(wrap[:, :], p_small[0:SL, 4:7], float(N + C), float(N), ALU.is_ge, ALU.mult
                                      ).then_inc(S["wrap_done"], 1)
                    need(eng, "wrap_done", e.count(1, 1))
                    eng.scalar_tensor_tensor(out=idx[:, e.k, :], in0=p_small[0:SL, 4:7], scalar=-float(C), in1=wrap[:, :],
                                             op0=ALU.add, op1=ALU.subtract).then_inc(S["idx_done"], 1)
                if (stage, what) == ("F", "out"):
                    need(eng, "dn_ps", e.count(1, 1))
                    need(eng, y_out, e.count(48, 48, back=2))
                    need(eng, "gcol_done", e.count(2, 2))
                    n = CAP - 2 * SL
                    eng.tensor_tensor(yw[:, e.par, 0:2, :], p_dn[0:SL, 0:2 * D].rearrange("p (t d) -> p t d", t=2),
                                      gcol[:, e.par, 0:2].unsqueeze(2).to_broadcast([SL, 2, D]), ALU.mult
                                      ).then_inc(S["yw_done"], 1)
                    eng.tensor_scalar(yw[0:n, e.par, 2, :], p_dn[0:n, 2 * D:3 * D], gcol[0:n, e.par, 2:3], None, ALU.mult
                                      ).then_inc(S["yw_done"], 1)
            run2(eng, part2)


N_WEIGHTS = 23
BITS = 30
N_CONSTS = 42

_INS = ['x', 'L0_tok_kernel', 'L0_tok_bias', 'L0_attn_Wqkv', 'L0_attn_bqkv', 'L0_attn_Wout', 'L0_attn_bout',
        'L0_attn_ln_gamma', 'L0_attn_ln_beta', 'L0_attn_decay_logits', 'L0_ffn_W_router', 'L0_ffn_b_router',
        'L0_ffn_W_up', 'L0_ffn_b_up', 'L0_ffn_W_down', 'L0_ffn_b_down']
_OUTS = [((16, 742, 128), 'float32')]


def kernel(**inputs):
    import numpy as _np
    import concourse.bacc as _bacc
    from concourse import mybir as _mybir
    from concourse.bass_utils import run_bass_kernel_spmd as _run

    nc = _bacc.Bacc("TRN2", target_bir_lowering=False, num_devices=1)
    arrays, args = {}, []
    for name in _INS:
        a = _np.ascontiguousarray(inputs[name])
        arrays[f"in_{name}_dram"] = a
        args.append(nc.dram_tensor(f"in_{name}_dram", a.shape, _mybir.dt.from_np(a.dtype), kind="ExternalInput").ap())
    for i, (shape, dtype) in enumerate(_OUTS):
        dt = _mybir.dt.from_np(_np.dtype(dtype))
        args.append(nc.dram_tensor(f"out_{i}_dram", shape, dt, kind="ExternalOutput").ap())
    audio_tower_kernel(nc, *args)
    r = _run(nc, [arrays], core_ids=[0])
    return r.results[0]["out_0_dram"]
```

```python
import concourse.bass as bass
from concourse import mybir
from contextlib import ExitStack


def audio_tower_kernel(nc, x, tok_w, tok_b, w_qkv, b_qkv, w_out, b_out, ln_g, ln_b, decay,
                       w_router, b_router, w_up, b_up, w_down, b_down, out):
    f32, bf16, f16 = mybir.dt.float32, mybir.dt.bfloat16, mybir.dt.float16
    i32, u16 = mybir.dt.int32, mybir.dt.uint16
    ALU, ACT, AX = mybir.AluOpType, mybir.ActivationFunctionType, mybir.AxisListType

    NB, L, CIN = x.shape
    TAPS, _, D = tok_w.shape
    LO = L - TAPS + 1
    C = 106
    NC = LO // C
    XC = (L - 1) // NC
    H = decay.shape[0]
    E = D // H
    E1 = E + 1
    N = NB * LO
    NJ = NB * NC
    NE = w_router.shape[1]
    NG = w_up.shape[0]
    GS = NE // NG
    F = w_up.shape[2]
    CAP = N // NE
    FC = 114
    SL = 124
    ROW = D + NE
    SEG = 128 // NE
    JS = NJ // SEG
    HALF = [(0, 4), (4, NC)]
    QH = LO // 2
    LAM = 1.0 / (1.0 + 1e-07)
    EPS_W, EPS_LN, EPS_DEN = 1e-07, 1e-05, 1e-05
    assert NC * C == LO and XC * NC == L - 1 and CAP * NE == N and 3 * FC == F + 1

    ctx = ExitStack()
    with ctx:
        def sb(name, shape, dt=f32):
            return ctx.enter_context(nc.sbuf_tensor(name, shape, dt))

        def pb(name):
            return ctx.enter_context(nc.psum_tensor(name, [128, 512], f32))

        def sem(name):
            return ctx.enter_context(nc.semaphore(name))

        rows = nc.dram_tensor("token_rows", (N, ROW), f32, kind="Internal").ap()

        ident = sb("ident", [128, 128])
        ones = sb("ones", [128, 1])
        wc = sb("wc", [128, (TAPS + 1) // 2, D])
        wqkv = sb("wqkv", [128, 3 * D])
        wo = sb("wo", [128, D])
        wr = sb("wr", [128, NE])
        bqk = sb("bqk", [128, 2])
        rowb = sb("rowb", [128, 5, D])
        brow = sb("brow", [128, NE])
        lam_in = sb("lam_in", [128, 1])
        lam_row_in = sb("lam_row_in", [128, H])
        lam = sb("lam", [128, 1])
        lam_row = sb("lam_row", [128, H])
        lamc = sb("lamc", [128, 1])
        steps = sb("steps", [128, C])
        steps_neg = sb("steps_neg", [128, C])
        step_cols = sb("step_cols", [128, H])
        cexp = sb("cexp", [128, 1])
        dq = sb("dq", [128, C])
        dk = sb("dk", [128, C])
        dks8 = sb("dks8", [128, H])
        head4 = sb("head4", [128, 4])
        blk = sb("blk", [128, H * E1])
        causal = sb("causal", [128, C])
        expo = sb("expo", [128, 3, NC])

        xw = sb("xw", [XC, 2, NC, 2 * CIN])
        xT = sb("xT", [128, L - 1])
        sq = sb("sq", [128, L - 1])
        sq2 = sb("sq2", [128, L - 1])
        sq4 = sb("sq4", [128, LO])
        wnorm = sb("wnorm", [C, 4, NC])
        y = sb("y", [C, NC, D])
        hres = sb("hres", [C, 2, NC, D])
        st1 = sb("st1", [C, NC, 6])
        mv1 = sb("mv1", [C, NC])
        tmp1 = sb("tmp1", [C, 3, NC])
        ve1 = sb("ve1", [C, NC])
        rs1 = sb("rs1", [C, NC])
        hn = sb("hn", [C, NC, D])
        hnT = sb("hnT", [128, LO])
        tqk = sb("tqk", [128, 2, LO])
        eqk = sb("eqk", [128, 2, LO])
        fqk = sb("fqk", [128, 2, LO])
        qd = sb("qd", [128, 2, LO])
        qb = sb("qb", [128, 2, 4, LO])
        kd = sb("kd", [128, 2, LO])
        kt = sb("kt", [C, 2, NC, D])
        v1 = sb("v1", [C, 2, NC, H, E1])
        P = sb("P", [C, 2, H, C])
        state = sb("state", [128, 3, H * E1])
        state_in = sb("state_in", [128, H * E1])
        den = sb("den", [C, 2, H])
        o = sb("o", [C, 2, NC, D])
        oT = sb("oT", [128, LO])
        z = sb("z", [C, NC, D])
        st2 = sb("st2", [C, NC, 6])
        mv2 = sb("mv2", [C, NC])
        tmp2 = sb("tmp2", [C, 3, NC])
        ve2 = sb("ve2", [C, NC])
        rs2 = sb("rs2", [C, NC])
        hb = sb("hb", [C, NC, D])
        h2 = sb("h2", [C, 2, NC, D])
        st3 = sb("st3", [C, NC, 6])
        mv3 = sb("mv3", [C, NC])
        tmp3 = sb("tmp3", [C, 3, NC])
        ve3 = sb("ve3", [C, NC])
        rs3 = sb("rs3", [C, NC])
        row = sb("row", [C, 2, NC, ROW])
        h2T = sb("h2T", [128, LO])
        lg = sb("lg", [C, NC, NE])
        lmax = sb("lmax", [C, NC])
        lsum = sb("lsum", [C, 2, NC])
        probs = sb("probs", [C, NJ, NE])

        seg_probs = qb[:, 0, :, :].rearrange("p a b -> p (a b)")
        seg_hits = qb[:, 1, 0:2, :].rearrange("p a b -> p (a b)").bitcast(bf16)
        halves = seg_probs.bitcast(u16).rearrange("p (n two) -> p n two", two=2)
        high = qb[:, 1, 2:4, :].rearrange("p a b -> p (a b)").bitcast(u16)
        low = kd[:, :, :].rearrange("p a b -> p (a b)").bitcast(u16)
        low_tied = fqk[:, :, :].rearrange("p a b -> p (a b)").bitcast(u16)
        same_expert = sb("same_expert", [128, 128])
        bit = sb("bit", [128, 2])
        cand = sb("cand", [128, 1])
        hits = sb("hits", [128, 1])
        target = sb("target", [128, 2])
        step_to = sb("step_to", [128, 1])
        thr_high = sb("thr_high", [128, 2])
        thr_bits = sb("thr_bits", [128, 2], i32)
        thr_wide = sb("thr_wide", [NE, C])
        thr = sb("thr", [C, NE])
        onesb = sb("onesb", [128, 128], bf16)
        chunkb = sb("chunkb", [128, 1], bf16)
        above = sb("above", [C, C], bf16)
        upto = sb("upto", [C, C], bf16)
        before = sb("before", [NJ, NJ], bf16)
        slots_h = sb("slots_h", [NJ, CAP + 1], f16)
        slots_f = sb("slots_f", [C, CAP + 1])
        mask = sb("mask", [C, 1 + 2 * NJ], bf16)
        cnt = sb("cnt", [NJ, 2], bf16)
        cex = sb("cex", [NJ, 2])
        reach = sb("reach", [NJ, 2, CAP + 1], bf16)
        dcum = sb("dcum", [NJ, 2, C], bf16)
        inside = sb("inside", [C, CAP + 1], bf16)
        wrap = sb("wrap", [SL, 3])
        idx = sb("idx", [SL, 4, 3], i32)
        xg = qd[0:SL, :, 0:3 * ROW].rearrange("p a (t d) -> p a t d", t=3)
        gcol = sb("gcol", [SL, 2, 3])
        xgT = eqk[:, 0, 0:CAP]
        wup = sb("wup", [128, 4, F])
        wdn = sb("wdn", [FC, 4, 3, D])
        bup = sb("bup", [FC, NG, 3])
        act = sb("act", [FC, 2, 3, CAP])
        yw = tqk[0:SL, :, 0:3 * D].rearrange("p a (t d) -> p a t d", t=3)

        pa = [pb("pa0"), pb("pa1")]
        ps = [pb("ps0"), pb("ps1")]
        po = pb("po")
        pst = pb("pst")
        pc = [pb("pc0"), pb("pc1")]

        p_xg, p_up, p_dn, p_small, p_dcum, p_cum = pa[0], [pa[1], ps[0], ps[1]], po, pst, pc[0], pc[1]

        names = """weights_in consts_pool consts_dve lam_exp lam_done decays_done
            xt_ps xt_sb sq_done win_done wsum_ps wsum_sb wnorm_done scale_step conv_ps tanh_done ybias_done h_done
            stats1  ve1_done rs1_done hn_done hnt_ps hnt_sb qk_ps t_sb e_sb emin_done f_done qd_done qb_done
            kd_done v_ps v_sb kt_ps kt_sb s_ps p0_done p1_raw p1_done o_ps st_ps stm_done state_done den_step o_done
            ot_ps ot_sb wo_ps z_done stats2  ve2_done rs2_done zn_done zg_done hb_done h2_done
            stats3  ve3_done rs3_done hn2_done h2t_ps h2t_sb r_ps lg_done lmax_done lsub_done lexp_done
            lsum_done lrec_done probs_done probs_row
            held_sync held_pool held_act bup_in
            seg_ps seg_act seg_dve keys_done low_done bit_step hits_done hits_ps thr_step thr_ps thr_done
            mask_done cnt_ps cnt_sb cex_ps cex_sb dcum_ps dcum_sb reach_done cum_ps inside_done idx_ps wrap_done idx_done
            xgt_ps gcol_done xgt_sb up_ps act_done dn_ps yw_done eps1_done eps2_done eps3_done""".split()
        S = {n: sem(n) for n in names}
        x_in = [sem("x_in0"), sem("x_in1")]
        w_in = [sem(f"w_in{k}") for k in range(4)]
        x_got = [sem("x_got0"), sem("x_got1")]
        y_out = sem("y_out")
        h2_out = [sem("h2_out0"), sem("h2_out1")]
        row_out = [sem("row_out0"), sem("row_out1")]

        class Batch:
            def __init__(self, m, par):
                self.m, self.par = m, par

            def count(self, per, k, back=0):
                return self.m * (2 * per) + (per * (self.par - back) + k)

            def index(self):
                return self.m * 2 + self.par

        def BEFORE(b):
            return Batch(b.m, 0) if b.par else Batch(b.m - 1, 1)

        def AFTER(b):
            return Batch(b.m + 1, 0) if b.par else Batch(b.m, 1)

        def need(eng, s, value):
            if isinstance(value, int) and value <= 0:
                return
            eng.wait_ge(S[s] if isinstance(s, str) else s, value)

        def chunks(half):
            return range(*HALF[half])

        def hold(eng, s, value):
            if isinstance(value, int) and value <= 0:
                return
            eng.wait_ge(S[s] if isinstance(s, str) else s, value)
            eng.sem_inc(S["held_sync" if eng is nc.sync else "held_pool" if eng is nc.gpsimd else "held_act"])

        ORDER = [("C", "o"), ("A", "x"), ("C", "w"), ("S", 0), ("C", "z0"), ("S", 1), ("A", "win"), ("V", 0),
                 ("C", "z1"), ("A", "conv0"), ("A", "w"), ("S", 2), ("A", "scale"), ("V", 1), ("C", "zn"),
                 ("A", "conv1"), ("S", 3), ("V", 2), ("A", "h0"), ("A", "st0"), ("A", "h1"), ("S", 4), ("V", 3),
                 ("C", "zg"), ("C", "h2"), ("A", "st1"), ("S", 5), ("V", 4), ("A", "hn"), ("C", "st0"),
                 ("C", "st1"), ("S", 6), ("A", "hnT"), ("V", 5), ("A", "q"), ("C", "hn"), ("A", "qd"),
                 ("A", "k"), ("V", 6), ("A", "v"), ("C", "t"), ("C", "r"), ("A", "kd"), ("A", "qb"),
                 ("C", "max"), ("A", "kt"), ("C", "soft")]
        PEEL_IN, TAIL = 4, 2
        QK = {("A", "q"): (0, 1), ("A", "k"): (2, 3)}
        WSUM_AT = [w for s, w in ORDER[ORDER.index(("A", "w")):] if s == "S"][0]

        def run(eng, part):
            def iteration(M, p, a, b, c):
                before = Batch(M, 0) if p else Batch(M - 1, 1)
                batch = {"A": Batch(M, p), "S": before, "V": before, "C": Batch(M - 1, p)}
                for stage, what in ORDER:
                    if {"A": a, "S": b, "V": b, "C": c}[stage]:
                        part(stage, what, batch[stage])
            for i in range(PEEL_IN):
                iteration(i // 2, i % 2, True, i >= 1, i >= 2)
            with eng.Fori(PEEL_IN // 2, NB // 2) as M:
                for p in range(2):
                    iteration(M, p, True, True, True)
            for i in range(NB, NB + TAIL):
                iteration(i // 2, i % 2, False, i < NB + 1, True)

        SEG_BANKS = [pa[0], pa[1], ps[0], ps[1], pc[0], pc[1], po]

        class Expert:
            def __init__(self, m, k):
                self.m, self.k = m + k // 4, k % 4
                self.par = k % 2

            def count(self, per, k, back=0):
                return self.m * (4 * per) + (per * (self.k - back) + k)

            def half(self, back=0):
                return self.m * 2 + (self.k // 2 + 1 - back)

            def index(self):
                return self.m * 4 + self.k

        ORDER2 = [("I", "mask"), ("F", "x"), ("D", "down0"), ("I", "cnt"), ("F", "up0"), ("F", "up1"), ("I", "reach"),
                  ("D", "down1"), ("I", "cum"), ("D", "down2"), ("D", "out"), ("I", "idx"), ("F", "up2")]
        UP, DOWN = ("up0", "up1", "up2"), ("down0", "down1", "down2")
        BEHIND = {"I": 0, "F": 2, "D": 3}

        def run2(eng, part):
            def iteration(M, p, on):
                for stage, what in ORDER2:
                    k = p - BEHIND[stage]
                    if on[stage]:
                        part(stage, what, Expert(M, k) if k >= 0 else Expert(M - 1, k + 4))
            for i in range(4):
                iteration(0, i, {stage: i >= back for stage, back in BEHIND.items()})
            with eng.Fori(1, NE // 4) as M:
                for p in range(4):
                    iteration(M, p, {stage: True for stage in BEHIND})
            for i in range(max(BEHIND.values())):
                iteration(NE // 4, i, {stage: i < back for stage, back in BEHIND.items()})

        block = ctx.enter_context(nc.Block())

        @block.sync
        def _(eng):
            w2 = tok_w[0:TAPS - 1, :, :].rearrange("(k t) c f -> t c k f", t=2)
            n = 0
            for dst, src in [
                (wc[0:CIN, 0:4, :], w2[0]), (wc[CIN:128, 0:4, :], w2[1]), (wc[CIN:128, 4, :], tok_w[TAPS - 1]),
                (wqkv[:, :], w_qkv), (wo[:, :], w_out), (wr[:, :], w_router),
                (bqk[:, 0:1], b_qkv[0:D].unsqueeze(1)), (bqk[:, 1:2], b_qkv[D:2 * D].unsqueeze(1)),
                (rowb[:, 0, :], tok_b.partition_broadcast(128)), (rowb[:, 1, :], b_qkv[2 * D:].partition_broadcast(128)),
                (rowb[:, 2, :], b_out.partition_broadcast(128)), (rowb[:, 3, :], ln_g.partition_broadcast(128)),
                (rowb[:, 4, :], ln_b.partition_broadcast(128)), (brow[:, :], b_router.partition_broadcast(128)),
                (lam_row_in[:, :], decay.partition_broadcast(128)),
            ] + [(lam_in[E * h:E * h + E, :], decay[h:h + 1].partition_broadcast(E)) for h in range(H)]:
                eng.dma_start(dst, src).then_inc(S["weights_in"], 16)
                n += 1
            assert n == N_WEIGHTS

            def store_rows(b):
                hold(eng, "hn2_done", b.count(2, 2))
                hold(eng, "probs_row", b.count(1, 1))
                eng.dma_start(rows[bass.ds(b.index() * LO, LO), :].rearrange("(c p) d -> p c d", p=C),
                              row[:, b.par, :, :]).then_inc(row_out[b.par], 16)

            def part(stage, what, b):
                if (stage, what) == ("A", "x"):
                    hold(eng, "xt_ps", b.count(2, 2, back=2))
                    for t in range(2):
                        eng.dma_start(xw[:, b.par, :, t * CIN:(t + 1) * CIN],
                                      x[b.index(), t:t + L - 1, :].rearrange("(c p) d -> p c d", p=XC)
                                      ).then_inc(x_in[b.par], 16)
                if (stage, what) == ("C", "hn"):
                    hold(eng, "h2_done", b.count(2, 2))
                    eng.dma_start(out[b.index(), :, :].rearrange("(c p) d -> p c d", p=C),
                                  h2[:, b.par, :, :]).then_inc(h2_out[b.par], 16)
                if (stage, what) == ("C", "w") and not (isinstance(b.m, int) and b.index() == 0):
                    store_rows(BEFORE(b))
            run(eng, part)
            store_rows(Batch(NB // 2 - 1, 1))
            for g in range(NG):
                for k in range(3):
                    n = FC if k < 2 else FC - 1
                    eng.dma_start(bup[0:n, g, k:k + 1], b_up[g, k * FC:k * FC + n].unsqueeze(1)).then_inc(S["bup_in"], 16)

            def part2(stage, what, e):
                if (stage, what) == ("I", "mask"):
                    hold(eng, "up_ps", e.count(3, 3, back=4))
                    hold(eng, "dn_ps", e.count(1, 1, back=4))
                    w = wdn[:, e.k, :, :]
                    n = e.index()
                    eng.dma_start(wup[:, e.k, :], w_up[e.m, :, :]).then_inc(w_in[e.k], 16)
                    eng.dma_start(w[:, 0:2, :], w_down[n, 0:2 * FC, :].rearrange("(k p) d -> p k d", p=FC)
                                  ).then_inc(w_in[e.k], 16)
                    eng.dma_start(w[0:FC - 1, 2, :], w_down[n, 2 * FC:F, :]).then_inc(w_in[e.k], 16)
                    eng.dma_start(w[FC - 1:FC, 2, :], b_down[bass.ds(n, 1), :]).then_inc(w_in[e.k], 16)
            run2(eng, part2)
            eng.wait_ge(y_out, 16 * 3 * NE)

        @block.gpsimd
        def _(eng):
            made = [0]

            def step(ins):
                made[0] += 1
                ins.then_inc(S["consts_pool"], 1)
                eng.wait_ge(S["consts_pool"], made[0])

            eng.memset(ones[:, :], 1.0).then_inc(S["consts_pool"], 1)
            eng.memset(v1[:, :, :, :, :], 1.0).then_inc(S["consts_pool"], 1)
            eng.memset(expo[:, 0, :], -0.5).then_inc(S["consts_pool"], 1)
            eng.memset(expo[:, 1, :], 0.5).then_inc(S["consts_pool"], 1)
            eng.memset(cexp[:, :], float(C)).then_inc(S["consts_pool"], 1)
            eng.memset(expo[:, 2, :], EPS_LN).then_inc(S["consts_pool"], 1)
            made[0] = 6
            eng.memset(ident[:, :], 0.0).then_inc(S["consts_pool"], 1)
            eng.memset(causal[:, :], 1.0).then_inc(S["consts_pool"], 1)
            eng.memset(head4[:, :], 1.0).then_inc(S["consts_pool"], 1)
            made[0] = 9
            step(eng.memset(blk[:, :], 1.0))
            step(eng.affine_select(out=ident[:, :], in_=ident[:, :], compare_op=ALU.not_equal, fill=1.0, base=0,
                                   pattern=[[-1, 128]], channel_multiplier=1))
            step(eng.affine_select(out=causal[:, :], in_=causal[:, :], compare_op=ALU.is_ge, fill=0.0, base=0,
                                   pattern=[[1, C]], channel_multiplier=-1))
            for g in range(2):
                w = head4[64 * g:64 * g + 64, :]
                step(eng.affine_select(out=w, in_=w, compare_op=ALU.is_ge, fill=0.0, base=0,
                                       pattern=[[-E, 4]], channel_multiplier=1))
                step(eng.affine_select(out=w, in_=w, compare_op=ALU.is_ge, fill=0.0, base=E - 1,
                                       pattern=[[E, 4]], channel_multiplier=-1))
            b3 = blk[:, :].rearrange("p (h e) -> p h e", h=H)
            step(eng.affine_select(out=b3, in_=b3, compare_op=ALU.is_ge, fill=0.0, base=0,
                                   pattern=[[-E, H], [0, E1]], channel_multiplier=1))
            step(eng.affine_select(out=b3, in_=b3, compare_op=ALU.is_ge, fill=0.0, base=E - 1,
                                   pattern=[[E, H], [0, E1]], channel_multiplier=-1))
            eng.iota(steps[:, :], pattern=[[1, C]], base=0, channel_multiplier=0,
                     allow_small_or_imprecise_dtypes=True).then_inc(S["consts_pool"], 1)
            eng.iota(steps_neg[:, :], pattern=[[-1, C]], base=0, channel_multiplier=0,
                     allow_small_or_imprecise_dtypes=True).then_inc(S["consts_pool"], 1)
            made[0] += 2
            step(eng.iota(step_cols[:, :], pattern=[[0, H]], base=C, channel_multiplier=-1,
                          allow_small_or_imprecise_dtypes=True))
            step(eng.memset(same_expert[:, :], 0.0))
            for k in range(-3, 4):
                step(eng.affine_select(out=same_expert[:, :], in_=same_expert[:, :], compare_op=ALU.not_equal, fill=1.0,
                                       base=NE * k, pattern=[[-1, 128]], channel_multiplier=1))
            eng.memset(onesb[:, :], 1.0).then_inc(S["consts_pool"], 1)
            eng.memset(chunkb[:, :], float(C)).then_inc(S["consts_pool"], 1)
            eng.memset(mask[:, :], 0.0).then_inc(S["consts_pool"], 1)
            eng.memset(act[:, :, :, :], 1.0).then_inc(S["consts_pool"], 1)
            eng.memset(target[:, :], float(CAP)).then_inc(S["consts_pool"], 1)
            made[0] += 5
            for m in (above, upto, before):
                step(eng.memset(m[:, :], 1.0))
            step(eng.affine_select(out=above[:, :], in_=above[:, :], compare_op=ALU.is_gt, fill=0.0, base=0,
                                   pattern=[[-1, C]], channel_multiplier=1))
            step(eng.affine_select(out=upto[:, :], in_=upto[:, :], compare_op=ALU.is_ge, fill=0.0, base=0,
                                   pattern=[[1, C]], channel_multiplier=-1))
            step(eng.affine_select(out=before[:, :], in_=before[:, :], compare_op=ALU.is_gt, fill=0.0, base=0,
                                   pattern=[[1, NJ]], channel_multiplier=-1))
            step(eng.iota(slots_h[:, :], pattern=[[1, CAP + 1]], base=0, channel_multiplier=0,
                          allow_small_or_imprecise_dtypes=True))
            step(eng.iota(slots_f[:, :], pattern=[[1, CAP + 1]], base=0, channel_multiplier=0,
                          allow_small_or_imprecise_dtypes=True))
            assert made[0] == N_CONSTS
            eng.wait_ge(S["lam_done"], 4)
            lb = lam[:, :].to_broadcast([128, C])
            eng.tensor_tensor(dq[:, :], lb, steps[:, :], ALU.pow).then_inc(S["decays_done"], 1)
            eng.tensor_tensor(dk[:, :], lb, steps_neg[:, :], ALU.pow).then_inc(S["decays_done"], 1)
            eng.tensor_tensor(dks8[:, :], lam_row[:, :], step_cols[:, :], ALU.pow).then_inc(S["decays_done"], 1)
            eng.tensor_tensor(lamc[:, :], lam[:, :], cexp[:, :], ALU.pow).then_inc(S["decays_done"], 1)
            eng.wait_ge(S["decays_done"], 4)
            eng.tensor_scalar(dq[:, :], dq[:, :], float(E) ** -0.5, None, ALU.mult).then_inc(S["decays_done"], 1)
            eng.wait_ge(S["decays_done"], 5)

            def part(stage, what, b):
                if (stage, what) == ("A", "w"):
                    need(eng, "wsum_sb", b.count(1, 1))
                    eng.tensor_tensor(wnorm[:, 1, :], wnorm[:, 0, :], expo[0:C, 1, :], ALU.pow).then_inc(S["wnorm_done"], 1)
                if (stage, what) == ("A", "st1"):
                    need(eng, "ve1_done", b.count(1, 1))
                    need(eng, "hn_done", b.count(2, 2, back=1))
                    eng.tensor_tensor(ve1[:, :], ve1[:, :], expo[0:C, 2, :], ALU.add).then_inc(S["eps1_done"], 1)
                    need(eng, "eps1_done", b.count(1, 1))
                    eng.tensor_tensor(rs1[:, :], ve1[:, :], expo[0:C, 0, :], ALU.pow).then_inc(S["rs1_done"], 1)
                if stage == "S":
                    c = what
                    hold(eng, "p1_raw", b.count(7, c + 1))
                    w = P[:, c % 2, 4:8, :]
                    eng.affine_select(out=w, in_=w, compare_op=ALU.is_ge, fill=0.0, base=0,
                                      pattern=[[0, 4], [1, C]], channel_multiplier=-1).then_inc(S["p1_done"], 1)
                if (stage, what) == ("C", "o"):
                    need(eng, "h2_done", b.count(2, 2, back=1))
                    eng.tensor_tensor(hb[:, :, :], hres[:, b.par, :, :],
                                      rowb[0:C, 4:5, :].to_broadcast([C, NC, D]), ALU.add).then_inc(S["hb_done"], 1)
                if (stage, what) == ("C", "z1"):
                    need(eng, "ve2_done", b.count(1, 1))
                    need(eng, "zn_done", b.count(2, 2, back=1))
                    eng.tensor_tensor(ve2[:, :], ve2[:, :], expo[0:C, 2, :], ALU.add).then_inc(S["eps2_done"], 1)
                    need(eng, "eps2_done", b.count(1, 1))
                    eng.tensor_tensor(rs2[:, :], ve2[:, :], expo[0:C, 0, :], ALU.pow).then_inc(S["rs2_done"], 1)
                if (stage, what) == ("C", "st1"):
                    need(eng, "ve3_done", b.count(1, 1))
                    need(eng, "hn2_done", b.count(2, 2, back=1))
                    eng.tensor_tensor(ve3[:, :], ve3[:, :], expo[0:C, 2, :], ALU.add).then_inc(S["eps3_done"], 1)
                    need(eng, "eps3_done", b.count(1, 1))
                    eng.tensor_tensor(rs3[:, :], ve3[:, :], expo[0:C, 0, :], ALU.pow).then_inc(S["rs3_done"], 1)
            eng.wait_ge(S["weights_in"], 16 * N_WEIGHTS)
            run(eng, part)
            for p in range(2):
                eng.wait_ge(h2_out[p], 16 * NB // 2)
                eng.wait_ge(row_out[p], 16 * NB // 2)
            out_rows = out.rearrange("b t d -> (b t) d")

            def rows_of(t):
                return SL if t < 2 else CAP - 2 * SL

            def part2(stage, what, e):
                if (stage, what) == ("I", "idx"):
                    hold(eng, "idx_done", e.count(1, 1))
                    hold(eng, "xgt_ps", e.count(1, 1, back=2))
                    hold(eng, "gcol_done", e.count(2, 2, back=2))
                    for t in range(3):
                        n = rows_of(t)
                        eng.indirect_dma_start(
                            out=xg[0:n, e.par, t, :], out_offset=None, in_=rows[:, :],
                            in_offset=bass.IndirectOffsetOnAxis(ap=idx[0:n, e.k, t:t + 1], axis=0)
                        ).then_inc(x_got[e.par], 16)
                if (stage, what) == ("D", "out"):
                    hold(eng, "yw_done", e.count(2, 2))
                    hold(eng, y_out, e.count(48, 0))
                    for t in range(3):
                        n = rows_of(t)
                        eng.indirect_dma_start(
                            out=out_rows, out_offset=bass.IndirectOffsetOnAxis(ap=idx[0:n, e.k, t:t + 1], axis=0),
                            in_=yw[0:n, e.par, t, :], in_offset=None, compute_op=ALU.add).then_inc(y_out, 16)
            run2(eng, part2)

        @block.scalar
        def _(eng):
            eng.wait_ge(S["weights_in"], 16 * N_WEIGHTS)
            eng.wait_ge(S["consts_pool"], N_CONSTS)
            eng.activation(lam[:, :], lam_in[:, :], ACT.Exp, scale=-1.0).then_inc(S["lam_exp"], 1)
            eng.activation(lam_row[:, :], lam_row_in[:, :], ACT.Exp, scale=-1.0).then_inc(S["lam_exp"], 1)

            def part(stage, what, b):
                if (stage, what) == ("A", "x"):
                    for half in range(2):
                        lo, hi = HALF[half]
                        need(eng, "xt_ps", b.count(2, half + 1))
                        need(eng, "sq_done", b.count(1, 1, back=1))
                        need(eng, "conv_ps", b.count(2, 2, back=1))
                        eng.activation(xT[:, lo * XC:hi * XC], pa[half][:, 0:(hi - lo) * XC],
                                       ACT.Copy).then_inc(S["xt_sb"], 1)
                    need(eng, "xt_sb", b.count(2, 2))
                    need(eng, "win_done", b.count(3, 3, back=1))
                    eng.activation(sq[:, :], xT[:, :], ACT.Square).then_inc(S["sq_done"], 1)
                if (stage, what) in (("A", "h0"), ("A", "h1")):
                    need(eng, "scale_step", b.count(3, 3))
                    for half in [int(what[1])]:
                        need(eng, "conv_ps", b.count(2, half + 1))
                        need(eng, "h_done", b.count(2, half + 1, back=1))
                        for c in chunks(half):
                            k = c - HALF[half][0]
                            eng.activation(y[:, c, :], pa[half][0:C, k * D:(k + 1) * D], ACT.Tanh,
                                           scale=wnorm[:, 3, c:c + 1]).then_inc(S["tanh_done"], 1)
                if (stage, what) == ("A", "hnT"):
                    for half in range(2):
                        lo, hi = HALF[half]
                        need(eng, "hnt_ps", b.count(2, half + 1))
                        need(eng, "v_ps", b.count(2, 2, back=1))
                        eng.activation(hnT[:, lo * C:hi * C], pa[half][:, 0:(hi - lo) * C],
                                       ACT.Copy).then_inc(S["hnt_sb"], 1)
                if (stage, what) in QK:
                    for n in QK[stage, what]:
                        w, half = n // 2, n % 2
                        need(eng, "qk_ps", b.count(4, n + 1))
                        need(eng, "f_done", b.count(4, n + 1, back=1))
                        cols = slice(half * QH, half * QH + QH)
                        eng.activation(tqk[:, w, cols], pa[half][:, 0:QH], ACT.Identity,
                                       bias=bqk[:, w:w + 1]).then_inc(S["t_sb"], 1)
                        need(eng, "t_sb", b.count(4, n + 1))
                        eng.activation(eqk[:, w, cols], tqk[:, w, cols], ACT.Exp).then_inc(S["e_sb"], 1)
                if (stage, what) == ("A", "qb"):
                    need(eng, "qd_done", b.count(1, 1))
                    need(eng, "s_ps", b.count(14, 14, back=2))
                    for j in range(4):
                        eng.activation(qb[:, b.par, j, :], qd[:, b.par, :], ACT.Copy, scale=head4[:, j:j + 1]
                                       ).then_inc(S["qb_done"], 1)
                if stage == "S":
                    c = what
                    need(eng, "s_ps", b.count(14, 2 * c + 2))
                    need(eng, "o_ps", b.count(7, c - 1))
                    eng.activation(P[:, c % 2, 4:8, :], ps[1][0:C, 0:4 * C].rearrange("p (h t) -> p h t", h=4),
                                   ACT.Copy).then_inc(S["p1_raw"], 1)
                if (stage, what) == ("C", "o"):
                    for half in range(2):
                        lo, hi = HALF[half]
                        need(eng, "ot_ps", b.count(2, half + 1))
                        need(eng, "wo_ps", b.count(2, 2, back=1))
                        eng.activation(oT[:, lo * C:hi * C], pc[half][:, 0:(hi - lo) * C],
                                       ACT.Copy).then_inc(S["ot_sb"], 1)
                if (stage, what) == ("C", "t"):
                    for half in range(2):
                        lo, hi = HALF[half]
                        need(eng, "h2t_ps", b.count(2, half + 1))
                        need(eng, "r_ps", b.count(2, 2, back=1))
                        eng.activation(h2T[:, lo * C:hi * C], pc[half][:, 0:(hi - lo) * C],
                                       ACT.Copy).then_inc(S["h2t_sb"], 1)
                if (stage, what) == ("C", "soft"):
                    need(eng, "lsub_done", b.count(1, 1))
                    eng.activation(lg[:, :, :], lg[:, :, :], ACT.Exp).then_inc(S["lexp_done"], 1)
            run(eng, part)
            for n in range(1, JS // 4, 2):
                eng.wait_ge(S["seg_ps"], n + 1)
                eng.activation(seg_probs[:, n * 4 * C:(n + 1) * 4 * C], SEG_BANKS[n][:, 0:4 * C],
                               ACT.Copy).then_inc(S["seg_act"], 1)
            eng.wait_ge(S["seg_dve"], (JS // 4 + 1) // 2)
            eng.wait_ge(S["seg_act"], JS // 8)
            eng.activation(low, halves[:, :, 0], ACT.Copy).then_inc(S["low_done"], 1)
            eng.wait_ge(S["bup_in"], 16 * 3 * NG)

            def part2(stage, what, e):
                if (stage, what) == ("F", "x"):
                    need(eng, "xgt_ps", e.count(1, 1))
                    need(eng, "up_ps", e.count(3, 3, back=1))
                    eng.activation(xgT, p_xg[:, 0:CAP], ACT.Copy).then_inc(S["xgt_sb"], 1)
                if stage == "F" and what in UP:
                    need(eng, "dn_ps", e.count(1, 1, back=2))
                    for k in [UP.index(what)]:
                        n = FC if k < 2 else FC - 1
                        hold(eng, "up_ps", e.count(3, k + 1))
                        eng.activation(act[0:n, e.par, k, :], p_up[k][0:n, 0:CAP], ACT.Silu,
                                       bias=bup[0:n, e.m, k:k + 1]).then_inc(S["act_done"], 1)
                if (stage, what) == ("I", "reach"):
                    need(eng, "dcum_ps", e.count(1, 1))
                    need(eng, "cum_ps", e.count(1, 1, back=1))
                    eng.activation(dcum[:, :, :], p_dcum[0:NJ, 0:2 * C].rearrange("p (h t) -> p h t", h=2),
                                   ACT.Copy).then_inc(S["dcum_sb"], 1)
            run2(eng, part2)

        @block.tensor
        def _(eng):
            eng.wait_ge(S["weights_in"], 16 * N_WEIGHTS)
            eng.wait_ge(S["consts_pool"], N_CONSTS)

            def part(stage, what, b):
                if (stage, what) == ("A", "x"):
                    need(eng, x_in[b.par], b.m * 32 + 32)
                    for half in range(2):
                        need(eng, "kt_sb", b.count(2, half + 1, back=1))
                        for c in chunks(half):
                            k = c - HALF[half][0]
                            mm = eng.transpose(pa[half][:, k * XC:(k + 1) * XC], xw[:, b.par, c, :], ident[0:XC, 0:XC])
                        mm.then_inc(S["xt_ps"], 1)
                if (stage, what) == ("A", "w"):
                    need(eng, "win_done", b.count(3, 3))
                    need(eng, "stm_done", BEFORE(b).count(5, WSUM_AT - 1))
                    for c in range(NC):
                        mm = eng.matmul(pst[0:C, c:c + 1], sq4[:, c * C:(c + 1) * C], ones[:, :], start=True, stop=True)
                    mm.then_inc(S["wsum_ps"], 1)
                if (stage, what) in (("A", "conv0"), ("A", "conv1")):
                    need(eng, "xt_sb", b.count(2, 2))
                    for half in [int(what[4])]:
                        for c in chunks(half):
                            k = c - HALF[half][0]
                            dst = pa[half][0:C, k * D:(k + 1) * D]
                            for t in range(4):
                                a = c * C + 2 * t
                                eng.matmul(dst, xT[:, a:a + C], wc[:, t, :], start=(t == 0), stop=False)
                            a = c * C + TAPS - 2
                            mm = eng.matmul(dst, xT[CIN:128, a:a + C], wc[CIN:128, 4, :], start=False, stop=True)
                        mm.then_inc(S["conv_ps"], 1)
                if (stage, what) == ("A", "hnT"):
                    for half in range(2):
                        need(eng, "hn_done", b.count(2, half + 1))
                        need(eng, "tanh_done", b.count(NC, HALF[half][1]))
                        for c in chunks(half):
                            k = c - HALF[half][0]
                            mm = eng.transpose(pa[half][:, k * C:(k + 1) * C], hn[:, c, :], ident[0:C, 0:C])
                        mm.then_inc(S["hnt_ps"], 1)
                if (stage, what) in QK:
                    for n in QK[stage, what]:
                        w, half = n // 2, n % 2
                        need(eng, "hnt_sb", b.count(2, 2 if half or w else 1))
                        if w:
                            need(eng, "t_sb", b.count(4, half + 1))
                        eng.matmul(pa[half][:, 0:QH], wqkv[:, w * D:(w + 1) * D], hnT[:, half * QH:half * QH + QH],
                                   start=True, stop=True).then_inc(S["qk_ps"], 1)
                if (stage, what) == ("A", "v"):
                    for half in range(2):
                        need(eng, "t_sb", b.count(4, half + 3))
                        for c in chunks(half):
                            k = c - HALF[half][0]
                            mm = eng.matmul(pa[half][0:C, k * D:(k + 1) * D], hnT[:, c * C:(c + 1) * C],
                                            wqkv[:, 2 * D:3 * D], start=True, stop=True)
                        mm.then_inc(S["v_ps"], 1)
                if (stage, what) == ("A", "kt"):
                    need(eng, "f_done", b.count(4, 4))
                    for half in range(2):
                        need(eng, "v_sb", b.count(2, half + 1))
                        for c in chunks(half):
                            k = c - HALF[half][0]
                            mm = eng.transpose(pa[half][0:C, k * D:(k + 1) * D], fqk[:, 1, c * C:(c + 1) * C], ident[:, :])
                        mm.then_inc(S["kt_ps"], 1)
                if stage == "S":
                    c = what
                    tok = slice(c * C, (c + 1) * C)
                    if c == 0:
                        need(eng, "qb_done", b.count(4, 4))
                        need(eng, "kd_done", b.count(1, 1))
                        need(eng, "kt_sb", b.count(2, 2))
                        need(eng, "v_sb", b.count(2, 2))
                    for g in range(2):
                        need(eng, ["p0_done", "p1_raw"][g], b.count(7, c))
                        eng.matmul(ps[g][0:C, 0:4 * C], kd[64 * g:64 * g + 64, b.par, tok],
                                   qb[64 * g:64 * g + 64, b.par, :, tok], start=True, stop=True).then_inc(S["s_ps"], 1)
                    if c < NC - 1:
                        if c == 1:
                            need(eng, "state_done", b.count(6, 1))
                        else:
                            need(eng, "stm_done", b.count(5, c - 1) if c else b.count(5, 5, back=1))
                        if c == WSUM_AT and not (isinstance(b.m, int) and b.index() == NB - 1):
                            need(eng, "wsum_sb", AFTER(b).count(1, 1))
                        eng.matmul(pst[:, 0:H * E1], kt[:, b.par, c, :],
                                   v1[:, b.par, c, :, :].rearrange("p h e -> p (h e)"),
                                   start=True, stop=True).then_inc(S["st_ps"], 1)
                if stage == "V":
                    c = what
                    tok = slice(c * C, (c + 1) * C)
                    need(eng, "o_done", b.count(7, c))
                    if c > 0:
                        need(eng, "state_done", b.count(6, c))
                        eng.matmul(po[0:C, 0:H * E1], qd[:, b.par, tok], state[:, c % 3, :], start=True, stop=False,
                                   skip_group_check=True)
                    for h in range(H):
                        if h % 4 == 0:
                            need(eng, ["p0_done", "p1_done"][h // 4], b.count(7, c + 1))
                        mm = eng.matmul(po[0:C, h * E1:(h + 1) * E1], P[:, c % 2, h, :], v1[:, b.par, c, h, :],
                                        start=(c == 0 and h == 0), stop=(h == H - 1), skip_group_check=True)
                    mm.then_inc(S["o_ps"], 1)
                if (stage, what) == ("C", "o"):
                    for half in range(2):
                        need(eng, "o_done", b.count(7, HALF[half][1]))
                        need(eng, "lg_done", b.count(2, half + 1, back=1))
                        for c in chunks(half):
                            k = c - HALF[half][0]
                            mm = eng.transpose(pc[half][:, k * C:(k + 1) * C], o[:, b.par, c, :], ident[0:C, 0:C])
                        mm.then_inc(S["ot_ps"], 1)
                if (stage, what) == ("C", "w"):
                    for half in range(2):
                        need(eng, "ot_sb", b.count(2, half + 1))
                        for c in chunks(half):
                            k = c - HALF[half][0]
                            mm = eng.matmul(pc[half][0:C, k * D:(k + 1) * D], oT[:, c * C:(c + 1) * C], wo[:, :],
                                            start=True, stop=True)
                        mm.then_inc(S["wo_ps"], 1)
                if (stage, what) == ("C", "t"):
                    for half in range(2):
                        need(eng, "hn2_done", b.count(2, half + 1))
                        need(eng, "z_done", b.count(2, half + 1))
                        for c in chunks(half):
                            k = c - HALF[half][0]
                            mm = eng.transpose(pc[half][:, k * C:(k + 1) * C], row[:, b.par, c, 0:D], ident[0:C, 0:C])
                        mm.then_inc(S["h2t_ps"], 1)
                if (stage, what) == ("C", "r"):
                    for half in range(2):
                        need(eng, "h2t_sb", b.count(2, half + 1))
                        for c in chunks(half):
                            k = c - HALF[half][0]
                            mm = eng.matmul(pc[half][0:C, k * NE:(k + 1) * NE], h2T[:, c * C:(c + 1) * C], wr[:, :],
                                            start=True, stop=True)
                        mm.then_inc(S["r_ps"], 1)
            run(eng, part)
            eng.wait_ge(S["probs_done"], NB)
            for n in range(JS // 4):
                for k in range(4):
                    j = 4 * (4 * n + k)
                    mm = eng.transpose(SEG_BANKS[n][:, k * C:(k + 1) * C],
                                       probs[:, j:j + 4, :].rearrange("p j e -> p (j e)"), ident[0:C, 0:C])
                mm.then_inc(S["seg_ps"], 1)
            def sum_hits(value):
                need(eng, "hits_done", value)
                eng.matmul(pst[:, 0:1], same_expert[:, :], hits[:, :], start=True, stop=True).then_inc(S["hits_ps"], 1)

            with eng.Fori(0, HIGH_BITS // 2) as r:
                for k in range(2):
                    sum_hits(r * 2 + (k + 1))
            sum_hits(HIGH_BITS + 1)
            with eng.Fori(0, LOW_BITS // 2) as r:
                for k in range(2):
                    sum_hits(r * 2 + (HIGH_BITS + 1 + k + 1))
            eng.wait_ge(S["thr_step"], 8)
            eng.transpose(pst[0:C, 0:NE], thr_wide[:, :], ident[0:NE, 0:NE]).then_inc(S["thr_ps"], 1)

            def part2(stage, what, e):
                if (stage, what) == ("F", "x"):
                    need(eng, x_got[e.par], e.half() * 48)
                    need(eng, "xgt_sb", e.count(1, 1, back=1))
                    for t in range(3):
                        n = SL if t < 2 else CAP - 2 * SL
                        mm = eng.transpose(p_xg[:, t * SL:t * SL + n], xg[0:n, e.par, t, 0:D], ident[0:n, 0:n])
                    mm.then_inc(S["xgt_ps"], 1)
                if stage == "F" and what in UP:
                    need(eng, w_in[e.k], e.m * 64 + 64)
                    need(eng, "xgt_sb", e.count(1, 1))
                    for k in [UP.index(what)]:
                        n = FC if k < 2 else FC - 1
                        need(eng, "act_done", e.count(3, k + 1, back=1))
                        eng.matmul(p_up[k][0:n, 0:CAP], wup[:, e.k, k * FC:k * FC + n], xgT,
                                   start=True, stop=True).then_inc(S["up_ps"], 1)
                if stage == "D" and what in DOWN:
                    need(eng, "yw_done", e.count(2, 2, back=1))
                    need(eng, "act_done", e.count(3, 3))
                    for t in [DOWN.index(what)]:
                        n = SL if t < 2 else CAP - 2 * SL
                        for k in range(3):
                            mm = eng.matmul(p_dn[0:n, t * D:(t + 1) * D], act[:, e.par, k, t * SL:t * SL + n],
                                            wdn[:, e.k, k, :], start=(k == 0), stop=(k == 2))
                    if what == DOWN[-1]:
                        mm.then_inc(S["dn_ps"], 1)
                if (stage, what) == ("I", "cnt"):
                    need(eng, "mask_done", e.count(2, 2))
                    need(eng, "idx_done", e.count(1, 1, back=1))
                    for h in range(2):
                        mm = eng.matmul(p_small[0:NJ, h:h + 1], mask[:, 1 + h * NJ:1 + (h + 1) * NJ], onesb[0:C, 0:1],
                                        start=True, stop=True)
                    mm.then_inc(S["cnt_ps"], 1)
                    need(eng, "dcum_sb", e.count(1, 1, back=1))
                    for h in range(2):
                        eng.matmul(p_dcum[0:NJ, h * C:(h + 1) * C], mask[:, h * NJ:(h + 1) * NJ], above[:, :],
                                   start=True, stop=False)
                        mm = eng.matmul(p_dcum[0:NJ, h * C:(h + 1) * C], mask[:, 1 + h * NJ:1 + (h + 1) * NJ], upto[:, :],
                                        start=False, stop=True)
                    mm.then_inc(S["dcum_ps"], 1)
                if (stage, what) == ("I", "reach"):
                    need(eng, "cnt_sb", e.count(1, 1))
                    eng.matmul(p_small[0:NJ, 2:3], before[:, :], cnt[:, 0:1], start=True, stop=True)
                    eng.matmul(p_small[0:NJ, 3:4], before[:, :], cnt[:, 1:2], start=True, stop=False)
                    eng.matmul(p_small[0:NJ, 3:4], onesb[0:NJ, 0:NJ], cnt[:, 0:1], start=False, stop=True
                               ).then_inc(S["cex_ps"], 1)
                if (stage, what) == ("I", "cum"):
                    need(eng, "reach_done", e.count(2, 2))
                    need(eng, "dcum_sb", e.count(1, 1))
                    need(eng, "inside_done", e.count(1, 1, back=1))
                    for h in range(2):
                        mm = eng.matmul(p_cum[0:C, 0:CAP + 1], dcum[:, h, :], reach[:, h, :], start=(h == 0), stop=(h == 1))
                    mm.then_inc(S["cum_ps"], 1)
                if (stage, what) == ("I", "idx"):
                    need(eng, "inside_done", e.count(1, 1))
                    for t in range(3):
                        sl = slice(t * SL, (t + 1) * SL)
                        dst = p_small[0:SL, 4 + t:5 + t]
                        eng.matmul(dst, inside[:, sl], onesb[0:C, 0:1], start=True, stop=False)
                        eng.matmul(dst, reach[:, 0, sl], chunkb[0:NJ, :], start=False, stop=False)
                        mm = eng.matmul(dst, reach[:, 1, sl], chunkb[0:NJ, :], start=False, stop=True)
                    mm.then_inc(S["idx_ps"], 1)
            run2(eng, part2)

        @block.vector
        def _(eng):
            eng.wait_ge(S["lam_exp"], 2)
            eng.tensor_scalar(lam[:, :], lam[:, :], 1.0, None, ALU.add).then_inc(S["lam_done"], 1)
            eng.tensor_scalar(lam_row[:, :], lam_row[:, :], 1.0, None, ALU.add).then_inc(S["lam_done"], 1)
            eng.wait_ge(S["lam_done"], 2)
            eng.reciprocal(lam[:, :], lam[:, :]).then_inc(S["lam_done"], 1)
            eng.reciprocal(lam_row[:, :], lam_row[:, :]).then_inc(S["lam_done"], 1)
            eng.wait_ge(S["decays_done"], 5)
            eng.wait_ge(S["weights_in"], 16 * N_WEIGHTS)
            eng.wait_ge(S["consts_pool"], N_CONSTS)

            def stats(b, half, src, st, mv, ve, tmp, steps_done, ve_done, root_done, last_read):
                base = NC + 5
                if half == 0:
                    need(eng, last_read, b.count(2, 2, back=1))
                    need(eng, root_done, b.count(1, 1, back=1))
                for c in chunks(half):
                    eng.bn_stats(st[:, c, :], src(c)).then_inc(S[steps_done], 1)
                if half == 0:
                    return
                need(eng, steps_done, b.count(base, NC))
                eng.tensor_tensor(tmp[:, 0, :], st[:, :, 1], st[:, :, 4], ALU.add).then_inc(S[steps_done], 1)
                eng.tensor_tensor(tmp[:, 1, :], st[:, :, 1], st[:, :, 4], ALU.subtract).then_inc(S[steps_done], 1)
                eng.tensor_tensor(tmp[:, 2, :], st[:, :, 2], st[:, :, 5], ALU.add).then_inc(S[steps_done], 1)
                need(eng, steps_done, b.count(base, NC + 3))
                eng.tensor_scalar(mv[:, :], tmp[:, 0, :], 0.5, None, ALU.mult).then_inc(S[steps_done], 1)
                eng.scalar_tensor_tensor(out=tmp[:, 1, :], in0=tmp[:, 1, :], scalar=0.25, in1=tmp[:, 1, :],
                                         op0=ALU.mult, op1=ALU.mult).then_inc(S[steps_done], 1)
                need(eng, steps_done, b.count(base, NC + 5))
                eng.scalar_tensor_tensor(out=ve[:, :], in0=tmp[:, 2, :], scalar=1.0 / D, in1=tmp[:, 1, :],
                                         op0=ALU.mult, op1=ALU.add).then_inc(S[ve_done], 1)

            def part(stage, what, b):
                if (stage, what) == ("A", "win"):
                    need(eng, "sq_done", b.count(1, 1))
                    need(eng, "wsum_ps", b.count(1, 1, back=1))
                    eng.tensor_tensor(sq2[:, 0:L - 3], sq[:, 0:L - 3], sq[:, 2:L - 1], ALU.add).then_inc(S["win_done"], 1)
                    need(eng, "win_done", b.count(3, 1))
                    eng.tensor_tensor(sq4[:, :], sq2[:, 0:LO], sq2[:, 4:LO + 4], ALU.add).then_inc(S["win_done"], 1)
                    need(eng, "win_done", b.count(3, 2))
                    eng.tensor_tensor(sq4[CIN:128, :], sq4[CIN:128, :], sq[CIN:128, TAPS - 2:TAPS - 2 + LO],
                                      ALU.add).then_inc(S["win_done"], 1)
                if (stage, what) == ("A", "w"):
                    need(eng, "wsum_ps", b.count(1, 1))
                    need(eng, "wnorm_done", b.count(1, 1, back=1))
                    eng.tensor_scalar(wnorm[:, 0, :], pst[0:C, 0:NC], 0.0, None, ALU.max).then_inc(S["wsum_sb"], 1)
                if (stage, what) == ("A", "scale"):
                    need(eng, "wnorm_done", b.count(1, 1))
                    eng.tensor_scalar(wnorm[:, 2, :], wnorm[:, 1, :], EPS_W, None, ALU.add).then_inc(S["scale_step"], 1)
                    need(eng, "scale_step", b.count(3, 1))
                    eng.reciprocal(wnorm[:, 2, :], wnorm[:, 2, :]).then_inc(S["scale_step"], 1)
                    need(eng, "scale_step", b.count(3, 2))
                    need(eng, "tanh_done", b.count(NC, NC, back=1))
                    eng.tensor_scalar(wnorm[:, 3, :], wnorm[:, 2, :], 1.0, LAM, ALU.min, ALU.mult).then_inc(S["scale_step"], 1)
                if (stage, what) in (("A", "h0"), ("A", "h1")):
                    for half in [int(what[1])]:
                        lo, hi = HALF[half]
                        need(eng, "tanh_done", b.count(NC, hi))
                        eng.tensor_tensor(y[:, lo:hi, :], y[:, lo:hi, :], rowb[0:C, 0:1, :].to_broadcast([C, hi - lo, D]),
                                          ALU.add).then_inc(S["ybias_done"], 1)
                        need(eng, "ybias_done", b.count(2, half + 1))
                        need(eng, "hb_done", b.count(1, 1, back=2))
                        eng.tensor_scalar(hres[:, b.par, lo:hi, :], y[:, lo:hi, :], 0.0, None,
                                          ALU.max).then_inc(S["h_done"], 1)
                if (stage, what) in (("A", "st0"), ("A", "st1")):
                    half = int(what[2])
                    need(eng, "h_done", b.count(2, half + 1))
                    stats(b, half, lambda c: hres[:, b.par, c, :], st1, mv1, ve1, tmp1, "stats1", "ve1_done", "rs1_done", "hn_done")
                if (stage, what) == ("A", "hn"):
                    need(eng, "rs1_done", b.count(1, 1))
                    need(eng, "hnt_ps", b.count(2, 2, back=1))
                    for half in range(2):
                        for c in chunks(half):
                            ins = eng.tensor_scalar(hn[:, c, :], hres[:, b.par, c, :], mv1[:, c:c + 1], rs1[:, c:c + 1],
                                                    ALU.subtract, ALU.mult)
                        ins.then_inc(S["hn_done"], 1)
                if (stage, what) in QK:
                    need(eng, "kt_ps", b.count(2, 2, back=1))
                    need(eng, "kd_done", b.count(1, 1, back=1))
                    for n in QK[stage, what]:
                        w, half = n // 2, n % 2
                        cols = slice(half * QH, half * QH + QH)
                        need(eng, "e_sb", b.count(4, n + 1))
                        eng.tensor_scalar(eqk[:, w, cols], eqk[:, w, cols], 1.0, None, ALU.min).then_inc(S["emin_done"], 1)
                        need(eng, "emin_done", b.count(4, n + 1))
                        eng.scalar_tensor_tensor(out=fqk[:, w, cols], in0=tqk[:, w, cols], scalar=0.0, in1=eqk[:, w, cols],
                                                 op0=ALU.max, op1=ALU.add).then_inc(S["f_done"], 1)
                if (stage, what) == ("A", "qd"):
                    need(eng, "f_done", b.count(4, 2))
                    need(eng, "o_ps", b.count(7, 7, back=2))
                    need(eng, "qb_done", b.count(4, 4, back=2))
                    eng.tensor_tensor(qd[:, b.par, :].rearrange("p (c t) -> p c t", c=NC),
                                      fqk[:, 0, :].rearrange("p (c t) -> p c t", c=NC),
                                      dq[:, :].unsqueeze(1).to_broadcast([128, NC, C]),
                                      ALU.mult).then_inc(S["qd_done"], 1)
                if (stage, what) == ("A", "kd"):
                    need(eng, "f_done", b.count(4, 4))
                    need(eng, "s_ps", b.count(14, 14, back=2))
                    eng.tensor_tensor(kd[:, b.par, :].rearrange("p (c t) -> p c t", c=NC),
                                      fqk[:, 1, :].rearrange("p (c t) -> p c t", c=NC),
                                      dk[:, :].unsqueeze(1).to_broadcast([128, NC, C]),
                                      ALU.mult).then_inc(S["kd_done"], 1)
                if (stage, what) == ("A", "v"):
                    need(eng, "o_ps", b.count(7, 7, back=2))
                    for half in range(2):
                        lo, hi = HALF[half]
                        need(eng, "v_ps", b.count(2, half + 1))
                        eng.tensor_tensor(v1[:, b.par, lo:hi, :, 0:E],
                                          pa[half][0:C, 0:(hi - lo) * D].rearrange("p (c h e) -> p c h e", h=H, e=E),
                                          rowb[0:C, 1:2, :].to_broadcast([C, hi - lo, D]).rearrange("p c (h e) -> p c h e", h=H),
                                          ALU.add).then_inc(S["v_sb"], 1)
                if (stage, what) == ("A", "kt"):
                    need(eng, "st_ps", b.count(6, 6, back=2))
                    for half in range(2):
                        lo, hi = HALF[half]
                        need(eng, "kt_ps", b.count(2, half + 1))
                        eng.tensor_tensor(kt[:, b.par, lo:hi, :].rearrange("p c (h e) -> p c h e", h=H),
                                          pa[half][0:C, 0:(hi - lo) * D].rearrange("p (c h e) -> p c h e", h=H, e=E),
                                          dks8[0:C, :].unsqueeze(1).unsqueeze(3).to_broadcast([C, hi - lo, H, E]),
                                          ALU.mult).then_inc(S["kt_sb"], 1)
                if stage == "S":
                    c = what
                    need(eng, "s_ps", b.count(14, 2 * c + 1))
                    need(eng, "o_ps", b.count(7, c - 1))
                    eng.tensor_tensor(P[:, c % 2, 0:4, :], ps[0][0:C, 0:4 * C].rearrange("p (h t) -> p h t", h=4),
                                      causal[0:C, :].unsqueeze(1).to_broadcast([C, 4, C]),
                                      ALU.mult).then_inc(S["p0_done"], 1)
                    if c < NC - 1:
                        need(eng, "st_ps", b.count(6, c + 1))
                        if c == 0:
                            need(eng, "o_ps", b.count(7, 7, back=1))
                            need(eng, "state_done", b.count(6, 6, back=1))
                            eng.tensor_tensor(state[:, 1, :], pst[:, 0:H * E1], blk[:, :], ALU.mult).then_inc(S["state_done"], 1)
                        else:
                            need(eng, "state_done", b.count(6, c))
                            eng.tensor_tensor(state_in[:, :], pst[:, 0:H * E1], blk[:, :], ALU.mult).then_inc(S["stm_done"], 1)
                            need(eng, "stm_done", b.count(5, c))
                            need(eng, "o_ps", b.count(7, c - 1))
                            eng.scalar_tensor_tensor(out=state[:, (c + 1) % 3, :], in0=state[:, c % 3, :], scalar=lamc[:, 0:1],
                                                     in1=state_in[:, :], op0=ALU.mult, op1=ALU.add).then_inc(S["state_done"], 1)
                if stage == "V":
                    c = what
                    need(eng, "o_ps", b.count(7, c + 1))
                    if c == 0:
                        need(eng, "ot_ps", b.count(2, 2, back=2))
                    ov = po[0:C, 0:H * E1].rearrange("p (h e) -> p h e", h=H)
                    need(eng, "o_done", b.count(7, c))
                    eng.tensor_scalar(den[:, 0, :], ov[:, :, E], EPS_DEN, None, ALU.add).then_inc(S["den_step"], 1)
                    need(eng, "den_step", b.count(14, 2 * c + 1))
                    eng.reciprocal(den[:, 1, :], den[:, 0, :]).then_inc(S["den_step"], 1)
                    need(eng, "den_step", b.count(14, 2 * c + 2))
                    eng.tensor_tensor(o[:, b.par, c, :].rearrange("p (h e) -> p h e", h=H), ov[:, :, 0:E],
                                      den[:, 1, :].unsqueeze(2).to_broadcast([C, H, E]), ALU.mult).then_inc(S["o_done"], 1)
                if (stage, what) in (("C", "z0"), ("C", "z1")):
                    half = int(what[1])
                    lo, hi = HALF[half]
                    need(eng, "wo_ps", b.count(2, half + 1))
                    need(eng, "h2_done", b.count(2, 2, back=1))
                    eng.tensor_tensor(z[:, lo:hi, :], pc[half][0:C, 0:(hi - lo) * D].rearrange("p (c d) -> p c d", d=D),
                                      rowb[0:C, 2:3, :].to_broadcast([C, hi - lo, D]), ALU.add).then_inc(S["z_done"], 1)
                    need(eng, "z_done", b.count(2, half + 1))
                    stats(b, half, lambda c: z[:, c, :], st2, mv2, ve2, tmp2, "stats2", "ve2_done", "rs2_done", "zn_done")
                if (stage, what) == ("C", "zn"):
                    need(eng, "rs2_done", b.count(1, 1))
                    for half in range(2):
                        lo, hi = HALF[half]
                        for c in chunks(half):
                            ins = eng.tensor_scalar(z[:, c, :], z[:, c, :], mv2[:, c:c + 1], rs2[:, c:c + 1],
                                                    ALU.subtract, ALU.mult)
                        ins.then_inc(S["zn_done"], 1)
                if (stage, what) == ("C", "zg"):
                    for half in range(2):
                        lo, hi = HALF[half]
                        need(eng, "zn_done", b.count(2, half + 1))
                        eng.tensor_tensor(z[:, lo:hi, :], z[:, lo:hi, :], rowb[0:C, 3:4, :].to_broadcast([C, hi - lo, D]),
                                          ALU.mult).then_inc(S["zg_done"], 1)
                if (stage, what) == ("C", "h2"):
                    need(eng, "hb_done", b.count(1, 1))
                    need(eng, h2_out[b.par], b.m * 16)
                    for half in range(2):
                        lo, hi = HALF[half]
                        need(eng, "zg_done", b.count(2, half + 1))
                        eng.tensor_tensor(h2[:, b.par, lo:hi, :], z[:, lo:hi, :], hb[:, lo:hi, :],
                                          ALU.add).then_inc(S["h2_done"], 1)
                if (stage, what) in (("C", "st0"), ("C", "st1")):
                    half = int(what[2])
                    need(eng, "h2_done", b.count(2, half + 1))
                    stats(b, half, lambda c: h2[:, b.par, c, :], st3, mv3, ve3, tmp3, "stats3", "ve3_done", "rs3_done", "hn2_done")
                if (stage, what) == ("C", "hn"):
                    need(eng, "rs3_done", b.count(1, 1))
                    need(eng, row_out[b.par], b.m * 16)
                    need(eng, "h2t_ps", b.count(2, 2, back=2))
                    for half in range(2):
                        for c in chunks(half):
                            ins = eng.tensor_scalar(row[:, b.par, c, 0:D], h2[:, b.par, c, :], mv3[:, c:c + 1], rs3[:, c:c + 1],
                                                    ALU.subtract, ALU.mult)
                        ins.then_inc(S["hn2_done"], 1)
                if (stage, what) == ("C", "max"):
                    need(eng, "probs_done", b.count(1, 1, back=1))
                    need(eng, "probs_row", b.count(1, 1, back=1))
                    for half in range(2):
                        lo, hi = HALF[half]
                        need(eng, "r_ps", b.count(2, half + 1))
                        eng.tensor_tensor(lg[:, lo:hi, :], pc[half][0:C, 0:(hi - lo) * NE].rearrange("p (c e) -> p c e", e=NE),
                                          brow[0:C, :].unsqueeze(1).to_broadcast([C, hi - lo, NE]), ALU.add).then_inc(S["lg_done"], 1)
                    need(eng, "lg_done", b.count(2, 2))
                    eng.tensor_reduce(lmax[:, :], lg[:, :, :], AX.X, ALU.max).then_inc(S["lmax_done"], 1)
                    need(eng, "lmax_done", b.count(1, 1))
                    eng.tensor_tensor(lg[:, :, :], lg[:, :, :], lmax[:, :].unsqueeze(2).to_broadcast([C, NC, NE]),
                                      ALU.subtract).then_inc(S["lsub_done"], 1)
                if (stage, what) == ("C", "soft"):
                    need(eng, "lexp_done", b.count(1, 1))
                    eng.tensor_reduce(lsum[:, 0, :], lg[:, :, :], AX.X, ALU.add).then_inc(S["lsum_done"], 1)
                    need(eng, "lsum_done", b.count(1, 1))
                    eng.reciprocal(lsum[:, 1, :], lsum[:, 0, :]).then_inc(S["lrec_done"], 1)
                    need(eng, "lrec_done", b.count(1, 1))
                    rb = lsum[:, 1, :].unsqueeze(2).to_broadcast([C, NC, NE])
                    eng.tensor_tensor(row[:, b.par, :, D:ROW], lg[:, :, :], rb, ALU.mult).then_inc(S["probs_row"], 1)
                    eng.tensor_tensor(probs[:, bass.ds(b.index() * NC, NC), :], lg[:, :, :], rb,
                                      ALU.mult).then_inc(S["probs_done"], 1)
            run(eng, part)
            for n in range(0, JS // 4, 2):
                eng.wait_ge(S["seg_ps"], n + 1)
                eng.tensor_copy(seg_probs[:, n * 4 * C:(n + 1) * 4 * C], SEG_BANKS[n][:, 0:4 * C]).then_inc(S["seg_dve"], 1)
            eng.wait_ge(S["seg_dve"], (JS // 4 + 1) // 2)
            eng.wait_ge(S["seg_act"], JS // 8)
            eng.tensor_copy(high, halves[:, :, 1]).then_inc(S["keys_done"], 1)
            eng.wait_ge(S["keys_done"], 1)

            def search(keys, goal, nbits, steps_before, counts_before):
                eng.memset(cand[:, :], float(1 << (nbits - 1))).then_inc(S["bit_step"], 1)
                eng.memset(bit[:, 0:1], float(1 << (nbits - 1))).then_inc(S["bit_step"], 1)
                with eng.Fori(0, nbits // 2) as r:
                    for k in range(2):
                        def after(n):
                            return r * 6 + (steps_before + 2 + 3 * k + n)
                        eng.wait_ge(S["bit_step"], after(0))
                        eng.tensor_scalar(seg_hits, keys, cand[:, :], None, ALU.is_ge, ALU.add,
                                          accum_out=hits[:, :]).then_inc(S["hits_done"], 1)
                        eng.tensor_scalar(bit[:, 1 - k:2 - k], bit[:, k:k + 1], 0.5, None, ALU.mult
                                          ).then_inc(S["bit_step"], 1)
                        eng.wait_ge(S["hits_ps"], r * 2 + (counts_before + k + 1))
                        eng.tensor_scalar(step_to[:, :], pst[:, 0:1], goal, 0.5, ALU.is_ge, ALU.subtract
                                          ).then_inc(S["bit_step"], 1)
                        eng.wait_ge(S["bit_step"], after(2))
                        eng.scalar_tensor_tensor(out=cand[:, :], in0=step_to[:, :], scalar=bit[:, k:k + 1], in1=cand[:, :],
                                                 op0=ALU.mult, op1=ALU.add).then_inc(S["bit_step"], 1)
                eng.wait_ge(S["bit_step"], steps_before + 2 + 3 * nbits)

            search(high, target[:, 0:1], HIGH_BITS, 0, 0)
            eng.tensor_scalar(thr_high[:, 0:1], cand[:, :], 0.5, None, ALU.subtract).then_inc(S["thr_step"], 1)
            eng.tensor_scalar(thr_high[:, 1:2], cand[:, :], 0.5, None, ALU.add).then_inc(S["thr_step"], 1)
            eng.wait_ge(S["thr_step"], 2)
            eng.tensor_scalar(seg_hits, high, thr_high[:, 1:2], None, ALU.is_ge, ALU.add,
                              accum_out=hits[:, :]).then_inc(S["hits_done"], 1)
            eng.wait_ge(S["low_done"], 1)
            eng.scalar_tensor_tensor(out=low_tied, in0=high, scalar=thr_high[:, 0:1], in1=low,
                                     op0=ALU.is_equal, op1=ALU.mult).then_inc(S["keys_done"], 1)
            eng.wait_ge(S["hits_ps"], HIGH_BITS + 1)
            eng.tensor_scalar(target[:, 1:2], pst[:, 0:1], -1.0, float(CAP), ALU.mult, ALU.add).then_inc(S["thr_step"], 1)
            eng.wait_ge(S["thr_step"], 3)
            eng.wait_ge(S["keys_done"], 2)
            search(low_tied, target[:, 1:2], LOW_BITS, 2 + 3 * HIGH_BITS, HIGH_BITS + 1)
            eng.tensor_scalar(thr_high[:, 1:2], cand[:, :], 0.5, None, ALU.subtract).then_inc(S["thr_step"], 1)
            eng.wait_ge(S["thr_step"], 4)
            eng.tensor_copy(thr_bits[:, :], thr_high[:, :]).then_inc(S["thr_step"], 1)
            eng.wait_ge(S["thr_step"], 5)
            eng.tensor_scalar(thr_bits[:, 0:1], thr_bits[:, 0:1], 16, None, ALU.logical_shift_left).then_inc(S["thr_step"], 1)
            eng.wait_ge(S["thr_step"], 6)
            eng.tensor_tensor(thr_bits[:, 0:1], thr_bits[:, 0:1], thr_bits[:, 1:2], ALU.bitwise_or).then_inc(S["thr_step"], 1)
            eng.wait_ge(S["thr_step"], 7)
            eng.tensor_copy(thr_wide[:, :], thr_bits[0:NE, 0:1].bitcast(f32).to_broadcast([NE, C])).then_inc(S["thr_step"], 1)
            eng.wait_ge(S["thr_ps"], 1)
            eng.tensor_copy(thr[:, :], pst[0:C, 0:NE]).then_inc(S["thr_done"], 1)
            eng.wait_ge(S["thr_done"], 1)

            def part2(stage, what, e):
                if (stage, what) == ("I", "mask"):
                    need(eng, "dcum_ps", e.count(1, 1, back=1))
                    own, at = probs[:, :, bass.ds(e.index(), 1)], thr[:, bass.ds(e.index(), 1)]
                    for h, op in enumerate((ALU.is_gt, ALU.is_equal)):
                        eng.tensor_scalar(mask[:, 1 + h * NJ:1 + (h + 1) * NJ].unsqueeze(2), own, at, None, op
                                          ).then_inc(S["mask_done"], 1)
                if (stage, what) == ("F", "x"):
                    need(eng, x_got[e.par], e.half() * 48)
                    need(eng, "yw_done", e.count(2, 2, back=2))
                    own = bass.ds(e.index() + D, 1)
                    eng.tensor_copy(gcol[:, e.par, 0:2].unsqueeze(2), xg[:, e.par, 0:2, own]).then_inc(S["gcol_done"], 1)
                    n = CAP - 2 * SL
                    eng.tensor_copy(gcol[0:n, e.par, 2:3], xg[0:n, e.par, 2, own]).then_inc(S["gcol_done"], 1)
                if (stage, what) == ("I", "cnt"):
                    need(eng, "cnt_ps", e.count(1, 1))
                    need(eng, "cex_ps", e.count(1, 1, back=1))
                    eng.tensor_copy(cnt[:, :], p_small[0:NJ, 0:2]).then_inc(S["cnt_sb"], 1)
                if (stage, what) == ("I", "reach"):
                    need(eng, "cex_ps", e.count(1, 1))
                    need(eng, "reach_done", e.count(2, 2, back=1))
                    eng.tensor_copy(cex[:, :], p_small[0:NJ, 2:4]).then_inc(S["cex_sb"], 1)
                    need(eng, "cex_sb", e.count(1, 1))
                    need(eng, "idx_ps", e.count(1, 1, back=1))
                    for h in range(2):
                        eng.tensor_scalar(reach[:, h, :], slots_h[:, :], cex[:, h:h + 1], None, ALU.is_ge
                                          ).then_inc(S["reach_done"], 1)
                if (stage, what) == ("I", "cum"):
                    need(eng, "cum_ps", e.count(1, 1))
                    eng.tensor_tensor(inside[:, :], p_cum[0:C, 0:CAP + 1], slots_f[:, :], ALU.is_le
                                      ).then_inc(S["inside_done"], 1)
                if (stage, what) == ("I", "idx"):
                    need(eng, "idx_ps", e.count(1, 1))
                    need(eng, "idx_done", e.count(1, 1, back=1))
                    need(eng, y_out, e.count(48, 0, back=3))
                    eng.tensor_scalar(wrap[:, :], p_small[0:SL, 4:7], float(N + C), float(N), ALU.is_ge, ALU.mult
                                      ).then_inc(S["wrap_done"], 1)
                    need(eng, "wrap_done", e.count(1, 1))
                    eng.scalar_tensor_tensor(out=idx[:, e.k, :], in0=p_small[0:SL, 4:7], scalar=-float(C), in1=wrap[:, :],
                                             op0=ALU.add, op1=ALU.subtract).then_inc(S["idx_done"], 1)
                if (stage, what) == ("D", "out"):
                    need(eng, "dn_ps", e.count(1, 1))
                    need(eng, y_out, e.count(48, 48, back=2))
                    need(eng, "gcol_done", e.count(2, 2))
                    n = CAP - 2 * SL
                    eng.tensor_tensor(yw[:, e.par, 0:2, :], p_dn[0:SL, 0:2 * D].rearrange("p (t d) -> p t d", t=2),
                                      gcol[:, e.par, 0:2].unsqueeze(2).to_broadcast([SL, 2, D]), ALU.mult
                                      ).then_inc(S["yw_done"], 1)
                    eng.tensor_scalar(yw[0:n, e.par, 2, :], p_dn[0:n, 2 * D:3 * D], gcol[0:n, e.par, 2:3], None, ALU.mult
                                      ).then_inc(S["yw_done"], 1)
            run2(eng, part2)


N_WEIGHTS = 23
HIGH_BITS, LOW_BITS = 14, 16
N_CONSTS = 42

_INS = ['x', 'L0_tok_kernel', 'L0_tok_bias', 'L0_attn_Wqkv', 'L0_attn_bqkv', 'L0_attn_Wout', 'L0_attn_bout',
        'L0_attn_ln_gamma', 'L0_attn_ln_beta', 'L0_attn_decay_logits', 'L0_ffn_W_router', 'L0_ffn_b_router',
        'L0_ffn_W_up', 'L0_ffn_b_up', 'L0_ffn_W_down', 'L0_ffn_b_down']
_OUTS = [((16, 742, 128), 'float32')]


def kernel(**inputs):
    import numpy as _np
    import concourse.bacc as _bacc
    from concourse import mybir as _mybir
    from concourse.bass_utils import run_bass_kernel_spmd as _run

    nc = _bacc.Bacc("TRN2", target_bir_lowering=False, num_devices=1)
    arrays, args = {}, []
    for name in _INS:
        a = _np.ascontiguousarray(inputs[name])
        arrays[f"in_{name}_dram"] = a
        args.append(nc.dram_tensor(f"in_{name}_dram", a.shape, _mybir.dt.from_np(a.dtype), kind="ExternalInput").ap())
    for i, (shape, dtype) in enumerate(_OUTS):
        dt = _mybir.dt.from_np(_np.dtype(dtype))
        args.append(nc.dram_tensor(f"out_{i}_dram", shape, dt, kind="ExternalOutput").ap())
    audio_tower_kernel(nc, *args)
    r = _run(nc, [arrays], core_ids=[0])
    return r.results[0]["out_0_dram"]
```

```python
import concourse.bass as bass
from concourse import mybir
from contextlib import ExitStack


def audio_tower_kernel(nc, x, tok_w, tok_b, w_qkv, b_qkv, w_out, b_out, ln_g, ln_b, decay,
                       w_router, b_router, w_up, b_up, w_down, b_down, out):
    f32, bf16, f16 = mybir.dt.float32, mybir.dt.bfloat16, mybir.dt.float16
    i32, u16 = mybir.dt.int32, mybir.dt.uint16
    ALU, ACT, AX = mybir.AluOpType, mybir.ActivationFunctionType, mybir.AxisListType

    NB, L, CIN = x.shape
    TAPS, _, D = tok_w.shape
    LO = L - TAPS + 1
    C = 106
    NC = LO // C
    XC = (L - 1) // NC
    H = decay.shape[0]
    E = D // H
    E1 = E + 1
    N = NB * LO
    NJ = NB * NC
    NE = w_router.shape[1]
    NG = w_up.shape[0]
    GS = NE // NG
    F = w_up.shape[2]
    CAP = N // NE
    FC = 114
    SL = 124
    ROW = D + NE
    DVE_KEYS = 2000
    SEG = 128 // NE
    JS = NJ // SEG
    ACT_HALF = SEG * (JS * C - DVE_KEYS) / 2
    HALF = [(0, 4), (4, NC)]
    HC = C // 2
    QH = LO // 2
    LAM = 1.0 / (1.0 + 1e-07)
    EPS_W, EPS_LN, EPS_DEN = 1e-07, 1e-05, 1e-05
    assert GS == 4 and 2 * HC == C and NC * C == LO and XC * NC == L - 1 and CAP * NE == N and 3 * FC == F + 1

    ctx = ExitStack()
    with ctx:
        ctx.enter_context(nc.allow_low_precision(reason="the search's counts are whole numbers up to 2048, exact in float16"))

        def sb(name, shape, dt=f32):
            return ctx.enter_context(nc.sbuf_tensor(name, shape, dt))

        def pb(name):
            return ctx.enter_context(nc.psum_tensor(name, [128, 512], f32))

        def sem(name):
            return ctx.enter_context(nc.semaphore(name))

        rows = nc.dram_tensor("token_rows", (N, ROW), f32, kind="Internal").ap()

        ident = sb("ident", [128, 128])
        ones = sb("ones", [128, 1])
        wc = sb("wc", [128, (TAPS + 1) // 2, D])
        wqkv = sb("wqkv", [128, 3 * D])
        wo = sb("wo", [128, D])
        wr = sb("wr", [128, NE])
        bqk = sb("bqk", [128, 2])
        rowb = sb("rowb", [128, 5, D])
        brow = sb("brow", [128, NE])
        lam_row_in = sb("lam_row_in", [128, H])
        lam_row = sb("lam_row", [128, H])
        lamc = sb("lamc", [128, 1])
        lamc_inv = sb("lamc_inv", [128, 1])
        step_cols = sb("step_cols", [128, 2, H])
        powers = sb("powers", [128, 2, H])
        spread = sb("spread", [C + 1, 2, D])
        dq = sb("dq", [128, C])
        dk = sb("dk", [128, C])
        head_scale = sb("head_scale", [128, 2, 4])
        head4 = sb("head4", [128, 4])
        blk = sb("blk", [128, H * E1])
        causal = sb("causal", [C, 2, HC])
        of_half = sb("of_half", [C, 2])
        expo = sb("expo", [128, 2, NC])

        xw = sb("xw", [XC, 2, NC, 2 * CIN])
        xT = sb("xT", [128, L - 1])
        sq = sb("sq", [128, L - 1])
        sq2 = sb("sq2", [128, L - 1])
        sq4 = sb("sq4", [128, LO])
        wnorm = sb("wnorm", [C, 4, NC])
        y = sb("y", [C, NC, D])
        hres = sb("hres", [C, 2, NC, D])
        st1 = sb("st1", [C, NC, 6])
        mv1 = sb("mv1", [C, NC])
        tmp1 = sb("tmp1", [C, 3, NC])
        ve1 = sb("ve1", [C, NC])
        rs1 = sb("rs1", [C, NC])
        mr1 = sb("mr1", [C, NC])
        hn = sb("hn", [C, NC, D])
        hnT = sb("hnT", [128, LO])
        tqk = sb("tqk", [128, 2, LO])
        eqk = sb("eqk", [128, 2, LO])
        fqk = sb("fqk", [128, 2, LO])
        qd = sb("qd", [128, 2, LO])
        qb = sb("qb", [128, 2, 2, 4, QH])
        kd = sb("kd", [128, 2, 2, LO])
        kt = sb("kt", [C, 2, NC, D])
        v1 = sb("v1", [C, 2, NC, H, E1])
        vm = sb("vm", [C, 2, NC, 2, H * E1])
        P = sb("P", [C, 2, 2, 4, HC])
        state = sb("state", [128, 3, 2, H * E1])
        state_in = sb("state_in", [128, 2, H * E1])
        den = sb("den", [HC, 2, 2 * H])
        o = sb("o", [HC, 2, NC, 2 * D])
        oT = sb("oT", [128, LO])
        z = sb("z", [C, NC, D])
        st2 = sb("st2", [C, NC, 6])
        mv2 = sb("mv2", [C, NC])
        tmp2 = sb("tmp2", [C, 3, NC])
        ve2 = sb("ve2", [C, NC])
        rs2 = sb("rs2", [C, NC])
        mr2 = sb("mr2", [C, NC])
        hb = sb("hb", [C, NC, D])
        h2 = sb("h2", [C, 2, NC, D])
        st3 = sb("st3", [C, NC, 6])
        mv3 = sb("mv3", [C, NC])
        tmp3 = sb("tmp3", [C, 3, NC])
        ve3 = sb("ve3", [C, NC])
        rs3 = sb("rs3", [C, NC])
        mr3 = sb("mr3", [C, NC])
        row = sb("row", [C, 2, NC, ROW])
        h2T = sb("h2T", [128, LO])
        lg = sb("lg", [C, NC, NE])
        lmax = sb("lmax", [C, NC])
        lsum = sb("lsum", [C, 2, NC])
        probs = sb("probs", [C, NJ, NE])

        seg_probs = qb[:, 0].rearrange("p k a b -> p (k a b)")
        seg_hits = qb[:, 1, 0].rearrange("p a b -> p (a b)").bitcast(bf16)
        signs = sq4[:, :].bitcast(bf16)[:, 0:JS * C - DVE_KEYS]
        halves = seg_probs.bitcast(u16).rearrange("p (n two) -> p n two", two=2)
        high = qb[:, 1, 1].rearrange("p a b -> p (a b)").bitcast(u16)
        low = kd[:, 0].rearrange("p a b -> p (a b)").bitcast(u16)
        low_tied = fqk[:, :, :].rearrange("p a b -> p (a b)").bitcast(u16)
        same_expert = sb("same_expert", [128, 128], f16)
        bit = sb("bit", [128, 2])
        cand = sb("cand", [128, 1])
        hits = sb("hits", [128, 2], f16)
        sign_sum = sb("sign_sum", [128, 1], f16)
        half_expert = sb("half_expert", [128, 128], f16)
        target = sb("target", [128, 2])
        step_to = sb("step_to", [128, 1])
        thr_high = sb("thr_high", [128, 2])
        thr_bits = sb("thr_bits", [128, 2], i32)
        thr_wide = sb("thr_wide", [NE, C])
        thr = sb("thr", [C, NE])
        onesb = sb("onesb", [128, 128], bf16)
        chunkb = sb("chunkb", [128, 1], bf16)
        above = sb("above", [C, C], bf16)
        upto = sb("upto", [C, C], bf16)
        before = sb("before", [NJ, NJ], bf16)
        slots_h = sb("slots_h", [NJ, CAP + 1], f16)
        slots_f = sb("slots_f", [C, CAP + 1])
        mask = sb("mask", [C, 1 + 2 * NJ], bf16)
        cnt = sb("cnt", [NJ, 2], bf16)
        cex = sb("cex", [NJ, 2])
        reach = hnT[0:NJ, :].bitcast(bf16)[:, 0:2 * (CAP + 1)].rearrange("p (h n) -> p h n", h=2)
        dcum = sb("dcum", [NJ, 2, C], bf16)
        inside = sb("inside", [C, CAP + 1], bf16)
        wrap = sb("wrap", [SL, 3])
        idx = sb("idx", [SL, 4, 3], i32)
        xg = qd[0:SL, :, 0:3 * ROW].rearrange("p a (t d) -> p a t d", t=3)
        gcol = sb("gcol", [SL, 2, 3])
        xgT = eqk[:, 0, 0:CAP]
        wup = kd[:, 1].rearrange("p a b -> p (a b)")[:, 0:4 * F].rearrange("p (k f) -> p k f", k=4)
        wdn = qb[0:FC, 1].rearrange("p a b c -> p (a b c)")[:, 0:12 * D].rearrange("p (k c d) -> p k c d", k=4, c=3)
        bup = sb("bup", [FC, NG, 3])
        act = seg_probs[0:FC, 0:6 * CAP].rearrange("p (a k n) -> p a k n", a=2, k=3)
        yw = tqk[0:SL, :, 0:3 * D].rearrange("p a (t d) -> p a t d", t=3)

        pa = [pb("pa0"), pb("pa1")]
        ps = [pb("ps0"), pb("ps1")]
        po = pb("po")
        pst = pb("pst")
        pc = [pb("pc0"), pb("pc1")]

        p_xg, p_up, p_dn, p_small, p_dcum, p_cum = pa[0], [pa[1], ps[0], ps[1]], po, pst, pc[0], pc[1]

        names = """weights_in wc_in decay_in consts_pool lam_exp powers_done spread_done spread_ps lam_done
            decays_done xt_ps xt_sb sq_done win_done wsum_ps wsum_sb wnorm_done scale_step conv_ps tanh_done
            ybias_done h_done stats1 ve1_done rs1_done hn_done hnt_ps hnt_sb qk_ps t_sb e_sb f_done qd_done
            qb_done kd_done v_ps v_sb kt_ps kt_sb s_ps p_done vm_done kdec_done nine_done qm_done ones_done
            o_ps st_ps stm_done state_done den_step o_done ot_ps ot_sb wo_ps z_done stats2 ve2_done rs2_done
            zn_done zg_done hb_done h2_done stats3 ve3_done rs3_done hn2_done h2t_ps h2t_sb r_ps lg_done
            lmax_done lsub_done lexp_done lsum_done lrec_done probs_done probs_row held_sync held_pool
            held_act bup_in seg_ps seg_act seg_dve keys_done low_done bit_step hits_done signs_done hits_ps
            thr_step thr_ps thr_done mask_done cnt_ps cnt_sb cex_ps cex_sb dcum_ps dcum_sb reach_done cum_ps
            inside_done idx_ps wrap_done idx_done xgt_ps gcol_done xgt_sb up_ps act_done dn_ps yw_done
            mr1_done mr2_done mr3_done hn_done1 zn_done1 hn2_done1""".split()
        S = {n: sem(n) for n in names}
        x_in = [sem("x_in0"), sem("x_in1")]
        w_in = [sem(f"w_in{k}") for k in range(4)]
        x_got = [sem("x_got0"), sem("x_got1")]
        y_out = sem("y_out")
        h2_out = [sem("h2_out0"), sem("h2_out1")]
        row_out = [sem("row_out0"), sem("row_out1")]

        class Batch:
            def __init__(self, m, par):
                self.m, self.par = m, par

            def count(self, per, k, back=0):
                return self.m * (2 * per) + (per * (self.par - back) + k)

            def index(self):
                return self.m * 2 + self.par

        def BEFORE(b):
            return Batch(b.m, 0) if b.par else Batch(b.m - 1, 1)

        def AFTER(b):
            return Batch(b.m + 1, 0) if b.par else Batch(b.m, 1)

        def need(eng, s, value):
            if isinstance(value, int) and value <= 0:
                return
            eng.wait_ge(S[s] if isinstance(s, str) else s, value)

        def need_both(eng, s, value):
            need(eng, s, value)
            need(eng, s + "1", value)

        def chunks(half):
            return range(*HALF[half])

        def hold(eng, s, value):
            if isinstance(value, int) and value <= 0:
                return
            eng.wait_ge(S[s] if isinstance(s, str) else s, value)
            eng.sem_inc(S["held_sync" if eng is nc.sync else "held_pool" if eng is nc.gpsimd else "held_act"])

        ORDER = [("C", "o0"), ("A", "x"), ("S", 0), ("C", "o1"), ("C", "w0"), ("C", "w1"), ("T", 0), ("A", "sq"),
                 ("C", "z0"), ("S", 1), ("T", 1), ("V", 0), ("S", 2), ("A", "win"), ("C", "z1"), ("C", "zn"),
                 ("A", "conv0"), ("A", "win1"), ("T", 2), ("V", 1), ("A", "w"), ("V", 2), ("A", "scale"),
                 ("C", "zg"), ("S", 3), ("T", 3), ("A", "h0"), ("S", 4), ("A", "conv1"), ("A", "st0"),
                 ("A", "h1"), ("T", 4), ("V", 3), ("A", "st1"), ("S", 5), ("C", "h2"), ("T", 5), ("A", "hn0"),
                 ("V", 4), ("C", "st0"), ("A", "hn1"), ("C", "st1"), ("S", 6), ("A", "hnT0"), ("A", "hnT1"),
                 ("A", "q0"), ("C", "hn0"), ("A", "q1"), ("V", 5), ("C", "hn1"), ("A", "qd"), ("A", "k0"),
                 ("T", 6), ("A", "qm0"), ("A", "k1"), ("C", "t0"), ("A", "kd"), ("A", "qb0"), ("C", "t1"),
                 ("A", "qm1"), ("A", "qb1"), ("A", "kd0"), ("C", "r0"), ("A", "kd1"), ("A", "v0"), ("A", "v1"),
                 ("C", "r1"), ("C", "max"), ("V", 6), ("A", "kt0"), ("A", "kt1"), ("C", "soft"), ("A", "vm")]
        PEEL_IN, TAIL = 4, 2
        QK = ("q0", "q1", "k0", "k1")
        WSUM_AT = [w for s, w in ORDER[ORDER.index(("A", "w")):] if s == "T"][0]

        def run(eng, part):
            def iteration(M, p, a, b, c):
                before = Batch(M, 0) if p else Batch(M - 1, 1)
                batch = {"A": Batch(M, p), "S": before, "T": before, "V": before, "C": Batch(M - 1, p)}
                for stage, what in ORDER:
                    if {"A": a, "S": b, "T": b, "V": b, "C": c}[stage]:
                        part(stage, what, batch[stage])
            for i in range(PEEL_IN):
                iteration(i // 2, i % 2, True, i >= 1, i >= 2)
            with eng.Fori(PEEL_IN // 2, NB // 2) as M:
                for p in range(2):
                    iteration(M, p, True, True, True)
            for i in range(NB, NB + TAIL):
                iteration(i // 2, i % 2, False, i < NB + 1, True)

        SEG_BANKS = [pa[0], pa[1], ps[0], ps[1], po, pst, pc[0]]
        GROUPS, GC = JS // 4, 4 * C
        assert (GROUPS - 1) * 4 * SEG <= (NB - 1) * NC

        class Expert:
            def __init__(self, m, k):
                self.m, self.k = m + k // 4, k % 4
                self.par = k % 2

            def count(self, per, k, back=0):
                return self.m * (4 * per) + (per * (self.k - back) + k)

            def half(self, back=0):
                return self.m * 2 + (self.k // 2 + 1 - back)

            def index(self):
                return self.m * 4 + self.k

        ORDER2 = [("I", "mask"), ("F", "x"), ("D", "down0"), ("I", "cnt"), ("D", "down1"), ("I", "reach"),
                  ("D", "down2"), ("D", "out"), ("F", "up0"), ("I", "cum"), ("F", "up1"), ("I", "idx"),
                  ("F", "up2")]
        UP, DOWN = ("up0", "up1", "up2"), ("down0", "down1", "down2")
        BEHIND = {"I": 0, "F": 2, "D": 3}

        def run2(eng, part):
            def iteration(M, p, on):
                for stage, what in ORDER2:
                    k = p - BEHIND[stage]
                    if on[stage]:
                        part(stage, what, Expert(M, k) if k >= 0 else Expert(M - 1, k + 4))
            for i in range(4):
                iteration(0, i, {stage: i >= back for stage, back in BEHIND.items()})
            with eng.Fori(1, NE // 4) as M:
                for p in range(4):
                    iteration(M, p, {stage: True for stage in BEHIND})
            for i in range(max(BEHIND.values())):
                iteration(NE // 4, i, {stage: i < back for stage, back in BEHIND.items()})

        def half_tokens(x, u):
            return x.rearrange("p (c u t) -> p u c t", c=NC, u=2)[:, u]

        def last(b):
            return isinstance(b.m, int) and b.index() == NB - 1

        def first(b):
            return isinstance(b.m, int) and b.index() == 0

        block = ctx.enter_context(nc.Block())

        @block.sync
        def _(eng):
            w2 = tok_w[0:TAPS - 1, :, :].rearrange("(k t) c f -> t c k f", t=2)

            def load_x(b):
                for t in range(2):
                    eng.dma_start(xw[:, b.par, :, t * CIN:(t + 1) * CIN],
                                  x[b.index(), t:t + L - 1, :].rearrange("(c p) d -> p c d", p=XC)
                                  ).then_inc(x_in[b.par], 16)

            load_x(Batch(0, 0))
            eng.dma_start(wc[0:CIN, 0:4, :], w2[0]).then_inc(S["wc_in"], 16)
            eng.dma_start(wc[CIN:128, 0:4, :], w2[1]).then_inc(S["wc_in"], 16)
            eng.dma_start(wc[CIN:128, 4, :], tok_w[TAPS - 1]).then_inc(S["wc_in"], 16)
            eng.dma_start(lam_row_in[:, :], decay.partition_broadcast(128)).then_inc(S["decay_in"], 16)
            n = 0
            for dst, src in [
                (rowb[:, 0, :], tok_b.partition_broadcast(128)),
                (wqkv[:, :], w_qkv), (bqk[:, 0:1], b_qkv[0:D].unsqueeze(1)), (bqk[:, 1:2], b_qkv[D:2 * D].unsqueeze(1)),
                (rowb[:, 1, :], b_qkv[2 * D:].partition_broadcast(128)), (wo[:, :], w_out), (wr[:, :], w_router),
                (rowb[:, 2, :], b_out.partition_broadcast(128)), (rowb[:, 3, :], ln_g.partition_broadcast(128)),
                (rowb[:, 4, :], ln_b.partition_broadcast(128)), (brow[:, :], b_router.partition_broadcast(128)),
            ]:
                eng.dma_start(dst, src).then_inc(S["weights_in"], 16)
                n += 1
            assert n == N_WEIGHTS

            def store_rows(b):
                hold(eng, "hn2_done", b.count(1, 1))
                hold(eng, "hn2_done1", b.count(1, 1))
                hold(eng, "probs_row", b.count(1, 1))
                eng.dma_start(rows[bass.ds(b.index() * LO, LO), :].rearrange("(c p) d -> p c d", p=C),
                              row[:, b.par, :, :]).then_inc(row_out[b.par], 16)

            def part(stage, what, b):
                if (stage, what) == ("A", "x") and not first(b):
                    hold(eng, "xt_ps", b.count(2, 2, back=2))
                    load_x(b)
                if (stage, what) == ("C", "hn0"):
                    hold(eng, "h2_done", b.count(2, 2))
                    eng.dma_start(out[b.index(), :, :].rearrange("(c p) d -> p c d", p=C),
                                  h2[:, b.par, :, :]).then_inc(h2_out[b.par], 16)
                if (stage, what) == ("C", "w1") and not first(b):
                    store_rows(BEFORE(b))
            run(eng, part)
            store_rows(Batch(NB // 2 - 1, 1))
            for g in range(NG):
                for k in range(3):
                    n = FC if k < 2 else FC - 1
                    eng.dma_start(bup[0:n, g, k:k + 1], b_up[g, k * FC:k * FC + n].unsqueeze(1)).then_inc(S["bup_in"], 16)

            def part2(stage, what, e):
                if (stage, what) == ("I", "mask"):
                    if isinstance(e.m, int) and e.index() == 0:
                        eng.wait_ge(S["thr_done"], 1)
                    hold(eng, "up_ps", e.count(3, 3, back=4))
                    hold(eng, "dn_ps", e.count(1, 1, back=4))
                    w = wdn[:, e.k, :, :]
                    n = e.index()
                    eng.dma_start(wup[:, e.k, :], w_up[e.m, :, :]).then_inc(w_in[e.k], 16)
                    eng.dma_start(w[:, 0:2, :], w_down[n, 0:2 * FC, :].rearrange("(k p) d -> p k d", p=FC)
                                  ).then_inc(w_in[e.k], 16)
                    eng.dma_start(w[0:FC - 1, 2, :], w_down[n, 2 * FC:F, :]).then_inc(w_in[e.k], 16)
                    eng.dma_start(w[FC - 1:FC, 2, :], b_down[bass.ds(n, 1), :]).then_inc(w_in[e.k], 16)
            run2(eng, part2)
            eng.wait_ge(y_out, 16 * 3 * NE)

        @block.gpsimd
        def _(eng):
            made = [0]

            def step(ins):
                made[0] += 1
                ins.then_inc(S["consts_pool"], 1)
                eng.wait_ge(S["consts_pool"], made[0])

            step(eng.memset(ident[:, :], 0.0))
            step(eng.affine_select(out=ident[:, :], in_=ident[:, :], compare_op=ALU.not_equal, fill=1.0, base=0,
                                   pattern=[[-1, 128]], channel_multiplier=1))
            eng.memset(ones[:, :], 1.0).then_inc(S["consts_pool"], 1)
            eng.memset(expo[:, 0, :], -0.5).then_inc(S["consts_pool"], 1)
            eng.memset(expo[:, 1, :], 0.5).then_inc(S["consts_pool"], 1)
            made[0] += 3
            step(eng.iota(step_cols[:, 0, :], pattern=[[0, H]], base=0, channel_multiplier=1,
                          allow_small_or_imprecise_dtypes=True))
            step(eng.iota(step_cols[:, 1, :], pattern=[[0, H]], base=0, channel_multiplier=-1,
                          allow_small_or_imprecise_dtypes=True))
            assert made[0] == FIRST_CONSTS
            eng.wait_ge(S["lam_done"], 2)
            eng.tensor_tensor(powers[:, :, :], lam_row[:, :].unsqueeze(1).to_broadcast([128, 2, H]), step_cols[:, :, :],
                              ALU.pow).then_inc(S["powers_done"], 1)
            eng.memset(v1[:, :, :, :, :], 1.0).then_inc(S["consts_pool"], 1)
            eng.memset(causal[:, :, :], 1.0).then_inc(S["consts_pool"], 1)
            eng.memset(of_half[:, :], 1.0).then_inc(S["consts_pool"], 1)
            eng.memset(kd[:, :, :, :], 0.0).then_inc(S["consts_pool"], 1)
            eng.memset(head4[:, :], 1.0).then_inc(S["consts_pool"], 1)
            made[0] += 5
            step(eng.memset(blk[:, :], 1.0))
            for u in range(2):
                w = causal[:, u, :]
                step(eng.affine_select(out=w, in_=w, compare_op=ALU.is_ge, fill=0.0, base=u * HC,
                                       pattern=[[1, HC]], channel_multiplier=-1))
            w = causal[:, 1, :]
            step(eng.affine_select(out=w, in_=w, compare_op=ALU.is_ge, fill=0.0, base=-HC,
                                   pattern=[[0, HC]], channel_multiplier=1))
            step(eng.tensor_tensor(causal[:, 0, :], causal[:, 0, :], causal[:, 1, :], ALU.add))
            for u in range(2):
                w = of_half[:, u:u + 1]
                step(eng.affine_select(out=w, in_=w, compare_op=ALU.is_ge, fill=0.0, base=-HC if u else HC - 1,
                                       pattern=[[0, 1]], channel_multiplier=1 if u else -1))
            for g in range(2):
                w = head4[64 * g:64 * g + 64, :]
                step(eng.affine_select(out=w, in_=w, compare_op=ALU.is_ge, fill=0.0, base=0,
                                       pattern=[[-E, 4]], channel_multiplier=1))
                step(eng.affine_select(out=w, in_=w, compare_op=ALU.is_ge, fill=0.0, base=E - 1,
                                       pattern=[[E, 4]], channel_multiplier=-1))
            b3 = blk[:, :].rearrange("p (h e) -> p h e", h=H)
            step(eng.affine_select(out=b3, in_=b3, compare_op=ALU.is_ge, fill=0.0, base=0,
                                   pattern=[[-E, H], [0, E1]], channel_multiplier=1))
            step(eng.affine_select(out=b3, in_=b3, compare_op=ALU.is_ge, fill=0.0, base=E - 1,
                                   pattern=[[E, H], [0, E1]], channel_multiplier=-1))
            assert made[0] == ATTENTION_CONSTS

            def late_constants():
                step(eng.memset(same_expert[:, :], 0.0))
                for k in range(-3, 4):
                    step(eng.affine_select(out=same_expert[:, :], in_=same_expert[:, :], compare_op=ALU.not_equal,
                                           fill=1.0, base=NE * k, pattern=[[-1, 128]], channel_multiplier=1))
                eng.memset(onesb[:, :], 1.0).then_inc(S["consts_pool"], 1)
                eng.memset(chunkb[:, :], float(C)).then_inc(S["consts_pool"], 1)
                eng.memset(mask[:, :], 0.0).then_inc(S["consts_pool"], 1)
                eng.memset(target[:, :], float(CAP) - ACT_HALF).then_inc(S["consts_pool"], 1)
                eng.tensor_scalar(half_expert[:, :], same_expert[:, :], -0.5, None, ALU.mult).then_inc(S["consts_pool"], 1)
                made[0] += 5
                for m in (above, upto, before):
                    step(eng.memset(m[:, :], 1.0))
                step(eng.affine_select(out=above[:, :], in_=above[:, :], compare_op=ALU.is_gt, fill=0.0, base=0,
                                       pattern=[[-1, C]], channel_multiplier=1))
                step(eng.affine_select(out=upto[:, :], in_=upto[:, :], compare_op=ALU.is_ge, fill=0.0, base=0,
                                       pattern=[[1, C]], channel_multiplier=-1))
                step(eng.affine_select(out=before[:, :], in_=before[:, :], compare_op=ALU.is_gt, fill=0.0, base=0,
                                       pattern=[[1, NJ]], channel_multiplier=-1))
                step(eng.iota(slots_h[:, :], pattern=[[1, CAP + 1]], base=0, channel_multiplier=0,
                              allow_small_or_imprecise_dtypes=True))
                step(eng.iota(slots_f[:, :], pattern=[[1, CAP + 1]], base=0, channel_multiplier=0,
                              allow_small_or_imprecise_dtypes=True))
                assert made[0] == N_CONSTS

            def root(b, ve, mv, rs, mr, ve_done, root_done, done, last_read):
                need(eng, ve_done, b.count(1, 1))
                need_both(eng, last_read, b.count(1, 1, back=1))
                eng.tensor_tensor(rs[:, :], ve[:, :], expo[0:C, 0, :], ALU.pow).then_inc(S[root_done], 1)
                need(eng, root_done, b.count(1, 1))
                eng.tensor_tensor(mr[:, :], mv[:, :], rs[:, :], ALU.mult).then_inc(S[done], 1)
                need(eng, done, b.count(1, 1))

            def part(stage, what, b):
                if (stage, what) == ("A", "win"):
                    need(eng, "sq_done", b.count(1, 1))
                    need(eng, "wsum_ps", b.count(1, 1, back=1))
                    eng.tensor_tensor(sq2[:, 0:L - 3], sq[:, 0:L - 3], sq[:, 2:L - 1], ALU.add).then_inc(S["win_done"], 1)
                    need(eng, "win_done", b.count(2, 1))
                    eng.tensor_tensor(sq4[:, :], sq2[:, 0:LO], sq2[:, 4:LO + 4], ALU.add).then_inc(S["win_done"], 1)
                    need(eng, "win_done", b.count(2, 2))
                if stage == "A" and what in ("qm0", "qm1"):
                    need(eng, "qd_done", b.count(1, 1))
                    need(eng, "s_ps", b.count(7, 7, back=2))
                    g = int(what[-1])
                    rows_g = slice(64 * g, 64 * g + 64)
                    eng.tensor_tensor(qb[rows_g, b.par, 1, :, :].rearrange("p j (c t) -> p j c t", c=NC),
                                      half_tokens(qd[rows_g, b.par, :], 1 - g).unsqueeze(1).to_broadcast([64, 4, NC, HC]),
                                      head_scale[rows_g, 1, :].unsqueeze(2).unsqueeze(3).to_broadcast([64, 4, NC, HC]),
                                      ALU.mult).then_inc(S["qm_done"], 1)
                    need(eng, "qm_done", b.count(2, g + 1))
                if (stage, what) == ("A", "w"):
                    need(eng, "wsum_sb", b.count(1, 1))
                    eng.tensor_tensor(wnorm[:, 1, :], wnorm[:, 0, :], expo[0:C, 1, :], ALU.pow).then_inc(S["wnorm_done"], 1)
                    need(eng, "wnorm_done", b.count(1, 1))
                if (stage, what) == ("A", "st1"):
                    root(b, ve1, mv1, rs1, mr1, "ve1_done", "rs1_done", "mr1_done", "hn_done")
                if (stage, what) == ("C", "o0"):
                    if first(b):
                        late_constants()
                        eng.wait_ge(S["weights_in"], 16 * N_WEIGHTS)
                    need(eng, "h2_done", b.count(2, 2, back=1))
                    eng.tensor_tensor(hb[:, :, :], hres[:, b.par, :, :],
                                      rowb[0:C, 4:5, :].to_broadcast([C, NC, D]), ALU.add).then_inc(S["hb_done"], 1)
                    need(eng, "hb_done", b.count(1, 1))
                if (stage, what) == ("C", "z1"):
                    root(b, ve2, mv2, rs2, mr2, "ve2_done", "rs2_done", "mr2_done", "zn_done")
                if (stage, what) == ("C", "st1"):
                    root(b, ve3, mv3, rs3, mr3, "ve3_done", "rs3_done", "mr3_done", "hn2_done")
            run(eng, part)
            eng.wait_ge(S["keys_done"], 3)
            eng.memset(act[:, :, 2, :], 1.0).then_inc(S["ones_done"], 1)
            for p in range(2):
                eng.wait_ge(h2_out[p], 16 * NB // 2)
                eng.wait_ge(row_out[p], 16 * NB // 2)
            out_rows = out.rearrange("b t d -> (b t) d")

            def rows_of(t):
                return SL if t < 2 else CAP - 2 * SL

            def part2(stage, what, e):
                if (stage, what) == ("I", "idx"):
                    hold(eng, "idx_done", e.count(1, 1))
                    hold(eng, "xgt_ps", e.count(1, 1, back=2))
                    hold(eng, "gcol_done", e.count(2, 2, back=2))
                    for t in range(3):
                        n = rows_of(t)
                        eng.indirect_dma_start(
                            out=xg[0:n, e.par, t, :], out_offset=None, in_=rows[:, :],
                            in_offset=bass.IndirectOffsetOnAxis(ap=idx[0:n, e.k, t:t + 1], axis=0)
                        ).then_inc(x_got[e.par], 16)
                if (stage, what) == ("D", "out"):
                    hold(eng, "yw_done", e.count(2, 2))
                    hold(eng, y_out, e.count(48, 0))
                    for t in range(3):
                        n = rows_of(t)
                        eng.indirect_dma_start(
                            out=out_rows, out_offset=bass.IndirectOffsetOnAxis(ap=idx[0:n, e.k, t:t + 1], axis=0),
                            in_=yw[0:n, e.par, t, :], in_offset=None, compute_op=ALU.add).then_inc(y_out, 16)
            run2(eng, part2)

        @block.scalar
        def _(eng):
            eng.wait_ge(S["decay_in"], 16)
            eng.activation(lam_row[:, :], lam_row_in[:, :], ACT.Exp, scale=-1.0).then_inc(S["lam_exp"], 1)

            def part(stage, what, b):
                if (stage, what) == ("C", "z0") and last(b):
                    for n in range(GROUPS - 1):
                        eng.wait_ge(S["seg_ps"], n + 1)
                        eng.activation(seg_probs[:, n * GC:(n + 1) * GC], SEG_BANKS[n][:, 0:GC],
                                       ACT.Copy).then_inc(S["seg_act"], 1)
                if (stage, what) == ("C", "st0") and last(b):
                    eng.wait_ge(S["seg_act"], GROUPS - 1)
                    eng.activation(high[:, 0:(GROUPS - 1) * GC], halves[:, 0:(GROUPS - 1) * GC, 1], ACT.Copy
                                   ).then_inc(S["keys_done"], 1)
                    eng.activation(low[:, 0:(GROUPS - 1) * GC], halves[:, 0:(GROUPS - 1) * GC, 0], ACT.Copy
                                   ).then_inc(S["low_done"], 1)
                if (stage, what) == ("A", "x"):
                    for half in range(2):
                        lo, hi = HALF[half]
                        need(eng, "xt_ps", b.count(2, half + 1))
                        need(eng, "sq_done", b.count(1, 1, back=1))
                        need(eng, "conv_ps", b.count(2, 2, back=1))
                        eng.activation(xT[:, lo * XC:hi * XC], pa[half][:, 0:(hi - lo) * XC],
                                       ACT.Copy).then_inc(S["xt_sb"], 1)
                if (stage, what) == ("A", "sq"):
                    need(eng, "xt_sb", b.count(2, 2))
                    need(eng, "nine_done", b.count(1, 1, back=1))
                    eng.activation(sq[:, :], xT[:, :], ACT.Square).then_inc(S["sq_done"], 1)
                if (stage, what) in (("A", "h0"), ("A", "h1")):
                    need(eng, "scale_step", b.count(3, 3))
                    for half in [int(what[1])]:
                        need(eng, "conv_ps", b.count(2, half + 1))
                        need(eng, "h_done", b.count(2, half + 1, back=1))
                        for c in chunks(half):
                            k = c - HALF[half][0]
                            eng.activation(y[:, c, :], pa[half][0:C, k * D:(k + 1) * D], ACT.Tanh,
                                           scale=wnorm[:, 3, c:c + 1]).then_inc(S["tanh_done"], 1)
                if stage == "A" and what in ("hnT0", "hnT1"):
                    for half in [int(what[-1])]:
                        lo, hi = HALF[half]
                        need(eng, "hnt_ps", b.count(2, half + 1))
                        need(eng, "v_ps", b.count(2, 2, back=1))
                        eng.activation(hnT[:, lo * C:hi * C], pa[half][:, 0:(hi - lo) * C],
                                       ACT.Copy).then_inc(S["hnt_sb"], 1)
                if (stage, what) == ("A", "hn1"):
                    need(eng, "mr1_done", b.count(1, 1))
                    need(eng, "hnt_ps", b.count(2, 2, back=1))
                    for c in chunks(1):
                        ins = eng.activation(hn[:, c, :], hres[:, b.par, c, :], ACT.Identity, scale=rs1[:, c:c + 1],
                                             bias=mr1[:, c:c + 1])
                    ins.then_inc(S["hn_done1"], 1)
                if (stage, what) == ("C", "zn"):
                    need(eng, "mr2_done", b.count(1, 1))
                    for half in range(2):
                        for c in chunks(half):
                            ins = eng.activation(z[:, c, :], z[:, c, :], ACT.Identity, scale=rs2[:, c:c + 1],
                                                 bias=mr2[:, c:c + 1])
                        ins.then_inc(S[("zn_done", "zn_done1")[half]], 1)
                if (stage, what) == ("C", "hn1"):
                    need(eng, "mr3_done", b.count(1, 1))
                    need(eng, row_out[b.par], b.m * 16)
                    need(eng, "h2t_ps", b.count(2, 2, back=2))
                    for c in chunks(1):
                        ins = eng.activation(row[:, b.par, c, 0:D], h2[:, b.par, c, :], ACT.Identity,
                                             scale=rs3[:, c:c + 1], bias=mr3[:, c:c + 1])
                    ins.then_inc(S["hn2_done1"], 1)
                if stage == "A" and what in QK:
                    for n in [QK.index(what)]:
                        w, half = n // 2, n % 2
                        if first(b) and n == 0:
                            eng.wait_ge(S["weights_in"], 16 * N_WEIGHTS)
                        need(eng, "qk_ps", b.count(4, n + 1))
                        need(eng, "f_done", b.count(4, n + 1, back=1))
                        if w:
                            need(eng, "kd_done", b.count(4, 4, back=1))
                            need(eng, "kt_ps", b.count(2, 2, back=1))
                        cols = slice(half * QH, half * QH + QH)
                        eng.activation(eqk[:, w, cols], pa[half][:, 0:QH], ACT.Exp,
                                       bias=bqk[:, w:w + 1]).then_inc(S["e_sb"], 1)
                        eng.activation(tqk[:, w, cols], pa[half][:, 0:QH], ACT.Relu,
                                       bias=bqk[:, w:w + 1]).then_inc(S["t_sb"], 1)
                if stage == "A" and what in ("qb0", "qb1"):
                    if first(b):
                        eng.wait_ge(S["consts_pool"], ATTENTION_CONSTS)
                    need(eng, "qd_done", b.count(1, 1))
                    need(eng, "s_ps", b.count(7, 7, back=2))
                    g = int(what[-1])
                    rows_g = slice(64 * g, 64 * g + 64)
                    for j in range(4):
                        eng.activation(qb[rows_g, b.par, 0, j, :].rearrange("p (c t) -> p c t", c=NC),
                                       half_tokens(qd[rows_g, b.par, :], g), ACT.Copy,
                                       scale=head_scale[rows_g, 0, j:j + 1]).then_inc(S["qb_done"], 1)
                if stage == "A" and what in ("kt0", "kt1"):
                    half = int(what[-1])
                    lo, hi = HALF[half]
                    need(eng, "kt_ps", b.count(2, half + 1))
                    need(eng, "st_ps", b.count(7, 7, back=2))
                    eng.activation(kt[:, b.par, lo:hi, :], pa[half][0:C, 0:(hi - lo) * D].rearrange("p (c d) -> p c d", d=D),
                                   ACT.Copy).then_inc(S["kt_sb"], 1)
                if stage == "C" and what in ("o0", "o1"):
                    for half in [int(what[-1])]:
                        lo, hi = HALF[half]
                        need(eng, "ot_ps", b.count(2, half + 1))
                        need(eng, "wo_ps", b.count(2, 2, back=1))
                        eng.activation(oT[:, lo * C:hi * C], pc[half][:, 0:(hi - lo) * C],
                                       ACT.Copy).then_inc(S["ot_sb"], 1)
                if stage == "C" and what in ("t0", "t1"):
                    for half in [int(what[-1])]:
                        lo, hi = HALF[half]
                        need(eng, "h2t_ps", b.count(2, half + 1))
                        need(eng, "r_ps", b.count(2, 2, back=1))
                        eng.activation(h2T[:, lo * C:hi * C], pc[half][:, 0:(hi - lo) * C],
                                       ACT.Copy).then_inc(S["h2t_sb"], 1)
                if (stage, what) == ("C", "soft"):
                    need(eng, "lsub_done", b.count(1, 1))
                    eng.activation(lg[:, :, :], lg[:, :, :], ACT.Exp).then_inc(S["lexp_done"], 1)
            run(eng, part)
            eng.wait_ge(S["seg_dve"], 1)
            eng.activation(low[:, (GROUPS - 1) * GC:], halves[:, (GROUPS - 1) * GC:, 0], ACT.Copy).then_inc(S["low_done"], 1)

            def count_signs(keys, nbits, steps_before, counts_before):
                with eng.Fori(0, nbits // 2) as r:
                    for k in range(2):
                        hold(eng, "bit_step", r * 6 + (steps_before + 2 + 3 * k))
                        eng.activation(signs, keys[:, DVE_KEYS:], ACT.Sign, scale=-1.0, bias=cand[:, :],
                                       accum_out=sign_sum[:, :]).then_inc(S["signs_done"], 1)

            eng.wait_ge(S["keys_done"], 2)
            count_signs(high, HIGH_BITS, 0, 0)
            eng.wait_ge(S["keys_done"], 3)
            count_signs(low_tied, LOW_BITS, 2 + 3 * HIGH_BITS, HIGH_BITS)
            eng.wait_ge(S["bup_in"], 16 * 3 * NG)
            eng.wait_ge(S["ones_done"], 1)

            def part2(stage, what, e):
                if (stage, what) == ("F", "x"):
                    need(eng, "xgt_ps", e.count(1, 1))
                    need(eng, "up_ps", e.count(3, 3, back=1))
                    eng.activation(xgT, p_xg[:, 0:CAP], ACT.Copy).then_inc(S["xgt_sb"], 1)
                if stage == "F" and what in UP:
                    need(eng, "dn_ps", e.count(1, 1, back=2))
                    for k in [UP.index(what)]:
                        n = FC if k < 2 else FC - 1
                        hold(eng, "up_ps", e.count(3, k + 1))
                        eng.activation(act[0:n, e.par, k, :], p_up[k][0:n, 0:CAP], ACT.Silu,
                                       bias=bup[0:n, e.m, k:k + 1]).then_inc(S["act_done"], 1)
                if (stage, what) == ("I", "reach"):
                    need(eng, "dcum_ps", e.count(1, 1))
                    need(eng, "cum_ps", e.count(1, 1, back=1))
                    eng.activation(dcum[:, :, :], p_dcum[0:NJ, 0:2 * C].rearrange("p (h t) -> p h t", h=2),
                                   ACT.Copy).then_inc(S["dcum_sb"], 1)
            run2(eng, part2)

        @block.tensor
        def _(eng):
            eng.wait_ge(S["consts_pool"], FIRST_CONSTS)

            def turn(n):
                eng.wait_ge(S["probs_done"], NB if n == GROUPS - 1 else NB - 1)
                eng.wait_ge(S["consts_pool"], N_CONSTS)
                for k in range(4):
                    j = 4 * (4 * n + k)
                    mm = eng.transpose(SEG_BANKS[n][:, k * C:(k + 1) * C],
                                       probs[:, j:j + 4, :].rearrange("p j e -> p (j e)"), ident[0:C, 0:C])
                mm.then_inc(S["seg_ps"], 1)

            def part(stage, what, b):
                if (stage, what) == ("C", "z0") and last(b):
                    for n in range(GROUPS - 1):
                        turn(n)
                if (stage, what) == ("A", "x"):
                    need(eng, x_in[b.par], b.m * 32 + 32)
                    for half in range(2):
                        need(eng, "kt_sb", b.count(2, half + 1, back=1))
                        for c in chunks(half):
                            k = c - HALF[half][0]
                            mm = eng.transpose(pa[half][:, k * XC:(k + 1) * XC], xw[:, b.par, c, :], ident[0:XC, 0:XC])
                        mm.then_inc(S["xt_ps"], 1)
                if (stage, what) == ("A", "w"):
                    need(eng, "nine_done", b.count(1, 1))
                    need(eng, *(("state_done", BEFORE(b).count(7, 1)) if WSUM_AT == 1 else
                                ("stm_done", BEFORE(b).count(6, max(WSUM_AT - 1, 0)))))
                    for c in range(NC):
                        mm = eng.matmul(pst[0:C, c:c + 1], sq4[:, c * C:(c + 1) * C], ones[:, :], start=True, stop=True)
                    mm.then_inc(S["wsum_ps"], 1)
                if (stage, what) in (("A", "conv0"), ("A", "conv1")):
                    if first(b):
                        eng.wait_ge(S["wc_in"], 16 * 3)
                    need(eng, "xt_sb", b.count(2, 2))
                    for half in [int(what[4])]:
                        for c in chunks(half):
                            k = c - HALF[half][0]
                            dst = pa[half][0:C, k * D:(k + 1) * D]
                            for t in range(4):
                                a = c * C + 2 * t
                                eng.matmul(dst, xT[:, a:a + C], wc[:, t, :], start=(t == 0), stop=False)
                            a = c * C + TAPS - 2
                            mm = eng.matmul(dst, xT[CIN:128, a:a + C], wc[CIN:128, 4, :], start=False, stop=True)
                        mm.then_inc(S["conv_ps"], 1)
                if stage == "A" and what in ("hnT0", "hnT1"):
                    for half in [int(what[-1])]:
                        need(eng, ("hn_done", "hn_done1")[half], b.count(1, 1))
                        need(eng, "tanh_done", b.count(NC, HALF[half][1]))
                        for c in chunks(half):
                            k = c - HALF[half][0]
                            mm = eng.transpose(pa[half][:, k * C:(k + 1) * C], hn[:, c, :], ident[0:C, 0:C])
                        mm.then_inc(S["hnt_ps"], 1)
                if stage == "A" and what in QK:
                    for n in [QK.index(what)]:
                        w, half = n // 2, n % 2
                        need(eng, "hnt_sb", b.count(2, 2 if half or w else 1))
                        if first(b) and n == 0:
                            eng.wait_ge(S["weights_in"], 16 * N_WEIGHTS)
                            eng.wait_ge(S["spread_done"], 2)
                            for k in range(2):
                                mm = eng.transpose(po[:, k * 128:k * 128 + C + 1], spread[:, k, :], ident[0:C + 1, 0:C + 1])
                            mm.then_inc(S["spread_ps"], 1)
                        if w:
                            need(eng, "t_sb", b.count(4, half + 1))
                        eng.matmul(pa[half][:, 0:QH], wqkv[:, w * D:(w + 1) * D], hnT[:, half * QH:half * QH + QH],
                                   start=True, stop=True).then_inc(S["qk_ps"], 1)
                if stage == "A" and what in ("v0", "v1"):
                    for half in [int(what[-1])]:
                        need(eng, "t_sb", b.count(4, half + 3))
                        for c in chunks(half):
                            k = c - HALF[half][0]
                            mm = eng.matmul(pa[half][0:C, k * D:(k + 1) * D], hnT[:, c * C:(c + 1) * C],
                                            wqkv[:, 2 * D:3 * D], start=True, stop=True)
                        mm.then_inc(S["v_ps"], 1)
                if stage == "A" and what in ("kt0", "kt1"):
                    need(eng, "kdec_done", b.count(1, 1))
                    for half in [int(what[-1])]:
                        need(eng, "v_sb", b.count(2, half + 1))
                        for c in chunks(half):
                            k = c - HALF[half][0]
                            mm = eng.transpose(pa[half][0:C, k * D:(k + 1) * D], eqk[:, 1, c * C:(c + 1) * C], ident[:, :])
                        mm.then_inc(S["kt_ps"], 1)
                if stage == "S":
                    c = what
                    tok = slice(c * C, (c + 1) * C)
                    if c == 0:
                        need(eng, "qb_done", b.count(8, 8))
                        need(eng, "qm_done", b.count(2, 2))
                        need(eng, "kd_done", b.count(4, 4))
                        need(eng, "kt_sb", b.count(2, 2))
                        need(eng, "v_sb", b.count(2, 2))
                    need(eng, "p_done", b.count(7, c - 1))
                    for pack in range(2):
                        mm = eng.matmul(ps[c % 2][0:C, pack * 4 * HC:(pack + 1) * 4 * HC], kd[:, b.par, pack, tok],
                                        qb[:, b.par, pack, :, c * HC:(c + 1) * HC], start=True, stop=True)
                    mm.then_inc(S["s_ps"], 1)
                if stage == "T":
                    c = what
                    if c == 1:
                        need(eng, "state_done", b.count(7, 1))
                    else:
                        need(eng, "stm_done", b.count(6, max(c - 1, 0)))
                    if c == WSUM_AT and not last(b):
                        need(eng, "wsum_sb", AFTER(b).count(1, 1))
                    if c < NC - 1:
                        eng.matmul(pst[:, 0:H * E1], kt[:, b.par, c, :],
                                   v1[:, b.par, c, :, :].rearrange("p h e -> p (h e)"), start=True, stop=True)
                    eng.matmul(pst[:, H * E1:2 * H * E1], kt[0:HC, b.par, c, :],
                               v1[0:HC, b.par, c, :, :].rearrange("p h e -> p (h e)"),
                               start=True, stop=True).then_inc(S["st_ps"], 1)
                if stage == "V":
                    c = what
                    if first(b) and c == 0:
                        eng.wait_ge(S["decays_done"], 9)
                    if c == 0:
                        need(eng, "vm_done", b.count(2, 2))
                    need(eng, "o_done", b.count(7, c))
                    need(eng, "state_done", b.count(7, c + 1))
                    if c > 0:
                        eng.matmul(po[0:HC, 0:H * E1], qd[:, b.par, c * C:c * C + HC], state[:, c % 3, 0, :],
                                   start=True, stop=False, skip_group_check=True)
                    eng.matmul(po[0:HC, H * E1:2 * H * E1], qd[:, b.par, c * C + HC:(c + 1) * C], state[:, (c + 1) % 3, 1, :],
                               start=(c == 0), stop=False, skip_group_check=True)
                    need(eng, "p_done", b.count(7, c + 1))
                    values = vm[:, b.par, c, :, :].rearrange("p u (g j e) -> p (u g) j e", g=2, j=4)
                    outs = po[0:HC, 0:2 * H * E1].rearrange("p (a j e) -> p a j e", a=4, j=4)
                    for pack, pair in enumerate((slice(0, 4, 3), slice(1, 3))):
                        for j in range(4):
                            mm = eng.matmul(outs[:, pair, j, :], P[:, c % 2, pack, j, :], values[:, pair, j, :],
                                            start=False, stop=(pack == 1 and j == 3), skip_group_check=True)
                    mm.then_inc(S["o_ps"], 1)
                if stage == "C" and what in ("o0", "o1"):
                    for half in [int(what[-1])]:
                        need(eng, "o_done", b.count(7, HALF[half][1]))
                        need(eng, "lg_done", b.count(2, half + 1, back=1))
                        for c in chunks(half):
                            k = c - HALF[half][0]
                            for u in range(2):
                                dst, src = pc[half][:, k * C + u * HC:k * C + (u + 1) * HC], o[:, b.par, c, u * D:(u + 1) * D]
                                if k == 0 and u == 0:
                                    eng.matmul(dst, src, ident[0:HC, 0:HC], start=True, stop=True)
                                else:
                                    mm = eng.transpose(dst, src, ident[0:HC, 0:HC])
                        mm.then_inc(S["ot_ps"], 1)
                if stage == "C" and what in ("w0", "w1"):
                    for half in [int(what[-1])]:
                        need(eng, "ot_sb", b.count(2, half + 1))
                        for c in chunks(half):
                            k = c - HALF[half][0]
                            mm = eng.matmul(pc[half][0:C, k * D:(k + 1) * D], oT[:, c * C:(c + 1) * C], wo[:, :],
                                            start=True, stop=True)
                        mm.then_inc(S["wo_ps"], 1)
                if stage == "C" and what in ("t0", "t1"):
                    for half in [int(what[-1])]:
                        need(eng, ("hn2_done", "hn2_done1")[half], b.count(1, 1))
                        need(eng, "z_done", b.count(2, half + 1))
                        for c in chunks(half):
                            k = c - HALF[half][0]
                            mm = eng.transpose(pc[half][:, k * C:(k + 1) * C], row[:, b.par, c, 0:D], ident[0:C, 0:C])
                        mm.then_inc(S["h2t_ps"], 1)
                if stage == "C" and what in ("r0", "r1"):
                    for half in [int(what[-1])]:
                        need(eng, "h2t_sb", b.count(2, half + 1))
                        for c in chunks(half):
                            k = c - HALF[half][0]
                            mm = eng.matmul(pc[half][0:C, k * NE:(k + 1) * NE], h2T[:, c * C:(c + 1) * C], wr[:, :],
                                            start=True, stop=True)
                        mm.then_inc(S["r_ps"], 1)
            run(eng, part)
            turn(GROUPS - 1)

            def sum_hits(value, signs_value):
                need(eng, "hits_done", value)
                eng.matmul(pst[:, 0:1], same_expert[:, :], hits[:, 0:1], start=True, stop=False)
                if signs_value is None:
                    mm = eng.matmul(pst[:, 0:1], same_expert[:, :], hits[:, 1:2], start=False, stop=True)
                else:
                    need(eng, "signs_done", signs_value)
                    mm = eng.matmul(pst[:, 0:1], half_expert[:, :], sign_sum[:, :], start=False, stop=True)
                mm.then_inc(S["hits_ps"], 1)

            with eng.Fori(0, HIGH_BITS // 2) as r:
                for k in range(2):
                    sum_hits(r * 2 + (k + 1), r * 2 + (k + 1))
            sum_hits(HIGH_BITS + 2, None)
            with eng.Fori(0, LOW_BITS // 2) as r:
                for k in range(2):
                    sum_hits(r * 2 + (HIGH_BITS + 2 + k + 1), r * 2 + (HIGH_BITS + k + 1))
            eng.wait_ge(S["thr_step"], 8)
            eng.transpose(pst[0:C, 0:NE], thr_wide[:, :], ident[0:NE, 0:NE]).then_inc(S["thr_ps"], 1)

            def part2(stage, what, e):
                if (stage, what) == ("F", "x"):
                    need(eng, x_got[e.par], e.half() * 48)
                    need(eng, "xgt_sb", e.count(1, 1, back=1))
                    for t in range(3):
                        n = SL if t < 2 else CAP - 2 * SL
                        mm = eng.transpose(p_xg[:, t * SL:t * SL + n], xg[0:n, e.par, t, 0:D], ident[0:n, 0:n])
                    mm.then_inc(S["xgt_ps"], 1)
                if stage == "F" and what in UP:
                    need(eng, w_in[e.k], e.m * 64 + 64)
                    need(eng, "xgt_sb", e.count(1, 1))
                    for k in [UP.index(what)]:
                        n = FC if k < 2 else FC - 1
                        need(eng, "act_done", e.count(3, k + 1, back=1))
                        eng.matmul(p_up[k][0:n, 0:CAP], wup[:, e.k, k * FC:k * FC + n], xgT,
                                   start=True, stop=True).then_inc(S["up_ps"], 1)
                if stage == "D" and what in DOWN:
                    need(eng, "yw_done", e.count(2, 2, back=1))
                    need(eng, "act_done", e.count(3, 3))
                    for t in [DOWN.index(what)]:
                        n = SL if t < 2 else CAP - 2 * SL
                        for k in range(3):
                            mm = eng.matmul(p_dn[0:n, t * D:(t + 1) * D], act[:, e.par, k, t * SL:t * SL + n],
                                            wdn[:, e.k, k, :], start=(k == 0), stop=(k == 2))
                    if what == DOWN[-1]:
                        mm.then_inc(S["dn_ps"], 1)
                if (stage, what) == ("I", "cnt"):
                    need(eng, "mask_done", e.count(2, 2))
                    need(eng, "idx_done", e.count(1, 1, back=1))
                    for h in range(2):
                        mm = eng.matmul(p_small[0:NJ, h:h + 1], mask[:, 1 + h * NJ:1 + (h + 1) * NJ], onesb[0:C, 0:1],
                                        start=True, stop=True)
                    mm.then_inc(S["cnt_ps"], 1)
                    need(eng, "dcum_sb", e.count(1, 1, back=1))
                    for h in range(2):
                        eng.matmul(p_dcum[0:NJ, h * C:(h + 1) * C], mask[:, h * NJ:(h + 1) * NJ], above[:, :],
                                   start=True, stop=False)
                        mm = eng.matmul(p_dcum[0:NJ, h * C:(h + 1) * C], mask[:, 1 + h * NJ:1 + (h + 1) * NJ], upto[:, :],
                                        start=False, stop=True)
                    mm.then_inc(S["dcum_ps"], 1)
                if (stage, what) == ("I", "reach"):
                    need(eng, "cnt_sb", e.count(1, 1))
                    eng.matmul(p_small[0:NJ, 2:3], before[:, :], cnt[:, 0:1], start=True, stop=True)
                    eng.matmul(p_small[0:NJ, 3:4], before[:, :], cnt[:, 1:2], start=True, stop=False)
                    eng.matmul(p_small[0:NJ, 3:4], onesb[0:NJ, 0:NJ], cnt[:, 0:1], start=False, stop=True
                               ).then_inc(S["cex_ps"], 1)
                if (stage, what) == ("I", "cum"):
                    need(eng, "reach_done", e.count(2, 2))
                    need(eng, "dcum_sb", e.count(1, 1))
                    need(eng, "inside_done", e.count(1, 1, back=1))
                    for h in range(2):
                        mm = eng.matmul(p_cum[0:C, 0:CAP + 1], dcum[:, h, :], reach[:, h, :], start=(h == 0), stop=(h == 1))
                    mm.then_inc(S["cum_ps"], 1)
                if (stage, what) == ("I", "idx"):
                    need(eng, "inside_done", e.count(1, 1))
                    for t in range(3):
                        sl = slice(t * SL, (t + 1) * SL)
                        dst = p_small[0:SL, 4 + t:5 + t]
                        eng.matmul(dst, inside[:, sl], onesb[0:C, 0:1], start=True, stop=False)
                        eng.matmul(dst, reach[:, 0, sl], chunkb[0:NJ, :], start=False, stop=False)
                        mm = eng.matmul(dst, reach[:, 1, sl], chunkb[0:NJ, :], start=False, stop=True)
                    mm.then_inc(S["idx_ps"], 1)
            run2(eng, part2)

        @block.vector
        def _(eng):
            eng.wait_ge(S["lam_exp"], 1)
            eng.tensor_scalar(lam_row[:, :], lam_row[:, :], 1.0, None, ALU.add).then_inc(S["lam_done"], 1)
            eng.wait_ge(S["lam_done"], 1)
            eng.reciprocal(lam_row[:, :], lam_row[:, :]).then_inc(S["lam_done"], 1)

            def stats(b, half, src, st, mv, ve, tmp, steps_done, ve_done, root_done, last_read):
                base = NC + 5
                if half == 0:
                    need_both(eng, last_read, b.count(1, 1, back=1))
                    need(eng, root_done, b.count(1, 1, back=1))
                for c in chunks(half):
                    eng.bn_stats(st[:, c, :], src(c)).then_inc(S[steps_done], 1)
                if half == 0:
                    return
                need(eng, steps_done, b.count(base, NC))
                eng.tensor_tensor(tmp[:, 0, :], st[:, :, 1], st[:, :, 4], ALU.add).then_inc(S[steps_done], 1)
                eng.tensor_tensor(tmp[:, 1, :], st[:, :, 1], st[:, :, 4], ALU.subtract).then_inc(S[steps_done], 1)
                eng.scalar_tensor_tensor(out=tmp[:, 2, :], in0=st[:, :, 2], scalar=D * EPS_LN, in1=st[:, :, 5],
                                         op0=ALU.add, op1=ALU.add).then_inc(S[steps_done], 1)
                need(eng, steps_done, b.count(base, NC + 3))
                eng.tensor_scalar(mv[:, :], tmp[:, 0, :], -0.5, None, ALU.mult).then_inc(S[steps_done], 1)
                eng.scalar_tensor_tensor(out=tmp[:, 1, :], in0=tmp[:, 1, :], scalar=0.25, in1=tmp[:, 1, :],
                                         op0=ALU.mult, op1=ALU.mult).then_inc(S[steps_done], 1)
                need(eng, steps_done, b.count(base, NC + 5))
                eng.scalar_tensor_tensor(out=ve[:, :], in0=tmp[:, 2, :], scalar=1.0 / D, in1=tmp[:, 1, :],
                                         op0=ALU.mult, op1=ALU.add).then_inc(S[ve_done], 1)

            def part(stage, what, b):
                if (stage, what) == ("A", "win1"):
                    need(eng, "win_done", b.count(2, 2))
                    eng.tensor_tensor(sq4[CIN:128, :], sq4[CIN:128, :], sq[CIN:128, TAPS - 2:TAPS - 2 + LO],
                                      ALU.add).then_inc(S["nine_done"], 1)
                if (stage, what) == ("A", "w"):
                    need(eng, "wsum_ps", b.count(1, 1))
                    need(eng, "wnorm_done", b.count(1, 1, back=1))
                    eng.tensor_scalar(wnorm[:, 0, :], pst[0:C, 0:NC], 0.0, None, ALU.max).then_inc(S["wsum_sb"], 1)
                if (stage, what) == ("A", "scale"):
                    need(eng, "wnorm_done", b.count(1, 1))
                    eng.tensor_scalar(wnorm[:, 2, :], wnorm[:, 1, :], EPS_W, None, ALU.add).then_inc(S["scale_step"], 1)
                    need(eng, "scale_step", b.count(3, 1))
                    eng.reciprocal(wnorm[:, 2, :], wnorm[:, 2, :]).then_inc(S["scale_step"], 1)
                    need(eng, "scale_step", b.count(3, 2))
                    need(eng, "tanh_done", b.count(NC, NC, back=1))
                    eng.tensor_scalar(wnorm[:, 3, :], wnorm[:, 2, :], 1.0, LAM, ALU.min, ALU.mult).then_inc(S["scale_step"], 1)
                if (stage, what) in (("A", "h0"), ("A", "h1")):
                    for half in [int(what[1])]:
                        lo, hi = HALF[half]
                        need(eng, "tanh_done", b.count(NC, hi))
                        if first(b) and half == 0:
                            eng.wait_ge(S["weights_in"], 16 * N_WEIGHTS)
                            eng.wait_ge(S["powers_done"], 1)
                            for k in range(2):
                                eng.tensor_copy(spread[:, k, :].rearrange("p (h e) -> p h e", h=H),
                                                powers[0:C + 1, k, :].unsqueeze(2).to_broadcast([C + 1, H, E])
                                                ).then_inc(S["spread_done"], 1)
                        eng.tensor_tensor(y[:, lo:hi, :], y[:, lo:hi, :], rowb[0:C, 0:1, :].to_broadcast([C, hi - lo, D]),
                                          ALU.add).then_inc(S["ybias_done"], 1)
                        need(eng, "ybias_done", b.count(2, half + 1))
                        need(eng, "hb_done", b.count(1, 1, back=2))
                        eng.tensor_scalar(hres[:, b.par, lo:hi, :], y[:, lo:hi, :], 0.0, None,
                                          ALU.max).then_inc(S["h_done"], 1)
                if (stage, what) in (("A", "st0"), ("A", "st1")):
                    half = int(what[2])
                    need(eng, "h_done", b.count(2, half + 1))
                    stats(b, half, lambda c: hres[:, b.par, c, :], st1, mv1, ve1, tmp1, "stats1", "ve1_done", "mr1_done", "hn_done")
                if (stage, what) == ("A", "hn0"):
                    need(eng, "rs1_done", b.count(1, 1))
                    need(eng, "hnt_ps", b.count(2, 2, back=1))
                    for c in chunks(0):
                        ins = eng.tensor_scalar(hn[:, c, :], hres[:, b.par, c, :], mv1[:, c:c + 1], rs1[:, c:c + 1],
                                                ALU.add, ALU.mult)
                    ins.then_inc(S["hn_done"], 1)
                if stage == "A" and what in QK:
                    need(eng, "kt_ps", b.count(2, 2, back=1))
                    need(eng, "kdec_done", b.count(1, 1, back=1))
                    for n in [QK.index(what)]:
                        w, half = n // 2, n % 2
                        cols = slice(half * QH, half * QH + QH)
                        need(eng, "e_sb", b.count(4, n + 1))
                        need(eng, "t_sb", b.count(4, n + 1))
                        eng.scalar_tensor_tensor(out=fqk[:, w, cols], in0=eqk[:, w, cols], scalar=1.0, in1=tqk[:, w, cols],
                                                 op0=ALU.min, op1=ALU.add).then_inc(S["f_done"], 1)
                if (stage, what) == ("A", "qd"):
                    if first(b):
                        eng.wait_ge(S["consts_pool"], ATTENTION_CONSTS)
                        eng.wait_ge(S["spread_ps"], 1)
                        eng.tensor_copy(lamc[:, :], po[:, C:C + 1]).then_inc(S["decays_done"], 1)
                        eng.tensor_copy(lamc_inv[:, :], po[:, 128 + C:129 + C]).then_inc(S["decays_done"], 1)
                        eng.tensor_copy(dk[:, :], po[:, 128:128 + C]).then_inc(S["decays_done"], 1)
                        eng.wait_ge(S["decays_done"], 2)
                        eng.tensor_scalar(dq[:, 0:HC], po[:, 0:HC], float(E) ** -0.5, lamc[:, 0:1], ALU.mult, ALU.mult
                                          ).then_inc(S["decays_done"], 1)
                        eng.tensor_scalar(dq[:, HC:C], po[:, HC:C], float(E) ** -0.5, None, ALU.mult
                                          ).then_inc(S["decays_done"], 1)
                        for pack in range(2):
                            for g in range(2):
                                rows_g = slice(64 * g, 64 * g + 64)
                                scale = lamc_inv[rows_g, 0:1] if pack == g else 1.0
                                eng.tensor_scalar(head_scale[rows_g, pack, :], head4[rows_g, :], scale, None, ALU.mult
                                                  ).then_inc(S["decays_done"], 1)
                        eng.wait_ge(S["decays_done"], 9)
                    need(eng, "f_done", b.count(4, 2))
                    need(eng, "o_ps", b.count(7, 7, back=2))
                    need(eng, "qb_done", b.count(8, 8, back=2))
                    need(eng, "qm_done", b.count(2, 2, back=2))
                    eng.tensor_tensor(qd[:, b.par, :].rearrange("p (c t) -> p c t", c=NC),
                                      fqk[:, 0, :].rearrange("p (c t) -> p c t", c=NC),
                                      dq[:, :].unsqueeze(1).to_broadcast([128, NC, C]),
                                      ALU.mult).then_inc(S["qd_done"], 1)
                if (stage, what) == ("A", "kd"):
                    need(eng, "f_done", b.count(4, 4))
                    eng.tensor_tensor(eqk[:, 1, :].rearrange("p (c t) -> p c t", c=NC),
                                      fqk[:, 1, :].rearrange("p (c t) -> p c t", c=NC),
                                      dk[:, :].unsqueeze(1).to_broadcast([128, NC, C]),
                                      ALU.mult).then_inc(S["kdec_done"], 1)
                if stage == "A" and what in ("kd0", "kd1"):
                    pack = int(what[-1])
                    need(eng, "kdec_done", b.count(1, 1))
                    need(eng, "s_ps", b.count(7, 7, back=2))
                    for g in range(2):
                        rows_g = slice(64 * g, 64 * g + 64)
                        eng.tensor_copy(half_tokens(kd[rows_g, b.par, pack, :], pack ^ g),
                                        half_tokens(eqk[rows_g, 1, :], pack ^ g)).then_inc(S["kd_done"], 1)
                if (stage, what) == ("A", "vm"):
                    need(eng, "v_sb", b.count(2, 2))
                    need(eng, "o_ps", b.count(7, 7, back=2))
                    for u in range(2):
                        eng.tensor_scalar(vm[:, b.par, :, u, :], v1[:, b.par, :, :, :].rearrange("p c h e -> p c (h e)"),
                                       of_half[:, u:u + 1], None, ALU.mult).then_inc(S["vm_done"], 1)
                if stage == "A" and what in ("v0", "v1"):
                    need(eng, "st_ps", b.count(7, 7, back=2))
                    need(eng, "vm_done", b.count(2, 2, back=2))
                    for half in [int(what[-1])]:
                        lo, hi = HALF[half]
                        need(eng, "v_ps", b.count(2, half + 1))
                        eng.tensor_tensor(v1[:, b.par, lo:hi, :, 0:E],
                                          pa[half][0:C, 0:(hi - lo) * D].rearrange("p (c h e) -> p c h e", h=H, e=E),
                                          rowb[0:C, 1:2, :].to_broadcast([C, hi - lo, D]).rearrange("p c (h e) -> p c h e", h=H),
                                          ALU.add).then_inc(S["v_sb"], 1)
                if stage == "S":
                    c = what
                    need(eng, "s_ps", b.count(7, c + 1))
                    need(eng, "o_ps", b.count(7, c - 1))
                    eng.tensor_tensor(P[:, c % 2, :, :, :].rearrange("p k j t -> p (k j) t"),
                                      ps[c % 2][0:C, 0:H * HC].rearrange("p (h t) -> p h t", h=H),
                                      causal[:, 0:1, :].to_broadcast([C, H, HC]), ALU.mult).then_inc(S["p_done"], 1)
                if stage == "T":
                    c = what
                    need(eng, "o_ps", b.count(7, c - 1))
                    need(eng, "st_ps", b.count(7, c + 1))
                    lo = 0 if c < NC - 1 else 1
                    new = state[:, (c + 1) % 3, lo:2, :]
                    added = state_in[:, lo:2, :] if c else new
                    need(eng, "state_done", b.count(7, c))
                    if c == 0:
                        need(eng, "o_ps", b.count(7, 7, back=1))
                    eng.tensor_tensor(added, pst[:, lo * H * E1:2 * H * E1].rearrange("p (k e) -> p k e", e=H * E1),
                                      blk[:, :].unsqueeze(1).to_broadcast([128, 2 - lo, H * E1]), ALU.mult
                                      ).then_inc(S["stm_done" if c else "state_done"], 1)
                    if c:
                        need(eng, "stm_done", b.count(6, c))
                        eng.scalar_tensor_tensor(out=new, in0=state[:, c % 3, 0:1, :].to_broadcast([128, 2 - lo, H * E1]),
                                                 scalar=lamc[:, 0:1], in1=added, op0=ALU.mult, op1=ALU.add
                                                 ).then_inc(S["state_done"], 1)
                if stage == "V":
                    c = what
                    need(eng, "o_ps", b.count(7, c + 1))
                    if c == 0:
                        need(eng, "ot_ps", b.count(2, 2, back=2))
                    ov = po[0:HC, 0:2 * H * E1].rearrange("p (a e) -> p a e", a=2 * H)
                    need(eng, "o_done", b.count(7, c))
                    eng.tensor_scalar(den[:, 0, :], ov[:, :, E], EPS_DEN, None, ALU.add).then_inc(S["den_step"], 1)
                    need(eng, "den_step", b.count(14, 2 * c + 1))
                    eng.reciprocal(den[:, 1, :], den[:, 0, :]).then_inc(S["den_step"], 1)
                    need(eng, "den_step", b.count(14, 2 * c + 2))
                    eng.tensor_tensor(o[:, b.par, c, :].rearrange("p (a e) -> p a e", a=2 * H), ov[:, :, 0:E],
                                      den[:, 1, :].unsqueeze(2).to_broadcast([HC, 2 * H, E]), ALU.mult).then_inc(S["o_done"], 1)
                if (stage, what) in (("C", "z0"), ("C", "z1")):
                    half = int(what[1])
                    lo, hi = HALF[half]
                    need(eng, "wo_ps", b.count(2, half + 1))
                    need(eng, "h2_done", b.count(2, 2, back=1))
                    eng.tensor_tensor(z[:, lo:hi, :], pc[half][0:C, 0:(hi - lo) * D].rearrange("p (c d) -> p c d", d=D),
                                      rowb[0:C, 2:3, :].to_broadcast([C, hi - lo, D]), ALU.add).then_inc(S["z_done"], 1)
                    need(eng, "z_done", b.count(2, half + 1))
                    stats(b, half, lambda c: z[:, c, :], st2, mv2, ve2, tmp2, "stats2", "ve2_done", "mr2_done", "zn_done")
                if (stage, what) == ("C", "zg"):
                    for half in range(2):
                        lo, hi = HALF[half]
                        need(eng, ("zn_done", "zn_done1")[half], b.count(1, 1))
                        eng.tensor_tensor(z[:, lo:hi, :], z[:, lo:hi, :], rowb[0:C, 3:4, :].to_broadcast([C, hi - lo, D]),
                                          ALU.mult).then_inc(S["zg_done"], 1)
                if (stage, what) == ("C", "h2"):
                    need(eng, "hb_done", b.count(1, 1))
                    need(eng, h2_out[b.par], b.m * 16)
                    for half in range(2):
                        lo, hi = HALF[half]
                        need(eng, "zg_done", b.count(2, half + 1))
                        eng.tensor_tensor(h2[:, b.par, lo:hi, :], z[:, lo:hi, :], hb[:, lo:hi, :],
                                          ALU.add).then_inc(S["h2_done"], 1)
                if (stage, what) in (("C", "st0"), ("C", "st1")):
                    half = int(what[2])
                    need(eng, "h2_done", b.count(2, half + 1))
                    stats(b, half, lambda c: h2[:, b.par, c, :], st3, mv3, ve3, tmp3, "stats3", "ve3_done", "mr3_done", "hn2_done")
                if (stage, what) == ("C", "hn0"):
                    need(eng, "rs3_done", b.count(1, 1))
                    need(eng, row_out[b.par], b.m * 16)
                    need(eng, "h2t_ps", b.count(2, 2, back=2))
                    for c in chunks(0):
                        ins = eng.tensor_scalar(row[:, b.par, c, 0:D], h2[:, b.par, c, :], mv3[:, c:c + 1], rs3[:, c:c + 1],
                                                ALU.add, ALU.mult)
                    ins.then_inc(S["hn2_done"], 1)
                if (stage, what) == ("C", "max"):
                    need(eng, "probs_done", b.count(1, 1, back=1))
                    need(eng, "probs_row", b.count(1, 1, back=1))
                    for half in range(2):
                        lo, hi = HALF[half]
                        need(eng, "r_ps", b.count(2, half + 1))
                        eng.tensor_tensor(lg[:, lo:hi, :], pc[half][0:C, 0:(hi - lo) * NE].rearrange("p (c e) -> p c e", e=NE),
                                          brow[0:C, :].unsqueeze(1).to_broadcast([C, hi - lo, NE]), ALU.add).then_inc(S["lg_done"], 1)
                    need(eng, "lg_done", b.count(2, 2))
                    eng.tensor_reduce(lmax[:, :], lg[:, :, :], AX.X, ALU.max).then_inc(S["lmax_done"], 1)
                    need(eng, "lmax_done", b.count(1, 1))
                    eng.tensor_tensor(lg[:, :, :], lg[:, :, :], lmax[:, :].unsqueeze(2).to_broadcast([C, NC, NE]),
                                      ALU.subtract).then_inc(S["lsub_done"], 1)
                if (stage, what) == ("C", "soft"):
                    need(eng, "lexp_done", b.count(1, 1))
                    eng.tensor_reduce(lsum[:, 0, :], lg[:, :, :], AX.X, ALU.add).then_inc(S["lsum_done"], 1)
                    need(eng, "lsum_done", b.count(1, 1))
                    eng.reciprocal(lsum[:, 1, :], lsum[:, 0, :]).then_inc(S["lrec_done"], 1)
                    need(eng, "lrec_done", b.count(1, 1))
                    rb = lsum[:, 1, :].unsqueeze(2).to_broadcast([C, NC, NE])
                    eng.tensor_tensor(row[:, b.par, :, D:ROW], lg[:, :, :], rb, ALU.mult).then_inc(S["probs_row"], 1)
                    eng.tensor_tensor(probs[:, bass.ds(b.index() * NC, NC), :], lg[:, :, :], rb,
                                      ALU.mult).then_inc(S["probs_done"], 1)
            run(eng, part)
            eng.wait_ge(S["seg_ps"], GROUPS)
            eng.tensor_copy(seg_probs[:, (GROUPS - 1) * GC:], SEG_BANKS[-1][:, 0:GC]).then_inc(S["seg_dve"], 1)
            assert DVE_KEYS <= 2048 and JS * C - DVE_KEYS <= 2048
            eng.wait_ge(S["seg_dve"], 1)
            eng.tensor_copy(high[:, (GROUPS - 1) * GC:], halves[:, (GROUPS - 1) * GC:, 1]).then_inc(S["keys_done"], 1)
            eng.wait_ge(S["keys_done"], 2)

            def search(keys, goal, nbits, steps_before, counts_before):
                eng.memset(cand[:, :], float(1 << (nbits - 1)) - 0.5).then_inc(S["bit_step"], 1)
                eng.memset(bit[:, 0:1], float(1 << (nbits - 1))).then_inc(S["bit_step"], 1)
                with eng.Fori(0, nbits // 2) as r:
                    for k in range(2):
                        def after(n):
                            return r * 6 + (steps_before + 2 + 3 * k + n)
                        eng.wait_ge(S["bit_step"], after(0))
                        eng.tensor_scalar(seg_hits[:, 0:DVE_KEYS], keys[:, 0:DVE_KEYS], cand[:, :], None, ALU.is_ge, ALU.add,
                                          accum_out=hits[:, 0:1]).then_inc(S["hits_done"], 1)
                        eng.tensor_scalar(bit[:, 1 - k:2 - k], bit[:, k:k + 1], 0.5, None, ALU.mult
                                          ).then_inc(S["bit_step"], 1)
                        eng.wait_ge(S["hits_ps"], r * 2 + (counts_before + k + 1))
                        eng.tensor_scalar(step_to[:, :], pst[:, 0:1], goal, 0.5, ALU.is_ge, ALU.subtract
                                          ).then_inc(S["bit_step"], 1)
                        eng.wait_ge(S["bit_step"], after(2))
                        eng.scalar_tensor_tensor(out=cand[:, :], in0=step_to[:, :], scalar=bit[:, k:k + 1], in1=cand[:, :],
                                                 op0=ALU.mult, op1=ALU.add).then_inc(S["bit_step"], 1)
                eng.wait_ge(S["bit_step"], steps_before + 2 + 3 * nbits)

            eng.wait_ge(S["consts_pool"], N_CONSTS)
            search(high, target[:, 0:1], HIGH_BITS, 0, 0)
            eng.tensor_copy(thr_high[:, 0:1], cand[:, :]).then_inc(S["thr_step"], 1)
            eng.tensor_scalar(thr_high[:, 1:2], cand[:, :], 1.0, None, ALU.add).then_inc(S["thr_step"], 1)
            eng.wait_ge(S["thr_step"], 2)
            for k, cols in enumerate((slice(0, DVE_KEYS), slice(DVE_KEYS, JS * C))):
                eng.tensor_scalar(seg_hits[:, cols], high[:, cols], thr_high[:, 1:2], None, ALU.is_ge, ALU.add,
                                  accum_out=hits[:, k:k + 1]).then_inc(S["hits_done"], 1)
            eng.wait_ge(S["low_done"], 2)
            eng.scalar_tensor_tensor(out=low_tied, in0=high, scalar=thr_high[:, 0:1], in1=low,
                                     op0=ALU.is_equal, op1=ALU.mult).then_inc(S["keys_done"], 1)
            eng.wait_ge(S["hits_ps"], HIGH_BITS + 1)
            eng.tensor_scalar(target[:, 1:2], pst[:, 0:1], -1.0, float(CAP) - ACT_HALF, ALU.mult, ALU.add
                              ).then_inc(S["thr_step"], 1)
            eng.wait_ge(S["thr_step"], 3)
            eng.wait_ge(S["keys_done"], 3)
            search(low_tied, target[:, 1:2], LOW_BITS, 2 + 3 * HIGH_BITS, HIGH_BITS + 1)
            eng.tensor_copy(thr_high[:, 1:2], cand[:, :]).then_inc(S["thr_step"], 1)
            eng.wait_ge(S["thr_step"], 4)
            eng.tensor_copy(thr_bits[:, :], thr_high[:, :]).then_inc(S["thr_step"], 1)
            eng.wait_ge(S["thr_step"], 5)
            eng.tensor_scalar(thr_bits[:, 0:1], thr_bits[:, 0:1], 16, None, ALU.logical_shift_left).then_inc(S["thr_step"], 1)
            eng.wait_ge(S["thr_step"], 6)
            eng.tensor_tensor(thr_bits[:, 0:1], thr_bits[:, 0:1], thr_bits[:, 1:2], ALU.bitwise_or).then_inc(S["thr_step"], 1)
            eng.wait_ge(S["thr_step"], 7)
            eng.tensor_copy(thr_wide[:, :], thr_bits[0:NE, 0:1].bitcast(f32).to_broadcast([NE, C])).then_inc(S["thr_step"], 1)
            eng.wait_ge(S["thr_ps"], 1)
            eng.tensor_copy(thr[:, :], pst[0:C, 0:NE]).then_inc(S["thr_done"], 1)
            eng.wait_ge(S["thr_done"], 1)

            def part2(stage, what, e):
                if (stage, what) == ("I", "mask"):
                    need(eng, "dcum_ps", e.count(1, 1, back=1))
                    own, at = probs[:, :, bass.ds(e.index(), 1)], thr[:, bass.ds(e.index(), 1)]
                    for h, op in enumerate((ALU.is_gt, ALU.is_equal)):
                        eng.tensor_scalar(mask[:, 1 + h * NJ:1 + (h + 1) * NJ].unsqueeze(2), own, at, None, op
                                          ).then_inc(S["mask_done"], 1)
                if (stage, what) == ("F", "x"):
                    need(eng, x_got[e.par], e.half() * 48)
                    need(eng, "yw_done", e.count(2, 2, back=2))
                    own = bass.ds(e.index() + D, 1)
                    eng.tensor_copy(gcol[:, e.par, 0:2].unsqueeze(2), xg[:, e.par, 0:2, own]).then_inc(S["gcol_done"], 1)
                    n = CAP - 2 * SL
                    eng.tensor_copy(gcol[0:n, e.par, 2:3], xg[0:n, e.par, 2, own]).then_inc(S["gcol_done"], 1)
                if (stage, what) == ("I", "cnt"):
                    need(eng, "cnt_ps", e.count(1, 1))
                    need(eng, "cex_ps", e.count(1, 1, back=1))
                    eng.tensor_copy(cnt[:, :], p_small[0:NJ, 0:2]).then_inc(S["cnt_sb"], 1)
                if (stage, what) == ("I", "reach"):
                    need(eng, "cex_ps", e.count(1, 1))
                    need(eng, "reach_done", e.count(2, 2, back=1))
                    eng.tensor_copy(cex[:, :], p_small[0:NJ, 2:4]).then_inc(S["cex_sb"], 1)
                    need(eng, "cex_sb", e.count(1, 1))
                    need(eng, "idx_ps", e.count(1, 1, back=1))
                    for h in range(2):
                        eng.tensor_scalar(reach[:, h, :], slots_h[:, :], cex[:, h:h + 1], None, ALU.is_ge
                                          ).then_inc(S["reach_done"], 1)
                if (stage, what) == ("I", "cum"):
                    need(eng, "cum_ps", e.count(1, 1))
                    eng.tensor_tensor(inside[:, :], p_cum[0:C, 0:CAP + 1], slots_f[:, :], ALU.is_le
                                      ).then_inc(S["inside_done"], 1)
                if (stage, what) == ("I", "idx"):
                    need(eng, "idx_ps", e.count(1, 1))
                    need(eng, "idx_done", e.count(1, 1, back=1))
                    need(eng, y_out, e.count(48, 0, back=3))
                    eng.tensor_scalar(wrap[:, :], p_small[0:SL, 4:7], float(N + C), float(N), ALU.is_ge, ALU.mult
                                      ).then_inc(S["wrap_done"], 1)
                    need(eng, "wrap_done", e.count(1, 1))
                    eng.scalar_tensor_tensor(out=idx[:, e.k, :], in0=p_small[0:SL, 4:7], scalar=-float(C), in1=wrap[:, :],
                                             op0=ALU.add, op1=ALU.subtract).then_inc(S["idx_done"], 1)
                if (stage, what) == ("D", "out"):
                    need(eng, "dn_ps", e.count(1, 1))
                    need(eng, y_out, e.count(48, 48, back=2))
                    need(eng, "gcol_done", e.count(2, 2))
                    n = CAP - 2 * SL
                    eng.tensor_tensor(yw[:, e.par, 0:2, :], p_dn[0:SL, 0:2 * D].rearrange("p (t d) -> p t d", t=2),
                                      gcol[:, e.par, 0:2].unsqueeze(2).to_broadcast([SL, 2, D]), ALU.mult
                                      ).then_inc(S["yw_done"], 1)
                    eng.tensor_scalar(yw[0:n, e.par, 2, :], p_dn[0:n, 2 * D:3 * D], gcol[0:n, e.par, 2:3], None, ALU.mult
                                      ).then_inc(S["yw_done"], 1)
            run2(eng, part2)


N_WEIGHTS = 11
HIGH_BITS, LOW_BITS = 14, 16
FIRST_CONSTS, ATTENTION_CONSTS, N_CONSTS = 7, 25, 46

_INS = ['x', 'L0_tok_kernel', 'L0_tok_bias', 'L0_attn_Wqkv', 'L0_attn_bqkv', 'L0_attn_Wout', 'L0_attn_bout',
        'L0_attn_ln_gamma', 'L0_attn_ln_beta', 'L0_attn_decay_logits', 'L0_ffn_W_router', 'L0_ffn_b_router',
        'L0_ffn_W_up', 'L0_ffn_b_up', 'L0_ffn_W_down', 'L0_ffn_b_down']
_OUTS = [((16, 742, 128), 'float32')]


def kernel(**inputs):
    import numpy as _np
    import concourse.bacc as _bacc
    from concourse import mybir as _mybir
    from concourse.bass_utils import run_bass_kernel_spmd as _run

    nc = _bacc.Bacc("TRN2", target_bir_lowering=False, num_devices=1)
    arrays, args = {}, []
    for name in _INS:
        a = _np.ascontiguousarray(inputs[name])
        arrays[f"in_{name}_dram"] = a
        args.append(nc.dram_tensor(f"in_{name}_dram", a.shape, _mybir.dt.from_np(a.dtype), kind="ExternalInput").ap())
    for i, (shape, dtype) in enumerate(_OUTS):
        dt = _mybir.dt.from_np(_np.dtype(dtype))
        args.append(nc.dram_tensor(f"out_{i}_dram", shape, dt, kind="ExternalOutput").ap())
    audio_tower_kernel(nc, *args)
    r = _run(nc, [arrays], core_ids=[0])
    return r.results[0]["out_0_dram"]
```
